# Optimizing a Trainium2 kernel written in Bass

```python
import numpy as np
import jax
import jax.numpy as jnp

def _softmax(x, axis=-1):
    return jax.nn.softmax(x, axis=axis)

def _gelu(x):
    return jax.nn.gelu(x, approximate=True)

def _silu(x):
    return jax.nn.silu(x)

def _sigmoid(x):
    return jax.nn.sigmoid(x)

def _layernorm(x, axis=-1, eps=1e-05):
    m = jnp.mean(x, axis=axis, keepdims=True)
    v = jnp.var(x, axis=axis, keepdims=True)
    return (x - m) / jnp.sqrt(v + eps)

def _scatter_add(tgt, idx, src, axis=0):
    return tgt.at[idx].add(src)

def _segment_sum(src, seg, n):
    return jax.ops.segment_sum(src, seg, n)
kernel_name = 'mk_early_fusion_d2_tok_img256_r4_beaa24'

def setup_inputs(seed: int=0):
    np.random.seed(seed)
    _w = jnp.asarray

    def _rec_inputs():
        import jax
        import jax.numpy as jnp
        _rk = jax.random.key(seed)
        x = -0.000928989 + 1.00043 * jax.random.normal(jax.random.fold_in(_rk, 1), (8, 64, 64, 1), jnp.float32)
        txt = 0.142909 + 0.418953 * jax.random.normal(jax.random.fold_in(_rk, 2), (8, 512, 64), jnp.float32)
        return (x, txt)
    x, txt = _rec_inputs()

    def _L0_tok_setup():
        import jax, jax.numpy as jnp
        import numpy as np
        B, S, D_A, D_V, D_U, L, M1, M2 = (16, 64, 3, 32, 1, 4, 12, 12)
        MID = 4 * D_U

        def conv1x1(x, w, b):
            return jnp.einsum('bixy,oi->boxy', x, w) + b[None, :, None, None]

        def fourier_layer(x, fw_i):
            Bm, C, M, N = x.shape
            x_ft = jnp.fft.rfft2(x, s=(M, N), norm='ortho')
            w_lo = fw_i[0, ..., 0] + 1j * fw_i[0, ..., 1]
            w_hi = fw_i[1, ..., 0] + 1j * fw_i[1, ..., 1]
            lo = jnp.einsum('bixy,ioxy->boxy', x_ft[:, :, :M1, :M2], w_lo)
            hi = jnp.einsum('bixy,ioxy->boxy', x_ft[:, :, -M1:, :M2], w_hi)
            out_ft = jnp.zeros(x_ft.shape, dtype=x_ft.dtype)
            out_ft = out_ft.at[:, :, :M1, :M2].set(lo)
            out_ft = out_ft.at[:, :, -M1:, :M2].set(hi)
            return jnp.fft.irfft2(out_ft, s=(M, N), norm='ortho')

        def make_grid(b, sx, sy):
            gx = jnp.broadcast_to(jnp.linspace(0.0, 1.0, sx)[None, :, None], (b, sx, sy))
            gy = jnp.broadcast_to(jnp.linspace(0.0, 1.0, sy)[None, None, :], (b, sx, sy))
            return jnp.stack([gx, gy], axis=-1)
        key = jax.random.key(seed)
        ks = jax.random.split(key, 12)
        sc_v = 1.0 / np.sqrt(D_V)
        inp = {'x': jax.random.normal(ks[0], (B, S, S, D_A - 2), dtype=jnp.float32), 'p_w': jax.random.normal(ks[1], (D_V, D_A), dtype=jnp.float32) / np.sqrt(D_A), 'p_b': jnp.zeros((D_V,), dtype=jnp.float32), 'fw': jax.random.normal(ks[2], (L, 2, D_V, D_V, M1, M2, 2), dtype=jnp.float32) * sc_v, 'w1_w': jax.random.normal(ks[3], (L, D_V, D_V), dtype=jnp.float32) * sc_v, 'w1_b': jnp.zeros((L, D_V), dtype=jnp.float32), 'w2_w': jax.random.normal(ks[4], (L, D_V, D_V), dtype=jnp.float32) * sc_v, 'w2_b': jnp.zeros((L, D_V), dtype=jnp.float32), 'q1_w': jax.random.normal(ks[5], (MID, D_V), dtype=jnp.float32) * sc_v, 'q1_b': jnp.zeros((MID,), dtype=jnp.float32), 'q2_w': jax.random.normal(ks[6], (D_U, MID), dtype=jnp.float32) / np.sqrt(MID), 'q2_b': jnp.zeros((D_U,), dtype=jnp.float32)}
        return inp
    _L0_tok_all = _L0_tok_setup()
    _L0_tok_in = {k: v for k, v in _L0_tok_all.items() if k in ('p_w', 'p_b', 'fw', 'w1_w', 'w1_b', 'w2_w', 'w2_b', 'q1_w', 'q1_b', 'q2_w', 'q2_b')}
    del _L0_tok_all

    def _L0_attn_setup():
        import jax, jax.numpy as jnp
        import numpy as np
        D_MODEL = 64
        N_HEAD = 8

        def _l1_scores(q, k):
            scale = 1.0 / np.sqrt(q.shape[-1]).astype(np.float32)
            q_sbhw = q.transpose(1, 0, 2, 3)

            def one_query(qs):
                return -jnp.sum(jnp.abs(qs[:, None, :, :] - k), axis=-1) * scale
            s = jax.lax.map(one_query, q_sbhw)
            return s.transpose(1, 0, 2, 3)
        key = jax.random.key(seed)
        ks = jax.random.split(key, 3)
        b, t = (4, 250)
        x = jax.random.normal(ks[0], (b, t, D_MODEL), jnp.float32)
        wqv_w = 0.005 * jax.random.normal(ks[1], (3 * N_HEAD * D_MODEL, D_MODEL), jnp.float32)
        wqv_b = jnp.zeros((3 * N_HEAD * D_MODEL,), jnp.float32)
        wk = 0.005 * jnp.ones((N_HEAD, D_MODEL), jnp.float32)
        fanin_w = 0.005 * jax.random.normal(ks[2], (D_MODEL, D_MODEL), jnp.float32)
        fanin_b = jnp.zeros((D_MODEL,), jnp.float32)
        return dict(x=x, wqv_w=wqv_w, wqv_b=wqv_b, wk=wk, fanin_w=fanin_w, fanin_b=fanin_b)
    _L0_attn_all = _L0_attn_setup()
    _L0_attn_in = {k: v for k, v in _L0_attn_all.items() if k in ('wqv_w', 'wqv_b', 'wk', 'fanin_w', 'fanin_b')}
    del _L0_attn_all

    def _L0_ffn_setup():
        import jax, jax.numpy as jnp
        import numpy as np
        DIM = 64
        H = 8
        D = 64
        G = 64
        INNER = H * D
        SCALE = D ** (-0.5)
        key = jax.random.key(seed)
        ks = jax.random.split(key, 12)
        B, N = (4, 4096)
        x = jax.random.normal(ks[0], (B, N, DIM), dtype=jnp.float32)
        s = lambda fan_in: 1.0 / np.sqrt(fan_in)
        W_fx = jax.random.normal(ks[1], (DIM, INNER), dtype=jnp.float32) * s(DIM)
        b_fx = jnp.zeros((INNER,), dtype=jnp.float32)
        W_x = jax.random.normal(ks[2], (DIM, INNER), dtype=jnp.float32) * s(DIM)
        b_x = jnp.zeros((INNER,), dtype=jnp.float32)
        A = jax.random.normal(ks[3], (G, D), dtype=jnp.float32)
        Q, _ = jnp.linalg.qr(A.T)
        W_slice = Q[:, :G].astype(jnp.float32)
        b_slice = jnp.zeros((G,), dtype=jnp.float32)
        W_q = jax.random.normal(ks[4], (D, D), dtype=jnp.float32) * s(D)
        W_k = jax.random.normal(ks[5], (D, D), dtype=jnp.float32) * s(D)
        W_v = jax.random.normal(ks[6], (D, D), dtype=jnp.float32) * s(D)
        W_out = jax.random.normal(ks[7], (INNER, DIM), dtype=jnp.float32) * s(INNER)
        b_out = jnp.zeros((DIM,), dtype=jnp.float32)
        temperature = jnp.ones((1, H, 1, 1), dtype=jnp.float32) * 0.5
        return {'x': x, 'W_fx': W_fx, 'b_fx': b_fx, 'W_x': W_x, 'b_x': b_x, 'W_slice': W_slice, 'b_slice': b_slice, 'W_q': W_q, 'W_k': W_k, 'W_v': W_v, 'W_out': W_out, 'b_out': b_out, 'temperature': temperature}
    _L0_ffn_all = _L0_ffn_setup()
    _L0_ffn_in = {k: v for k, v in _L0_ffn_all.items() if k in ('W_fx', 'b_fx', 'W_x', 'b_x', 'W_slice', 'b_slice', 'W_q', 'W_k', 'W_v', 'W_out', 'b_out', 'temperature')}
    del _L0_ffn_all

    def _L1_attn_setup():
        import jax, jax.numpy as jnp
        import numpy as np
        B, S, C = (8, 256, 64)
        H, KD = (8, 64)
        HEAD_DIM = KD // H
        key = jax.random.key(seed)
        ks = jax.random.split(key, 5)
        sc = 0.02
        return {'x': jax.random.normal(ks[0], (B, S, C), dtype=jnp.float32), 'Wq': jax.random.normal(ks[1], (H * KD, C), dtype=jnp.float32) * sc, 'Wk': jax.random.normal(ks[2], (KD, C), dtype=jnp.float32) * sc, 'Wv': jax.random.normal(ks[3], (KD, C), dtype=jnp.float32) * sc, 'Wo': jax.random.normal(ks[4], (C, H * KD), dtype=jnp.float32) * sc}
    _L1_attn_all = _L1_attn_setup()
    _L1_attn_in = {k: v for k, v in _L1_attn_all.items() if k in ('Wq', 'Wk', 'Wv', 'Wo')}
    del _L1_attn_all

    def _L1_ffn_setup():
        import jax, jax.numpy as jnp
        import numpy as np
        B, A = (1024, 8)
        IN, OUT = (64, 64)
        SH1, SH2 = (64, 128)
        EH1, EH2 = (128, 64)
        E, TOPK = (4, 2)

        def _shared_mlp(x, W1, b1, W2, b2, W3, b3):
            h = jax.nn.relu(x @ W1 + b1)
            h = jax.nn.relu(h @ W2 + b2)
            return h @ W3 + b3

        def _experts_mlp(x, eW1, eb1, eW2, eb2, eW3, eb3):
            h = jax.nn.relu(jnp.einsum('baf,efh->ebah', x, eW1) + eb1[:, None, None, :])
            h = jax.nn.relu(jnp.einsum('ebah,ehg->ebag', h, eW2) + eb2[:, None, None, :])
            o = jnp.einsum('ebag,ego->ebao', h, eW3) + eb3[:, None, None, :]
            return jnp.moveaxis(o, 0, -1)
        key = jax.random.key(seed)
        ks = jax.random.split(key, 16)
        s = 0.05
        return {'x': jax.random.normal(ks[0], (B, A, IN), jnp.float32), 'sW1': jax.random.normal(ks[1], (IN, SH1), jnp.float32) * s, 'sb1': jnp.zeros((SH1,), jnp.float32), 'sW2': jax.random.normal(ks[2], (SH1, SH2), jnp.float32) * s, 'sb2': jnp.zeros((SH2,), jnp.float32), 'sW3': jax.random.normal(ks[3], (SH2, OUT), jnp.float32) * s, 'sb3': jnp.zeros((OUT,), jnp.float32), 'eW1': jax.random.normal(ks[4], (E, IN, EH1), jnp.float32) * s, 'eb1': jnp.zeros((E, EH1), jnp.float32), 'eW2': jax.random.normal(ks[5], (E, EH1, EH2), jnp.float32) * s, 'eb2': jnp.zeros((E, EH2), jnp.float32), 'eW3': jax.random.normal(ks[6], (E, EH2, OUT), jnp.float32) * s, 'eb3': jnp.zeros((E, OUT), jnp.float32), 'gW': jax.random.normal(ks[7], (IN, E), jnp.float32) * s, 'gb': jnp.zeros((E,), jnp.float32)}
    _L1_ffn_all = _L1_ffn_setup()
    _L1_ffn_in = {k: v for k, v in _L1_ffn_all.items() if k in ('sW1', 'sb1', 'sW2', 'sb2', 'sW3', 'sb3', 'eW1', 'eb1', 'eW2', 'eb2', 'eW3', 'eb3', 'gW', 'gb')}
    del _L1_ffn_all
    return {'x': x, 'txt': txt, 'L0_tok_p_w': _L0_tok_in['p_w'], 'L0_tok_p_b': _L0_tok_in['p_b'], 'L0_tok_fw': _L0_tok_in['fw'], 'L0_tok_w1_w': _L0_tok_in['w1_w'], 'L0_tok_w1_b': _L0_tok_in['w1_b'], 'L0_tok_w2_w': _L0_tok_in['w2_w'], 'L0_tok_w2_b': _L0_tok_in['w2_b'], 'L0_tok_q1_w': _L0_tok_in['q1_w'], 'L0_tok_q1_b': _L0_tok_in['q1_b'], 'L0_tok_q2_w': _L0_tok_in['q2_w'], 'L0_tok_q2_b': _L0_tok_in['q2_b'], 'L0_attn_wqv_w': _L0_attn_in['wqv_w'], 'L0_attn_wqv_b': _L0_attn_in['wqv_b'], 'L0_attn_wk': _L0_attn_in['wk'], 'L0_attn_fanin_w': _L0_attn_in['fanin_w'], 'L0_attn_fanin_b': _L0_attn_in['fanin_b'], 'L0_ffn_W_fx': _L0_ffn_in['W_fx'], 'L0_ffn_b_fx': _L0_ffn_in['b_fx'], 'L0_ffn_W_x': _L0_ffn_in['W_x'], 'L0_ffn_b_x': _L0_ffn_in['b_x'], 'L0_ffn_W_slice': _L0_ffn_in['W_slice'], 'L0_ffn_b_slice': _L0_ffn_in['b_slice'], 'L0_ffn_W_q': _L0_ffn_in['W_q'], 'L0_ffn_W_k': _L0_ffn_in['W_k'], 'L0_ffn_W_v': _L0_ffn_in['W_v'], 'L0_ffn_W_out': _L0_ffn_in['W_out'], 'L0_ffn_b_out': _L0_ffn_in['b_out'], 'L0_ffn_temperature': _L0_ffn_in['temperature'], 'L1_attn_Wq': _L1_attn_in['Wq'], 'L1_attn_Wk': _L1_attn_in['Wk'], 'L1_attn_Wv': _L1_attn_in['Wv'], 'L1_attn_Wo': _L1_attn_in['Wo'], 'L1_ffn_sW1': _L1_ffn_in['sW1'], 'L1_ffn_sb1': _L1_ffn_in['sb1'], 'L1_ffn_sW2': _L1_ffn_in['sW2'], 'L1_ffn_sb2': _L1_ffn_in['sb2'], 'L1_ffn_sW3': _L1_ffn_in['sW3'], 'L1_ffn_sb3': _L1_ffn_in['sb3'], 'L1_ffn_eW1': _L1_ffn_in['eW1'], 'L1_ffn_eb1': _L1_ffn_in['eb1'], 'L1_ffn_eW2': _L1_ffn_in['eW2'], 'L1_ffn_eb2': _L1_ffn_in['eb2'], 'L1_ffn_eW3': _L1_ffn_in['eW3'], 'L1_ffn_eb3': _L1_ffn_in['eb3'], 'L1_ffn_gW': _L1_ffn_in['gW'], 'L1_ffn_gb': _L1_ffn_in['gb']}

def reference(x, txt, L0_tok_p_w, L0_tok_p_b, L0_tok_fw, L0_tok_w1_w, L0_tok_w1_b, L0_tok_w2_w, L0_tok_w2_b, L0_tok_q1_w, L0_tok_q1_b, L0_tok_q2_w, L0_tok_q2_b, L0_attn_wqv_w, L0_attn_wqv_b, L0_attn_wk, L0_attn_fanin_w, L0_attn_fanin_b, L0_ffn_W_fx, L0_ffn_b_fx, L0_ffn_W_x, L0_ffn_b_x, L0_ffn_W_slice, L0_ffn_b_slice, L0_ffn_W_q, L0_ffn_W_k, L0_ffn_W_v, L0_ffn_W_out, L0_ffn_b_out, L0_ffn_temperature, L1_attn_Wq, L1_attn_Wk, L1_attn_Wv, L1_attn_Wo, L1_ffn_sW1, L1_ffn_sb1, L1_ffn_sW2, L1_ffn_sb2, L1_ffn_sW3, L1_ffn_sb3, L1_ffn_eW1, L1_ffn_eb1, L1_ffn_eW2, L1_ffn_eb2, L1_ffn_eW3, L1_ffn_eb3, L1_ffn_gW, L1_ffn_gb):
    import jax
    import jax.numpy as jnp

    def _L0_tok_ref(x, p_w, p_b, fw, w1_w, w1_b, w2_w, w2_b, q1_w, q1_b, q2_w, q2_b):
        import jax, jax.numpy as jnp
        import numpy as np
        B, S, D_A, D_V, D_U, L, M1, M2 = (16, 64, 3, 32, 1, 4, 12, 12)
        MID = 4 * D_U

        def conv1x1(x, w, b):
            return jnp.einsum('bixy,oi->boxy', x, w) + b[None, :, None, None]

        def fourier_layer(x, fw_i):
            Bm, C, M, N = x.shape
            x_ft = jnp.fft.rfft2(x, s=(M, N), norm='ortho')
            w_lo = fw_i[0, ..., 0] + 1j * fw_i[0, ..., 1]
            w_hi = fw_i[1, ..., 0] + 1j * fw_i[1, ..., 1]
            lo = jnp.einsum('bixy,ioxy->boxy', x_ft[:, :, :M1, :M2], w_lo)
            hi = jnp.einsum('bixy,ioxy->boxy', x_ft[:, :, -M1:, :M2], w_hi)
            out_ft = jnp.zeros(x_ft.shape, dtype=x_ft.dtype)
            out_ft = out_ft.at[:, :, :M1, :M2].set(lo)
            out_ft = out_ft.at[:, :, -M1:, :M2].set(hi)
            return jnp.fft.irfft2(out_ft, s=(M, N), norm='ortho')

        def make_grid(b, sx, sy):
            gx = jnp.broadcast_to(jnp.linspace(0.0, 1.0, sx)[None, :, None], (b, sx, sy))
            gy = jnp.broadcast_to(jnp.linspace(0.0, 1.0, sy)[None, None, :], (b, sx, sy))
            return jnp.stack([gx, gy], axis=-1)
        b, sx, sy = (x.shape[0], x.shape[1], x.shape[2])
        grid = make_grid(b, sx, sy)
        h = jnp.concatenate([x, grid], axis=-1)
        h = jnp.transpose(h, (0, 3, 1, 2))
        h = conv1x1(h, p_w, p_b)
        for i in range(L):
            x1 = fourier_layer(h, fw[i])
            x1 = jax.nn.relu(conv1x1(x1, w1_w[i], w1_b[i]))
            x1 = conv1x1(x1, w2_w[i], w2_b[i])
            h = h + x1
        h = conv1x1(h, q1_w, q1_b)
        h = jax.nn.relu(h)
        h = conv1x1(h, q2_w, q2_b)
        return jnp.squeeze(h)

    def _L0_attn_ref(x, wqv_w, wqv_b, wk, fanin_w, fanin_b):
        import jax, jax.numpy as jnp
        import numpy as np
        D_MODEL = 64
        N_HEAD = 8

        def _l1_scores(q, k):
            scale = 1.0 / np.sqrt(q.shape[-1]).astype(np.float32)
            q_sbhw = q.transpose(1, 0, 2, 3)

            def one_query(qs):
                return -jnp.sum(jnp.abs(qs[:, None, :, :] - k), axis=-1) * scale
            s = jax.lax.map(one_query, q_sbhw)
            return s.transpose(1, 0, 2, 3)
        b, t, d = x.shape
        h = N_HEAD
        v = (x @ wqv_w.T + wqv_b).reshape(b, t, 3 * h, d)
        q, vf, vb = (v[:, :, :h], v[:, :, h:2 * h], v[:, :, 2 * h:])
        k = x[:, :, None, :] * wk[None, None]
        a = _l1_scores(q, k)
        a = jnp.concatenate([a, jnp.zeros((b, 1, t, h), a.dtype)], axis=1)
        a = jax.nn.softmax(a, axis=1)[:, :t]
        bf = jnp.einsum('bsdh,bshw->bdhw', a, vf)
        bb = jnp.einsum('bdsh,bshw->bdhw', a, vb)
        o = (bf + bb).sum(axis=2).reshape(b, t, d)
        y = o * jax.nn.sigmoid(1.702 * o)
        y = y @ fanin_w.T + fanin_b
        return x + y

    def _L0_ffn_ref(x, W_fx, b_fx, W_x, b_x, W_slice, b_slice, W_q, W_k, W_v, W_out, b_out, temperature):
        import jax, jax.numpy as jnp
        import numpy as np
        DIM = 64
        H = 8
        D = 64
        G = 64
        INNER = H * D
        SCALE = D ** (-0.5)
        B, N, _ = x.shape
        fx_mid = (x @ W_fx + b_fx).reshape(B, N, H, D).transpose(0, 2, 1, 3)
        x_mid = (x @ W_x + b_x).reshape(B, N, H, D).transpose(0, 2, 1, 3)
        temp = jnp.clip(temperature, 0.1, 5.0)
        slice_weights = jax.nn.softmax((x_mid @ W_slice + b_slice) / temp, axis=-1)
        slice_norm = slice_weights.sum(axis=2)
        slice_token = jnp.einsum('bhnc,bhng->bhgc', fx_mid, slice_weights)
        slice_token = slice_token / (slice_norm[..., None] + 1e-05)
        q = slice_token @ W_q
        k = slice_token @ W_k
        v = slice_token @ W_v
        attn = jax.nn.softmax(jnp.einsum('bhgc,bhkc->bhgk', q, k) * SCALE, axis=-1)
        out_slice = jnp.einsum('bhgk,bhkc->bhgc', attn, v)
        out_x = jnp.einsum('bhgc,bhng->bhnc', out_slice, slice_weights)
        out_x = out_x.transpose(0, 2, 1, 3).reshape(B, N, INNER)
        return out_x @ W_out + b_out

    def _L1_attn_ref(x, Wq, Wk, Wv, Wo):
        import jax, jax.numpy as jnp
        import numpy as np
        B, S, C = (8, 256, 64)
        H, KD = (8, 64)
        HEAD_DIM = KD // H
        b, s, c = x.shape
        q = jnp.einsum('bsc,oc->bso', x, Wq).reshape(b, s, H, KD).transpose(0, 2, 1, 3)
        k = jnp.einsum('bsc,oc->bos', x, Wk)
        v_conv = jnp.einsum('bsc,oc->bos', x, Wv)
        v = v_conv.reshape(b, s, KD)
        scale = 1.0 / np.sqrt(HEAD_DIM).astype(np.float32)
        scores = jnp.einsum('bhsd,bdt->bhst', q, k) * scale
        attn = jax.nn.softmax(scores, axis=-1)
        ctx = jnp.einsum('bhst,btd->bhsd', attn, v)
        ctx = ctx.transpose(0, 2, 1, 3).reshape(b, H * KD, s)
        out = jnp.einsum('bcp,oc->bop', ctx, Wo)
        return out.transpose(0, 2, 1)

    def _L1_ffn_ref(x, sW1, sb1, sW2, sb2, sW3, sb3, eW1, eb1, eW2, eb2, eW3, eb3, gW, gb):
        import jax, jax.numpy as jnp
        import numpy as np
        B, A = (1024, 8)
        IN, OUT = (64, 64)
        SH1, SH2 = (64, 128)
        EH1, EH2 = (128, 64)
        E, TOPK = (4, 2)

        def _shared_mlp(x, W1, b1, W2, b2, W3, b3):
            h = jax.nn.relu(x @ W1 + b1)
            h = jax.nn.relu(h @ W2 + b2)
            return h @ W3 + b3

        def _experts_mlp(x, eW1, eb1, eW2, eb2, eW3, eb3):
            h = jax.nn.relu(jnp.einsum('baf,efh->ebah', x, eW1) + eb1[:, None, None, :])
            h = jax.nn.relu(jnp.einsum('ebah,ehg->ebag', h, eW2) + eb2[:, None, None, :])
            o = jnp.einsum('ebag,ego->ebao', h, eW3) + eb3[:, None, None, :]
            return jnp.moveaxis(o, 0, -1)
        all_out = _experts_mlp(x, eW1, eb1, eW2, eb2, eW3, eb3)
        shared = _shared_mlp(x, sW1, sb1, sW2, sb2, sW3, sb3)
        gates = jax.nn.softmax(x @ gW + gb, axis=-1)
        topv, topi = jax.lax.top_k(gates, TOPK)
        topw = jax.nn.softmax(topv, axis=-1)
        sel = jnp.take_along_axis(all_out, topi[:, :, None, :], axis=-1)
        gated = jnp.sum(sel * topw[:, :, None, :], axis=-1)
        return shared + gated
    h = _L0_tok_ref(x, L0_tok_p_w, L0_tok_p_b, L0_tok_fw, L0_tok_w1_w, L0_tok_w1_b, L0_tok_w2_w, L0_tok_w2_b, L0_tok_q1_w, L0_tok_q1_b, L0_tok_q2_w, L0_tok_q2_b)
    h = jnp.concatenate([h, txt], axis=1)
    h = h + _L0_attn_ref(_layernorm(h, axis=-1), L0_attn_wqv_w, L0_attn_wqv_b, L0_attn_wk, L0_attn_fanin_w, L0_attn_fanin_b)
    h = h + _L0_ffn_ref(_layernorm(h, axis=-1), L0_ffn_W_fx, L0_ffn_b_fx, L0_ffn_W_x, L0_ffn_b_x, L0_ffn_W_slice, L0_ffn_b_slice, L0_ffn_W_q, L0_ffn_W_k, L0_ffn_W_v, L0_ffn_W_out, L0_ffn_b_out, L0_ffn_temperature)
    h = h + _L1_attn_ref(_layernorm(h, axis=-1), L1_attn_Wq, L1_attn_Wk, L1_attn_Wv, L1_attn_Wo)
    h = h + _L1_ffn_ref(_layernorm(h, axis=-1), L1_ffn_sW1, L1_ffn_sb1, L1_ffn_sW2, L1_ffn_sb2, L1_ffn_sW3, L1_ffn_sb3, L1_ffn_eW1, L1_ffn_eb1, L1_ffn_eW2, L1_ffn_eb2, L1_ffn_eW3, L1_ffn_eb3, L1_ffn_gW, L1_ffn_gb)
    return h

_drawn_inputs = setup_inputs


def setup_inputs(seed=0):
    import zlib

    import numpy as np

    out = dict(_drawn_inputs(seed))
    spreads = {'L0_tok_p_b': (0.0, 0.1),
     'L0_tok_w1_b': (0.0, 0.1),
     'L0_tok_w2_b': (0.0, 0.1),
     'L0_tok_q1_b': (0.0, 0.377),
     'L0_attn_wqv_b': (0.0, 0.8),
     'L0_attn_wk': (0.004999999888241291, 0.6),
     'L0_attn_fanin_b': (0.0, 0.1),
     'L0_ffn_b_fx': (0.0, 0.1),
     'L0_ffn_b_x': (0.0, 0.8),
     'L0_ffn_b_slice': (0.0, 0.8),
     'L0_ffn_b_out': (0.0, 0.1),
     'L0_ffn_temperature': (0.5, 0.6),
     'L1_ffn_sb1': (0.0, 2.0),
     'L1_ffn_sb2': (0.0, 0.315),
     'L1_ffn_sb3': (0.0, 0.1),
     'L1_ffn_eb1': (0.0, 0.8),
     'L1_ffn_eb2': (0.0, 0.698),
     'L1_ffn_eb3': (0.0, 0.399),
     'L1_ffn_gb': (0.0, 0.443)}
    factors = {'L0_attn_wqv_w': 8.0,
     'L0_attn_fanin_w': 8.0,
     'L0_ffn_W_x': 6.321,
     'L0_ffn_W_slice': 6.979,
     'L0_ffn_W_q': 8.0,
     'L0_ffn_W_k': 8.0,
     'L1_attn_Wq': 8.0,
     'L1_attn_Wk': 8.0,
     'L1_attn_Wv': 8.0,
     'L1_attn_Wo': 8.0,
     'L1_ffn_eW1': 3.692,
     'L1_ffn_eW2': 3.061,
     'L1_ffn_sW1': 5.309}
    for name, (base, spread) in spreads.items():
        noise = np.random.default_rng([zlib.crc32(name.encode()), seed]).standard_normal(out[name].shape)
        drawn = base * np.exp(spread * noise) if base else spread * noise
        out[name] = jnp.asarray(drawn.astype(out[name].dtype))
    for name, factor in factors.items():
        out[name] = (out[name] * factor).astype(out[name].dtype)
    return out
```

```python
from contextlib import ExitStack

import numpy as np

import concourse.bass as bass
from concourse import mybir

F32 = mybir.dt.float32
ALU = mybir.AluOpType
ACT = mybir.ActivationFunctionType
AX = mybir.AxisListType.X

B = 8
S = 64
CH = 32
LAYERS = 4
MODES_Y = 12
MODES_X = 24
MID = 4
NIMG = B + 3

T = 576
ROWS = 5 * B
EPS = 1e-5

def fno_constants():
    y = np.arange(S)
    ky = np.arange(MODES_Y)
    kx = np.concatenate([np.arange(MODES_Y), np.arange(S - MODES_Y, S)])
    x = np.arange(S)
    norm = 1.0 / np.sqrt(S)
    ay = 2 * np.pi * np.outer(y, ky) / S
    ax = 2 * np.pi * np.outer(x, kx) / S
    fy = np.zeros((2, S, 2, MODES_Y, 2))
    for r in range(2):
        fy[r, :, r, :, 0] = np.cos(ay) * norm
        fy[r, :, r, :, 1] = -np.sin(ay) * norm
    fx = np.zeros((S, 2, MODES_X, 2))
    fx[:, 0, :, 0] = np.cos(ax) * norm
    fx[:, 0, :, 1] = -np.sin(ax) * norm
    fx[:, 1, :, 0] = np.sin(ax) * norm
    fx[:, 1, :, 1] = np.cos(ax) * norm
    bx = np.zeros((MODES_X, 2, S, 2))
    bx[:, 0, :, 0] = np.cos(ax).T * norm
    bx[:, 0, :, 1] = np.sin(ax).T * norm
    bx[:, 1, :, 0] = -np.sin(ax).T * norm
    bx[:, 1, :, 1] = np.cos(ax).T * norm
    wy = np.where(ky == 0, 1.0, 2.0)[:, None]
    by = np.zeros((4, MODES_Y, 2, 2, 2, S))
    for r in range(4):
        by[r, :, 0, r // 2, r % 2, :] = wy * np.cos(ay).T * norm
        by[r, :, 1, r // 2, r % 2, :] = -wy * np.sin(ay).T * norm
    g = np.linspace(0.0, 1.0, S, dtype=np.float32)
    grid = np.stack([np.broadcast_to(g[:, None], (S, S)), np.broadcast_to(g[None, :], (S, S)), np.ones((S, S))])
    f32 = np.float32
    return {
        "c_fy": fy.reshape(128, 48).astype(f32),
        "c_fx": fx.reshape(128, 48).astype(f32),
        "c_bx": bx.reshape(48, 128).astype(f32),
        "c_by": by.reshape(96, 2 * 128).astype(f32),
        "c_grid": grid.astype(f32),
        "c_ident": np.eye(128, dtype=f32),
    }


def fno_layout(i, c):
    f32 = np.float32
    x = np.asarray(i["x"])[..., 0]
    img = np.concatenate([x, c["c_grid"]])
    a = {}
    a["f_img_pix"] = img.reshape(NIMG, 32, 128).transpose(2, 1, 0)
    a["f_img_row"] = img.reshape(NIMG, 32 * 128)
    pw, pb = np.asarray(i["L0_tok_p_w"]), np.asarray(i["L0_tok_p_b"])
    lift = np.zeros((NIMG, B, CH), f32)
    for b in range(B):
        lift[b, b] = pw[:, 0]
        lift[B, b] = pw[:, 1]
        lift[B + 1, b] = pw[:, 2]
        lift[B + 2, b] = pb
    a["f_lift"] = lift.reshape(NIMG, B * CH)
    a["f_lift_t"] = lift.reshape(NIMG, 2, 128).transpose(2, 1, 0)
    fw = np.asarray(i["L0_tok_fw"])
    a["f_modes"] = fw.transpose(0, 6, 2, 5, 1, 4, 3).reshape(LAYERS, 64, 288 * CH)
    w1, w2 = np.asarray(i["L0_tok_w1_w"]), np.asarray(i["L0_tok_w2_w"])
    a["f_w1t"] = np.tile(w1.transpose(0, 2, 1), (1, 4, 1))
    w2n = np.zeros((LAYERS, 4, CH, 4, CH), f32)
    w2t = np.zeros((LAYERS, 4, CH, 4, CH), f32)
    q1 = np.zeros((4, CH, 4, MID), f32)
    for b in range(4):
        w2n[:, b, :, b, :] = w2
        w2t[:, b, :, b, :] = w2.transpose(0, 2, 1)
        q1[b, :, b, :] = np.asarray(i["L0_tok_q1_w"]).T
    a["f_w2n"] = w2n.reshape(LAYERS, 128, 128)
    a["f_w2t"] = w2t.reshape(LAYERS, 128, 128)
    a["f_q1"] = q1.reshape(128, 16)
    a["f_b1"] = np.tile(np.asarray(i["L0_tok_w1_b"]), (1, B)).reshape(LAYERS, 1, B * CH)
    a["f_b2"] = np.tile(np.asarray(i["L0_tok_w2_b"]), (1, 4)).T
    a["f_q1b"] = np.broadcast_to(np.asarray(i["L0_tok_q1_b"]), (128, MID))
    a["f_q2"] = np.broadcast_to(np.asarray(i["L0_tok_q2_w"]).reshape(-1), (128, MID))
    a["f_q2b"] = np.broadcast_to(np.asarray(i["L0_tok_q2_b"]), (128, 1))
    return a


class BankRing:

    def __init__(self, owners, size):
        self.owners, self.size = owners, size
        self.per = {e: owners.count(e) for e in ("v", "a")}

    def emptied(self, n):
        return self.owners[n], self.owners[:n + 1].count(self.owners[n])

    def latest(self, fills):
        need = {}
        for n in fills:
            who, count = self.emptied(n)
            need[who] = max(need.get(who, 0), count)
        return sorted(need.items())


def fno_steps():
    steps = [("proj", 1), ("modes", 3), ("mix1", 12), ("inv_x", 6), ("turn_y", 8), ("inv_y", 16), ("turn_r", 16),
             ("fwd_y", 8), ("turn_x", 6), ("fwd_x", 4), ("mix2", 4)]
    first, owners = {}, []
    for name, n in steps:
        first[name] = len(owners)
        owners += ["v"] * n if name in ("mix2", "proj") else ["va"[k % 2] for k in range(n)]
    return first, owners


def fno_stage(nc, d, h_spatial):
    FIRST, OWNERS = fno_steps()
    ring = BankRing(OWNERS, 6)
    NG = len(OWNERS)
    assert NG % ring.size == 0
    with ExitStack() as ctx:
        def sb(n, shape, dt=F32):
            return ctx.enter_context(nc.sbuf_tensor("fno_" + n, shape, dt))

        def sem(n):
            return ctx.enter_context(nc.semaphore("fno_" + n))

        mid = ctx.enter_context(nc.psum_tensor("fno_mid", [128, 2, 512], F32))
        bank = ctx.enter_context(nc.psum_tensor("fno_bank", [128, 6, 512], F32))

        fy = sb("fy", [128, 48]); fx = sb("fx", [128, 48]); bx = sb("bx", [48, 128]); by = sb("by", [96, 2, 128])
        ident = sb("ident", [128, 128])
        img_pix = sb("img_pix", [128, 32, NIMG]); img_row = sb("img_row", [NIMG, 32, 128])
        lift = sb("lift", [NIMG, 2, 128]); lift_t = sb("lift_t", [128, 2, NIMG])
        q1 = sb("q1", [128, 16]); q1b = sb("q1b", [128, MID]); q2 = sb("q2", [128, MID]); q2b = sb("q2b", [128, 1])
        b2 = sb("b2", [128, LAYERS]); b2s = sb("b2s", [128, 1])
        w_modes = sb("w_modes", [64, 288, CH])
        w1t = sb("w1t", [128, LAYERS, CH]); w2n = sb("w2n", [128, LAYERS, 128]); w2t = sb("w2t", [128, LAYERS, 128])
        b1 = sb("b1", [1, LAYERS, B * CH]); b1c = sb("b1c", [1, B * CH])
        w1c = sb("w1c", [128, CH]); w2c = sb("w2c", [128, 2, 128])
        spec = sb("spec", [128, 3, 2, 288])
        lhs = sb("lhs", [64, 2, B, 288])
        y_out = sb("y_out", [128, 3, MODES_X, 2, B])
        v_in = sb("v_in", [128, MODES_Y, B * CH])
        t_x = sb("t_x", [128, 2, S, MODES_Y, 2])
        t_y = sb("t_y", [96, 16, B * CH])
        relu_u = sb("relu_u", [128, 32, B * CH])
        proj = sb("proj", [128, 16])
        r_t = sb("r_t", [128, 8, 512])
        g_y = t_x[:].rearrange("p g x k c -> p (g x k c)").rearrange("p (g k x c) -> p g k x c", g=2, k=MODES_Y, c=2)
        g_x = v_in[:].rearrange("p k n -> p (k n)").rearrange("p (t n) -> p t n", n=128)
        p_x = sb("p_x", [128, 2, 576])
        img_y = sb("img_y", [NIMG, MODES_Y, S, 2]); img_t = sb("img_t", [128, MODES_Y, NIMG]); img_x = sb("img_x", [NIMG, 576])
        q0 = sb("q0", [NIMG, 2, 16])
        hid = sb("hid", [128, 32, B, MID]); feat = sb("feat", [128, 32, B]); feat_r = sb("feat_r", [128, 2, 4, 32])
        tok = sb("tok", [128, 2, 128])

        s_const = sem("const"); s_wm = sem("w_modes"); s_wd = sem("modes_used")
        s_full = sem("bank_full"); s_ev = sem("emptied_v"); s_ea = sem("emptied_a")
        s_wc = sem("layer_weights"); s_b1 = sem("bias1_added"); s_spec = sem("spectrum"); s_dc = sem("constant_term")
        s_lhs = sem("lhs_loaded"); s_fin = sem("tail_v"); s_pre = sem("pre_pe")
        s_pv = sem("pre_v"); s_layer = sem("layer_projected"); s_turn = sem("tail_pe"); s_tok = sem("tok_out");
        emptied_sem = {"v": s_ev, "a": s_ea}

        def emptied(eng, l, n):
            who, count = ring.emptied(n)
            eng.wait_ge(emptied_sem[who], l * ring.per[who] + count)

        def step_in_sbuf(eng, l, name, n):
            last = {}
            for k in range(FIRST[name], FIRST[name] + n):
                last[OWNERS[k]] = k
            for k in last.values():
                emptied(eng, l, k)

        block = ctx.enter_context(nc.Block())
        loads = [(fy, "c_fy"), (fx, "c_fx"), (bx, "c_bx"), (ident, "c_ident"), (q1, "f_q1"), (q1b, "f_q1b"),
                 (q2, "f_q2"), (q2b, "f_q2b"), (b2, "f_b2"), (img_pix, "f_img_pix"), (lift_t, "f_lift_t")]
        NCONST = 16 * (len(loads) + 7)

        @block.sync
        def _(sp):
            for t, name in loads:
                sp.dma_start(t[:], d[name]).then_inc(s_const, 16)
            sp.dma_start(by[:], d["c_by"].rearrange("p (s n) -> p s n", s=2)).then_inc(s_const, 16)
            sp.dma_start(img_row[:], d["f_img_row"].rearrange("p (s n) -> p s n", s=32)).then_inc(s_const, 16)
            sp.dma_start(lift[:], d["f_lift"].rearrange("p (s n) -> p s n", s=2)).then_inc(s_const, 16)
            sp.dma_start(w1t[:], d["f_w1t"].rearrange("l p n -> p l n")).then_inc(s_const, 16)
            sp.dma_start(w2n[:], d["f_w2n"].rearrange("l p n -> p l n")).then_inc(s_const, 16)
            sp.dma_start(w2t[:], d["f_w2t"].rearrange("l p n -> p l n")).then_inc(s_const, 16)
            sp.dma_start(b1[:], d["f_b1"].rearrange("l p n -> p l n")).then_inc(s_const, 16)

            def gather(l):
                sp.wait_ge(s_spec, l + 1)
                for c2, plane in ((0, (0, 1)), (1, (2, 0))):
                    for c in range(2):
                        for b4 in range(4):
                            sp.dma_start(lhs[32 * c2:32 * c2 + 32, c, :, :].rearrange("p (g b) m -> p g b m", g=2)[:, :, b4, :],
                                         spec[32 * b4:32 * b4 + 32, plane[c], :, :]).then_inc(s_lhs, 16)

            gather(0)
            with sp.Fori(1, LAYERS) as l:
                gather(l)
            for g in range(2):
                for b4 in range(4):
                    if g == 0 and b4 == 0:
                        sp.wait_ge(s_fin, 6)
                    sp.dma_start(h_spatial[4 * g + b4].rearrange("(a r) y -> a (r y)", r=2),
                                 tok[32 * b4:32 * b4 + 32, g, :]).then_inc(s_tok, 16)
            sp.wait_ge(s_tok, 16 * 8)

        @block.gpsimd
        def _(pool):
            pool.dma_start(w_modes[:], d["f_modes"][0].rearrange("p (m o) -> p m o", o=CH)).then_inc(s_wm, 16)
            with pool.Fori(1, LAYERS) as l:
                pool.wait_ge(s_full, (l - 1) * NG + 4)
                pool.dma_start(w_modes[:], d["f_modes"][bass.ds(l, 1)].rearrange("a p (m o) -> p (a m) o", o=CH)).then_inc(s_wm, 16)

        def add_spectrum(src, g, half, first):
            for c in range(2):
                dst = spec[:, c, g, 144 * half:144 * half + 144]
                if first:
                    i = nc.vector.tensor_copy(dst, src[:, c:288:2])
                else:
                    i = nc.vector.tensor_tensor(dst, dst, src[:, c:288:2], ALU.add)
            return i

        def empty_banks(eng, l, me):
            done = emptied_sem[me]

            def move(out, in_):
                return nc.vector.tensor_copy(out, in_) if me == "v" else nc.scalar.copy(out, in_)

            def mine(name, n):
                for k in range(n):
                    at = FIRST[name] + k
                    if OWNERS[at] == me:
                        eng.wait_ge(s_full, l * NG + at + 1)
                        yield k, bank[:, at % ring.size, :]

            for _, src in mine("proj", 1):
                move(proj[:], src[:, 0:16]).then_inc(done, 1)
            for r, src in mine("modes", 3):
                move(y_out[:, r].rearrange("p k c b -> p (k c b)"), src[:, 0:384]).then_inc(done, 1)
            for ky, src in mine("mix1", 12):
                i = move(v_in[0:48, ky, :], src[0:48, 0:256])
                if ky:
                    i.then_inc(done, 1)
                    continue
                i.then_inc(s_b1, 1)
                eng.wait_ge(s_b1, l + 1)
                nc.vector.scalar_tensor_tensor(out=v_in[0:1, 0, :], in0=b1c[:, :], scalar=float(S), in1=v_in[0:1, 0, :],
                                               op0=ALU.mult, op1=ALU.add).then_inc(done, 1)
            for k, src in mine("inv_x", 6):
                g, ky = divmod(4 * k, 12)
                move(t_x[:, g, :, ky:ky + 4, :].rearrange("p x k c -> p k x c"),
                     src.rearrange("p (k x c) -> p k x c", k=4, c=2)).then_inc(done, 1)
            for k, src in mine("turn_y", 8):
                move(t_y[:, 2 * k:2 * k + 2, :].rearrange("p a n -> p (a n)"), src[0:96, :]).then_inc(done, 1)
            for k, src in mine("inv_y", 16):
                out = relu_u[:, 2 * k:2 * k + 2, :].rearrange("p a n -> p (a n)")
                if me == "v":
                    nc.vector.tensor_scalar(out, src, 0.0, None, ALU.max).then_inc(done, 1)
                else:
                    nc.scalar.activation(out, src, ACT.Relu).then_inc(done, 1)
            for k, src in mine("turn_r", 16):
                move(r_t[:, k % 8, :], src).then_inc(done, 1)
            for k, src in mine("fwd_y", 8):
                g, x0 = k // 4, 16 * (k % 4)
                move(g_y[:, g, :, x0:x0 + 16, :].rearrange("p k x c -> p x k c"),
                     src[:, 0:384].rearrange("p (x k c) -> p x k c", x=16, c=2)).then_inc(done, 1)
            for k, src in mine("turn_x", 6):
                move(g_x[:, 4 * k:4 * k + 4, :].rearrange("p t n -> p (t n)"), src).then_inc(done, 1)
            for k, src in mine("fwd_x", 4):
                move(p_x[:, k // 2, 288 * (k % 2):288 * (k % 2) + 288], src[:, 0:288]).then_inc(done, 1)
            for k, src in mine("mix2", 4):
                add_spectrum(src, k // 2, k % 2, False).then_inc(done, 1)

        @block.scalar
        def _(act):
            with act.Fori(0, LAYERS) as l:
                empty_banks(act, l, "a")

        @block.vector
        def _(v):
            v.wait_ge(s_const, NCONST)
            nc.vector.tensor_reduce(b2s[:], b2[:], AX, ALU.add).then_inc(s_pv, 1)
            v.wait_ge(s_pv, 1)
            for g in range(2):
                nc.vector.tensor_tensor(lift_t[:, g, NIMG - 1:NIMG], lift_t[:, g, NIMG - 1:NIMG], b2s[:], ALU.add).then_inc(s_pv, 1)
            for k in range(4):
                v.wait_ge(s_pre, k + 1)
                nc.vector.tensor_copy(img_y[:, :, 16 * k:16 * k + 16, :].rearrange("p k x c -> p x k c"),
                                      bank[0:NIMG, k, 0:384].rearrange("p (x k c) -> p x k c", x=16, c=2)).then_inc(s_pv, 1)
            v.wait_ge(s_pre, 5)
            nc.vector.tensor_copy(img_t[:].rearrange("p k n -> p (k n)"), bank[:, 4, 0:12 * NIMG]).then_inc(s_pv, 1)
            v.wait_ge(s_pre, 6)
            nc.vector.tensor_copy(q0[:].rearrange("p g n -> p (g n)"), bank[0:NIMG, 5, 0:32]).then_inc(s_pv, 1)
            for k in range(2):
                v.wait_ge(s_pre, 7 + k)
                nc.vector.tensor_copy(img_x[:, 288 * k:288 * k + 288], bank[0:NIMG, k, 0:288]).then_inc(s_pv, 1)
            for k in range(4):
                v.wait_ge(s_pre, 9 + k)
                add_spectrum(bank[:, 2 + k, :], k // 2, k % 2, True).then_inc(s_pv, 1)
            v.wait_ge(s_pv, 15)
            nc.vector.tensor_scalar(spec[:, 2, :, :], spec[:, 1, :, :], -1.0, None, ALU.mult).then_inc(s_spec, 1)

            with v.Fori(0, LAYERS) as l:
                nc.vector.tensor_copy(w1c[:], w1t[:, bass.ds(l, 1), :].rearrange("p a n -> p (a n)")).then_inc(s_wc, 1)
                nc.vector.tensor_copy(w2c[:, 0, :], w2n[:, bass.ds(l, 1), :].rearrange("p a n -> p (a n)")).then_inc(s_wc, 1)
                nc.vector.tensor_copy(w2c[:, 1, :], w2t[:, bass.ds(l, 1), :].rearrange("p a n -> p (a n)")).then_inc(s_wc, 1)
                nc.vector.tensor_copy(b1c[:], b1[:, bass.ds(l, 1), :].rearrange("p a n -> p (a n)")).then_inc(s_wc, 1)
                empty_banks(v, l, "v")
                v.wait_ge(s_ev, (l + 1) * ring.per["v"])
                for g in range(2):
                    nc.vector.scalar_tensor_tensor(out=spec[:, 0, g, 0:1], in0=b2[:, bass.ds(l, 1)], scalar=float(S),
                                                   in1=spec[:, 0, g, 0:1], op0=ALU.mult, op1=ALU.add).then_inc(s_dc, 1)
                v.wait_ge(s_dc, l * 2 + 2)
                nc.vector.tensor_scalar(spec[:, 2, :, :], spec[:, 1, :, :], -1.0, None, ALU.mult).then_inc(s_spec, 1)

            v.wait_ge(s_layer, LAYERS)
            h3 = hid[:].rearrange("p x b j -> p (x b) j")
            nc.vector.tensor_tensor(h3, mid[:].rearrange("p k (n j) -> p (k n) j", j=MID),
                                    q1b[:, None, :].broadcast_to([128, 256, MID]), ALU.add).then_inc(s_fin, 1)
            v.wait_ge(s_fin, 1)
            nc.vector.scalar_tensor_tensor(out=h3, in0=h3, scalar=0.0, in1=q2[:, None, :].broadcast_to([128, 256, MID]),
                                           op0=ALU.max, op1=ALU.mult).then_inc(s_fin, 1)
            v.wait_ge(s_fin, 2)
            nc.vector.tensor_reduce(feat[:].rearrange("p x b -> p (x b)"), h3, AX, ALU.add).then_inc(s_fin, 1)
            v.wait_ge(s_fin, 3)
            nc.vector.tensor_scalar(feat_r[:].rearrange("p g b x -> p (g b) x"), feat[:].rearrange("p x b -> p b x"),
                                    q2b[:, 0:1], None, ALU.add).then_inc(s_fin, 1)
            for g in range(2):
                v.wait_ge(s_turn, g + 1)
                nc.vector.tensor_copy(tok[:, g, :], bank[:, g, 0:128]).then_inc(s_fin, 1)

        @block.tensor
        def _(pe):
            mm = nc.tensor.matmul
            pe.wait_ge(s_const, NCONST)
            for xh in range(32):
                i = mm(bank[0:NIMG, xh // 8, 48 * (xh % 8):48 * (xh % 8) + 48], img_pix[:, xh, :], fy[:], start=True, stop=True)
                if xh % 8 == 7:
                    i.then_inc(s_pre, 1)
            pe.wait_ge(s_pv, 7)
            for ky in range(12):
                i = nc.tensor.transpose(bank[:, 4, NIMG * ky:NIMG * ky + NIMG], img_y[:, ky, :, :].rearrange("p x c -> p (x c)"),
                                        ident[0:NIMG, 0:NIMG])
            i.then_inc(s_pre, 1)
            for g in range(2):
                i = mm(bank[0:NIMG, 5, 16 * g:16 * g + 16], lift_t[:, g, :], q1[:], start=True, stop=True)
            i.then_inc(s_pre, 1)
            pe.wait_ge(s_pv, 8)
            for ky in range(12):
                i = mm(bank[0:NIMG, ky // 6, 48 * (ky % 6):48 * (ky % 6) + 48], img_t[:, ky, :], fx[:], start=True, stop=True)
                if ky % 6 == 5:
                    i.then_inc(s_pre, 1)
            pe.wait_ge(s_pv, 11)
            for k in range(4):
                mm(bank[:, 2 + k, 0:288], lift[:, k // 2, :], img_x[:, 288 * (k % 2):288 * (k % 2) + 288], start=True, stop=True).then_inc(s_pre, 1)
            for xh in range(32):
                mm(mid[:, xh // 16, 32 * (xh % 16):32 * (xh % 16) + 32], img_row[:, xh, :], q0[:].rearrange("p g n -> p (g n)"),
                   start=(xh % 16 == 0), stop=False, skip_group_check=True)

            with pe.Fori(0, LAYERS) as l:
                def fill(name, k):
                    n = FIRST[name] + k
                    if n >= ring.size:
                        emptied(pe, l, n - ring.size)
                    return bank[:, n % ring.size, :]

                pe.wait_ge(s_lhs, 16 * 16 * (l + 1))
                pe.wait_ge(s_wm, 16 * (l + 1))
                pe.wait_ge(s_wc, 4 * (l + 1))
                out = fill("proj", 0)
                mm(out[:, 0:16], w2c[:, 0, :], q1[:], start=True, stop=True).then_inc(s_full, 1)
                for r in range(3):
                    out = fill("modes", r)
                    for kx in range(MODES_X):
                        for q in range(4):
                            m = (4 * r + q) * MODES_X + kx
                            i = mm(out[32 * q:32 * q + 32, 16 * kx:16 * kx + 16], w_modes[:, m, :], lhs[:, :, :, m],
                                   start=True, stop=True, tile_position=(0, 32 * q))
                    i.then_inc(s_full, 1)
                for ky in range(12):
                    r, q = divmod(ky, 4)
                    if q == 0:
                        emptied(pe, l, FIRST["modes"] + r)
                    out = fill("mix1", ky)
                    for b in range(B):
                        i = mm(out[0:48, 32 * b:32 * b + 32], y_out[32 * q:32 * q + 32, r, :, :, b].rearrange("p k c -> p (k c)"),
                               w1c[32 * q:32 * q + 32, :], start=True, stop=True, tile_position=(32 * q, 0))
                    i.then_inc(s_full, 1)
                step_in_sbuf(pe, l, "mix1", 12)
                for k in range(6):
                    out = fill("inv_x", k)
                    for j in range(4):
                        g, ky = divmod(4 * k + j, 12)
                        i = mm(out[:, 128 * j:128 * j + 128], v_in[0:48, ky, 128 * g:128 * g + 128], bx[:], start=True, stop=True)
                    i.then_inc(s_full, 1)
                step_in_sbuf(pe, l, "inv_x", 6)
                for k in range(8):
                    out = fill("turn_y", k)
                    for j in range(4):
                        x4, g = 2 * k + j // 2, j % 2
                        i = nc.tensor.transpose(out[0:96, 128 * j:128 * j + 128],
                                                t_x[:, g, 4 * x4:4 * x4 + 4, :, :].rearrange("p x k c -> p (x k c)"), ident[:])
                    i.then_inc(s_full, 1)
                for k in range(16):
                    emptied(pe, l, FIRST["turn_y"] + k // 2)
                    out = fill("inv_y", k)
                    for j in range(2):
                        i = mm(out[:, 256 * j:256 * j + 256], by[:, j, :], t_y[:, k, :], start=True, stop=True)
                    i.then_inc(s_full, 1)
                def project(k):
                    emptied(pe, l, FIRST["turn_r"] + k)
                    for j in range(4):
                        xh, g = 2 * k + j // 2, j % 2
                        at = 32 * (xh % 16) + 16 * g
                        i = mm(mid[:, xh // 16, at:at + 16], r_t[:, k % 8, 128 * j:128 * j + 128], proj[:],
                               start=False, stop=False, skip_group_check=True)
                    return i

                for k in range(16):
                    emptied(pe, l, FIRST["inv_y"] + k)
                    out = fill("turn_r", k)
                    for j in range(4):
                        xh, g = 2 * k + j // 2, j % 2
                        i = nc.tensor.transpose(out[:, 128 * j:128 * j + 128], relu_u[:, xh, 128 * g:128 * g + 128], ident[:])
                    i.then_inc(s_full, 1)
                    if k >= 2:
                        project(k - 2)
                project(14)
                project(15).then_inc(s_layer, 1)
                for k in range(8):
                    out = fill("fwd_y", k)
                    for j in range(8):
                        g, xh = k // 4, 8 * (k % 4) + j
                        i = mm(out[:, 48 * j:48 * j + 48], relu_u[:, xh, 128 * g:128 * g + 128], fy[:], start=True, stop=True)
                    i.then_inc(s_full, 1)
                step_in_sbuf(pe, l, "fwd_y", 8)
                for k in range(6):
                    out = fill("turn_x", k)
                    for j in range(4):
                        g, ky = divmod(4 * k + j, 12)
                        i = nc.tensor.transpose(out[:, 128 * j:128 * j + 128], g_y[:, g, ky, :, :].rearrange("p x c -> p (x c)"), ident[:])
                    i.then_inc(s_full, 1)
                step_in_sbuf(pe, l, "turn_x", 6)
                for k in range(4):
                    out = fill("fwd_x", k)
                    for j in range(6):
                        i = mm(out[:, 48 * j:48 * j + 48], g_x[:, 6 * k + j, :], fx[:], start=True, stop=True)
                    i.then_inc(s_full, 1)
                for k in range(4):
                    emptied(pe, l, FIRST["fwd_x"] + k)
                    out = fill("mix2", k)
                    mm(out[:, 0:288], w2c[:, 1, :], p_x[:, k // 2, 288 * (k % 2):288 * (k % 2) + 288], start=True, stop=True).then_inc(s_full, 1)

            pe.wait_ge(s_fin, 4)
            for g in range(2):
                nc.tensor.transpose(bank[:, g, 0:128], feat_r[:, g, :, :].rearrange("p b x -> p (b x)"), ident[:]).then_inc(s_turn, 1)


def wait_apart(eng, met, sem, value):
    if not isinstance(value, int):
        value = eng.to_reg(value)
    eng.wait_ge(*met)
    eng.wait_ge(sem, value)


def load_tokens(nc, d, h_spatial, res):
    with ExitStack() as ctx:
        s_in = ctx.enter_context(nc.semaphore("tok_loaded"))
        s_pad = ctx.enter_context(nc.semaphore("tok_pad"))
        r4 = res[:].rearrange("p (b c) f -> p b c f", b=B)
        block = ctx.enter_context(nc.Block())

        @block.sync
        def _(sp):
            txt = d["txt"]
            sp.dma_start(r4[0:64, :, 0, :], h_spatial.rearrange("b t f -> t b f")).then_inc(s_in, 16)
            sp.dma_start(r4[64:128, :, 0, :], txt[:, 0:64, :].rearrange("b t f -> t b f")).then_inc(s_in, 16)
            for c in range(1, 4):
                sp.dma_start(r4[:, :, c, :], txt[:, 128 * c - 64:128 * c + 64, :].rearrange("b t f -> t b f")).then_inc(s_in, 16)
            sp.dma_start(r4[0:64, :, 4, :], txt[:, 448:512, :].rearrange("b t f -> t b f")).then_inc(s_in, 16)
            sp.wait_ge(s_in, 16 * 6)

        @block.gpsimd
        def _(pool):
            nc.gpsimd.memset(r4[64:128, :, 4, :], 0.0).then_inc(s_pad, 1)
            pool.wait_ge(s_pad, 1)


def norm_stage(nc, tag, res, xn, xt, ident):
    PARTS = 4
    W = ROWS // PARTS
    with ExitStack() as ctx:
        def sb(n, shape, dt=F32):
            return ctx.enter_context(nc.sbuf_tensor(f"{tag}_{n}", shape, dt))

        def sem(n):
            return ctx.enter_context(nc.semaphore(f"{tag}_{n}"))

        sq = sb("sq", [128, ROWS, S])
        total = sb("total", [128, ROWS]); mean = sb("mean", [128, ROWS]); var = sb("var", [128, ROWS])
        std = sb("std", [128, ROWS]); rstd = sb("rstd", [128, ROWS]); eps = sb("eps", [128, 1])
        turned = ctx.enter_context(nc.psum_tensor(f"{tag}_turned", [128, 4, 1024], F32))
        s_one = sem("ones"); s_sum = sem("sum"); s_mean = sem("mean"); s_cen = sem("centred"); s_sq = sem("squares")
        s_var = sem("var"); s_std = sem("std"); s_rstd = sem("rstd"); s_xn = sem("xn"); s_turn = sem("turned"); s_out = sem("xt")
        block = ctx.enter_context(nc.Block())

        @block.gpsimd
        def _(pool):
            nc.gpsimd.memset(eps[:], EPS).then_inc(s_one, 1)
            pool.wait_ge(s_one, 1)
            nc.gpsimd.memset(xn[:, :, S:S + 1], 1.0).then_inc(s_one, 1)
            pool.wait_ge(s_one, 2)
            nc.gpsimd.memset(xt[S:S + 1, :, :], 1.0).then_inc(s_one, 1)
            pool.wait_ge(s_one, 3)

        @block.vector
        def _(v):
            for p in range(PARTS):
                rows = slice(W * p, W * p + W)
                nc.vector.tensor_reduce(total[:, rows], res[:, rows, :], AX, ALU.add).then_inc(s_sum, 1)
            for p in range(PARTS):
                rows = slice(W * p, W * p + W)
                v.wait_ge(s_sum, p + 1)
                nc.vector.tensor_scalar(mean[:, rows], total[:, rows], 1.0 / S, None, ALU.mult).then_inc(s_mean, 1)
            for p in range(PARTS):
                rows = slice(W * p, W * p + W)
                v.wait_ge(s_mean, p + 1)
                nc.vector.tensor_tensor(xn[:, rows, 0:S], res[:, rows, :], mean[:, rows, None].broadcast_to([128, W, S]),
                                        ALU.subtract).then_inc(s_cen, 1)
            for p in range(PARTS):
                rows = slice(W * p, W * p + W)
                v.wait_ge(s_cen, p + 1)
                nc.vector.tensor_tensor(sq[:, rows, :], xn[:, rows, 0:S], xn[:, rows, 0:S], ALU.mult).then_inc(s_sq, 1)
                v.wait_ge(s_sq, p + 1)
                nc.vector.tensor_reduce(var[:, rows], sq[:, rows, :], AX, ALU.add).then_inc(s_var, 1)
            for p in range(PARTS):
                rows = slice(W * p, W * p + W)
                v.wait_ge(s_std, p + 1)
                nc.vector.reciprocal(rstd[:, rows], std[:, rows]).then_inc(s_rstd, 1)
                v.wait_ge(s_rstd, p + 1)
                nc.vector.tensor_tensor(xn[:, rows, 0:S], xn[:, rows, 0:S], rstd[:, rows, None].broadcast_to([128, W, S]),
                                        ALU.mult).then_inc(s_xn, 1)

        @block.scalar
        def _(act):
            act.wait_ge(s_one, 3)
            for p in range(PARTS):
                rows = slice(W * p, W * p + W)
                act.wait_ge(s_var, p + 1)
                nc.scalar.activation(std[:, rows], var[:, rows], ACT.Sqrt, bias=eps[:, 0:1], scale=1.0 / S).then_inc(s_std, 1)
            for b in range(B):
                act.wait_ge(s_turn, b + 1)
                nc.scalar.copy(xt[0:S, b, :], turned[0:S, b % 4, 0:T]).then_inc(s_out, 1)

        @block.tensor
        def _(pe):
            for b in range(B):
                if b % 2 == 0:
                    pe.wait_ge(s_xn, b // 2 + 1)
                if b >= 4:
                    pe.wait_ge(s_out, b - 3)
                for c in range(5):
                    n = min(128, T - 128 * c)
                    i = nc.tensor.transpose(turned[0:S, b % 4, 128 * c:128 * c + n], xn[0:n, 5 * b + c, 0:S], ident[0:n, 0:n])
                i.then_inc(s_turn, 1)


def l1_layout(i):
    f32 = np.float32
    w, bias = np.asarray(i["L0_attn_wqv_w"]), np.asarray(i["L0_attn_wqv_b"])
    wt = np.concatenate([w.T, bias[None]])
    wk = np.asarray(i["L0_attn_wk"])
    a = {"l1_wq": wt[:, :512], "l1_wvf": wt[:, 512:1024]}
    wb = w[1024:].reshape(4, 2, S, S)
    both = np.zeros((2, S, 4, S + 1), f32)
    both[:, :, :, :S] = wb.transpose(1, 3, 0, 2)
    both[:, :, :, S] = wk.reshape(4, 2, S).transpose(1, 2, 0)
    a["l1_wvb"] = both.reshape(128, 4 * 65)
    bb = np.zeros((2, 4, S + 1), f32)
    bb[:, :, :S] = bias[1024:].reshape(4, 2, S).transpose(1, 0, 2)
    a["l1_bvb"] = bb.reshape(2, 4 * 65)
    a["l1_wk"] = wk.reshape(4, 128).T
    a["l1_fan"] = np.concatenate([np.asarray(i["L0_attn_fanin_w"]).T, np.asarray(i["L0_attn_fanin_b"])[None]])
    return a


def l1_constants():
    f32 = np.float32
    dup = np.concatenate([np.eye(S), np.eye(S)], 1)
    sel = np.zeros((128, 62))
    sel[:64, 30] = 2.0
    sel[64:, 31] = 2.0
    neg = np.zeros((2, S, S, 2))
    par = np.zeros((2, S, 2))
    for h in range(2):
        neg[h, :, :, h] = -1.0
        par[h, :, h] = 1.0
    return {"c_dup": dup.astype(f32), "c_sel": sel.astype(f32), "c_neg": neg.reshape(128, 128).astype(f32),
            "c_par": par.reshape(2, 128).astype(f32)}


def l1_stage(nc, d, xt, o_query, o_key, ident):
    RING = 16
    GROUPS = 16
    SCALE = 1.0 / 8.0
    FILLS = ["v"] * 2 + ["va"[k % 2] for k in range(22)]
    fills = BankRing(FILLS, 6)
    with ExitStack() as ctx:
        def sb(n, shape, dt=F32):
            return ctx.enter_context(nc.sbuf_tensor("l1_" + n, shape, dt))

        def sem(n):
            return ctx.enter_context(nc.semaphore("l1_" + n))

        wq = sb("wq", [65, 512]); wvf = sb("wvf", [65, 512]); wvb = sb("wvb", [128, 4, 65]); bvb = sb("bvb", [2, 4 * 65])
        wk = sb("wk", [128, 4]); nwk = sb("nwk", [128, 4])
        dup = sb("dup", [64, 128]); sel = sb("sel", [128, 62]); neg = sb("neg", [128, 128]); par = sb("par", [2, 128])
        xs = sb("xs", [65, T]); xdup = sb("xdup", [128, T]); xpar = sb("xpar", [128, T, 2])
        q = sb("q", [128, 4, T]); nk = sb("nk", [128, 36 * 64])
        vf = sb("vf", [128, 5, 512]); vb = sb("vb", [128, 36, 65])
        nks = sb("nks", [128, 3, 64])
        unit = sb("unit", [128, RING, T])
        e = sb("e", [128, 3, T]); z = sb("z", [128, 3]); z1 = sb("z1", [128, 3]); rz = sb("rz", [128, 3])
        at = sb("at", [128, 3, 5, 128])
        okf = sb("okf", [64, 36, S]); oks = sb("oks", [64, 9, S])
        score = ctx.enter_context(nc.psum_tensor("l1_score", [128, 6, 512], F32))
        turn = ctx.enter_context(nc.psum_tensor("l1_turn", [128, 512], F32))
        acc = ctx.enter_context(nc.psum_tensor("l1_acc", [128, 512], F32))

        s_w = sem("weights"); s_init = sem("init"); s_xs = sem("xs"); s_fill = sem("fill"); s_fv = sem("fill_emptied_v")
        s_fa = sem("fill_emptied_a"); s_xp = sem("x_by_parity"); s_nk = sem("minus_k"); s_nks = sem("minus_k_staged")
        s_uv = sem("units_v"); s_ua = sem("units_a"); s_use = sem("units_summed"); s_e = sem("exp")
        s_z1 = sem("z1"); s_rz = sem("rz"); s_p = sem("probs"); s_t = sem("turned"); s_ata = sem("at_a"); s_atv = sem("at_v")
        s_k = sem("key_out"); s_kc = sem("key_out_copied"); s_acc = sem("acc_copied"); s_add = sem("key_out_summed"); s_od = sem("o_key_moved")
        filled = {"v": s_fv, "a": s_fa}
        by_vector = [[True, False, True, g % 2 == 1] for g in range(GROUPS)]

        def emptied(eng, b, n):
            who, count = fills.emptied(n)
            eng.wait_ge(filled[who], b * fills.per[who] + count)

        block = ctx.enter_context(nc.Block())

        @block.sync
        def _(sp):
            for t, name in ((wq, "l1_wq"), (wvf, "l1_wvf"), (bvb, "l1_bvb"), (wk, "l1_wk"), (dup, "c_dup"), (sel, "c_sel"),
                            (neg, "c_neg"), (par, "c_par")):
                sp.dma_start(t[:], d[name]).then_inc(s_w, 16)
            sp.dma_start(wvb[:], d["l1_wvb"].rearrange("p (a n) -> p a n", a=4)).then_inc(s_w, 16)
            with sp.Fori(0, B) as b:
                sp.wait_ge(s_add, 3 * b + 3)
                sp.dma_start(o_key[0:64, bass.ds(5 * b, 5), :], oks[:, 0:9:2, :]).then_inc(s_od, 16)
                sp.dma_start(o_key[64:128, bass.ds(5 * b, 4), :], oks[:, 1:9:2, :]).then_inc(s_od, 16)

        def tiles(b, it, first):
            for k in range(3):
                prev = None if first and k == 0 else ((it - 1, 2) if k == 0 else (it, k - 1))
                yield k, prev

        def trips(eng, b, body, last):
            body(0, True)
            with eng.Fori(1, 12) as it:
                body(it, False)
            last(11, 2)

        @block.gpsimd
        def _(pool):
            for n, t in enumerate((xpar, vf, at, o_key, o_query)):
                if n:
                    pool.wait_ge(s_init, n)
                nc.gpsimd.memset(t[:], 0.0).then_inc(s_init, 1)
            with pool.Fori(0, B) as b:
                def stage(it, first):
                    for k in range(3):
                        n = 36 * b + 3 * it + k
                        if k == 0 and first:
                            wait_apart(pool, (s_w, 16 * 9), s_nk, 4 * b + 4)
                        if not first:
                            wait_apart(pool, (s_w, 16 * 9), s_uv, (n - 2) * GROUPS)
                            wait_apart(pool, (s_w, 16 * 9), s_ua, (n - 2) * GROUPS)
                        nc.gpsimd.tensor_copy(nks[:, k, :], nk[:, bass.ds(192 * it + 64 * k, 64)]).then_inc(s_nks, 1)

                stage(0, True)
                with pool.Fori(1, 12) as it:
                    stage(it, False)

        def empty_fills(me, got):
            def move(out, in_):
                i = nc.vector.tensor_copy(out, in_) if me == "v" else nc.scalar.copy(out, in_)
                i.then_inc(filled[me], 1)

            for n in range(2, 24):
                if FILLS[n] != me:
                    continue
                src = got(n)
                if n < 10:
                    hp, half = divmod(n - 2, 2)
                    move(q[:, hp, 288 * half:288 * half + 288], src[:, 0:288])
                elif n < 15:
                    rows = 128 if n < 14 else 64
                    move(vf[0:rows, n - 10, :], src[0:rows, :])
                else:
                    move(vb[:, n - 15:36:9, :], src[:, 0:260].rearrange("p (a n) -> p a n", a=4))

        @block.vector
        def _(v):
            v.wait_ge(s_w, 16 * 9)
            v.wait_ge(s_init, 5)
            nc.vector.tensor_scalar(nwk[:], wk[:], -1.0, None, ALU.mult).then_inc(s_z1, 1)
            nc.vector.tensor_scalar(wvb[:, :, S:S + 1], wvb[:, :, S:S + 1], -SCALE, None, ALU.mult).then_inc(s_z1, 1)
            with v.Fori(0, B) as b:
                nc.vector.tensor_copy(xs[:], xt[:, bass.ds(b, 1), :].rearrange("p a t -> p (a t)")).then_inc(s_xs, 1)

                def got(n):
                    v.wait_ge(s_fill, 24 * b + n + 1)
                    return score[:, n % 6, :]

                for n in range(2):
                    nc.vector.tensor_copy(xdup[:, 288 * n:288 * n + 288], got(n)[:, 0:288]).then_inc(s_fv, 1)
                v.wait_ge(s_fv, fills.per["v"] * b + 2)
                for h in range(2):
                    half = slice(64 * h, 64 * h + 64)
                    nc.vector.tensor_copy(xpar[half, :, h], xdup[half, :]).then_inc(s_xp, 1)
                v.wait_ge(s_z1, 36 * b + 2)
                for hp in range(4):
                    nc.vector.tensor_scalar(nk[:, T * hp:T * hp + T], xdup[:], nwk[:, hp:hp + 1], None, ALU.mult).then_inc(s_nk, 1)
                empty_fills("v", got)

                def produce(it, first):
                    for k, prev in tiles(b, it, first):
                        n = 36 * b + 3 * it + k
                        v.wait_ge(s_nks, n + 1)
                        for g in range(GROUPS):
                            if not (first and k == 0 and g < 4):
                                v.wait_ge(s_use, n * GROUPS + g - 3)
                            for j in range(4):
                                if by_vector[g][j]:
                                    u = 4 * g + j
                                    i = nc.vector.tensor_scalar(unit[:, u % RING, :], q[:, bass.ds(it // 3, 1), :].rearrange("p a t -> p (a t)"),
                                                                nks[:, k, 16 * j + g:16 * j + g + 1], 0.0, ALU.add, ALU.max)
                            i.then_inc(s_uv, 1)
                            if prev:
                                if g == 6:
                                    normalise(*prev)
                                if g == 10:
                                    last_chunk(*prev)

                def normalise(it, k):
                    n = 36 * b + 3 * it + k
                    v.wait_ge(s_e, n + 1)
                    nc.vector.tensor_scalar(z1[:, k:k + 1], z[:, k:k + 1], 1.0, None, ALU.add).then_inc(s_z1, 1)
                    v.wait_ge(s_z1, n + 3)
                    nc.vector.reciprocal(rz[:, k:k + 1], z1[:, k:k + 1]).then_inc(s_rz, 1)
                    v.wait_ge(s_rz, n + 1)
                    nc.vector.tensor_scalar(e[:, k, :], e[:, k, :], rz[:, k:k + 1], None, ALU.mult).then_inc(s_p, 1)

                def last_chunk(it, k):
                    n = 36 * b + 3 * it + k
                    v.wait_ge(s_t, n + 1)
                    nc.vector.tensor_copy(at[0:64, k, 4, :], score[0:64, 2 * k, 288:416]).then_inc(s_atv, 1)

                def finish(it, k):
                    normalise(it, k)
                    last_chunk(it, k)

                trips(v, b, produce, finish)
                v.wait_ge(s_kc, 36 * b + 36)
                nc.vector.tensor_tensor(oks[:], okf[:, 0:9, :], okf[:, 9:18, :], ALU.add).then_inc(s_add, 1)
                v.wait_ge(s_add, 3 * b + 1)
                nc.vector.tensor_tensor(oks[:], oks[:], okf[:, 18:27, :], ALU.add).then_inc(s_add, 1)
                v.wait_ge(s_add, 3 * b + 2)
                nc.vector.tensor_tensor(oks[:], oks[:], okf[:, 27:36, :], ALU.add).then_inc(s_add, 1)
                v.wait_ge(s_od, 32 * b + 32)

        @block.scalar
        def _(act):
            act.wait_ge(s_init, 5)
            with act.Fori(0, B) as b:
                def got(n):
                    act.wait_ge(s_fill, 24 * b + n + 1)
                    return score[:, n % 6, :]

                empty_fills("a", got)
                act.wait_ge(s_fv, (b + 1) * fills.per["v"])

                def produce(it, first):
                    for k, prev in tiles(b, it, first):
                        n = 36 * b + 3 * it + k
                        wait_apart(act, (s_w, 16 * 9), s_nks, n + 1)
                        for g in range(GROUPS):
                            if not (first and k == 0 and g < 4):
                                wait_apart(act, (s_w, 16 * 9), s_use, n * GROUPS + g - 3)
                            for j in range(4):
                                if not by_vector[g][j]:
                                    u = 4 * g + j
                                    i = nc.scalar.activation(unit[:, u % RING, :], q[:, bass.ds(it // 3, 1), :].rearrange("p a t -> p (a t)"), ACT.Relu,
                                                             bias=nks[:, k, 16 * j + g:16 * j + g + 1], scale=1.0)
                            i.then_inc(s_ua, 1)
                            if prev:
                                if g == 4:
                                    exp(*prev)
                                if g == 10:
                                    chunks(*prev)
                                if g == 14:
                                    key_out(*prev)

                def exp(it, k):
                    n = 36 * b + 3 * it + k
                    wait_apart(act, (s_w, 16 * 9), s_use, (n + 1) * GROUPS)
                    nc.scalar.activation(e[:, k, :].rearrange("p (a t) -> p a t", a=2), score[:, 2 * k:2 * k + 2, 0:288], ACT.Exp,
                                         bias=vb[:, bass.ds(3 * it + k, 1), S:S + 1].rearrange("p a n -> p (a n)"), scale=-SCALE,
                                         accum_out=z[:, k:k + 1]).then_inc(s_e, 1)

                def chunks(it, k):
                    n = 36 * b + 3 * it + k
                    act.wait_ge(s_t, n + 1)
                    nc.scalar.copy(at[:, k, 0:4, :].rearrange("p c r -> p (c r)"), turn[:]).then_inc(s_ata, 1)

                def key_out(it, k):
                    n = 36 * b + 3 * it + k
                    wait_apart(act, (s_w, 16 * 9), s_k, n + 1)
                    nc.scalar.copy(okf[:, bass.ds(3 * it + k, 1), :].rearrange("p a n -> p (a n)"), score[0:64, 2 * k + 1, 288:352]).then_inc(s_kc, 1)

                def finish(it, k):
                    exp(it, k)
                    chunks(it, k)
                    key_out(it, k)

                trips(act, b, produce, finish)
                nc.scalar.copy(o_query[:, bass.ds(5 * b, 4), :].rearrange("p c f -> p (c f)"), acc[:, 0:256]).then_inc(s_acc, 1)
                nc.scalar.copy(o_query[0:64, bass.ds(5 * b + 4, 1), :].rearrange("p c f -> p (c f)"), acc[0:64, 256:320]).then_inc(s_acc, 1)

        @block.tensor
        def _(pe):
            mm = nc.tensor.matmul
            pe.wait_ge(s_w, 16 * 9)
            pe.wait_ge(s_z1, 2)
            with pe.Fori(0, B) as b:
                def fill(n):
                    if n >= 6:
                        emptied(pe, b, n - 6)
                    return score[:, n % 6, :]

                pe.wait_ge(s_xs, b + 1)
                for n in range(2):
                    mm(fill(n)[:, 0:288], dup[:], xs[0:64, 288 * n:288 * n + 288], start=True, stop=True).then_inc(s_fill, 1)
                for n in range(2, 10):
                    hp, half = divmod(n - 2, 2)
                    mm(fill(n)[:, 0:288], wq[:, 128 * hp:128 * hp + 128], xs[:, 288 * half:288 * half + 288], start=True, stop=True).then_inc(s_fill, 1)
                for n in range(10, 15):
                    c = n - 10
                    rows = 128 if c < 4 else 64
                    mm(fill(n)[0:rows, :], xs[:, 128 * c:128 * c + rows], wvf[:], start=True, stop=True).then_inc(s_fill, 1)
                pe.wait_ge(s_xp, 2 * b + 2)
                for n in range(15, 24):
                    t0 = 64 * (n - 15)
                    out = fill(n)[:, 0:260]
                    mm(out, xpar[:, t0:t0 + 64, :].rearrange("p t h -> p (t h)"), wvb[:].rearrange("p a n -> p (a n)"), start=True, stop=False)
                    mm(out, par[:], bvb[:], start=False, stop=True).then_inc(s_fill, 1)
                for n in range(18, 24):
                    emptied(pe, b, n)

                def consume(it, first):
                    for k, prev in tiles(b, it, first):
                        n = 36 * b + 3 * it + k
                        if not first:
                            pe.wait_ge(s_kc, n - 2)
                        for half in range(2):
                            mm(score[:, 2 * k + half, 0:288], neg[:], q[:, bass.ds(it // 3, 1), 288 * half:288 * half + 288].rearrange("p a t -> p (a t)"),
                               start=True, stop=False, skip_group_check=True)
                        for g in range(GROUPS):
                            pe.wait_ge(s_uv, n * GROUPS + g + 1)
                            pe.wait_ge(s_ua, n * GROUPS + g + 1)
                            for j in range(4):
                                u = 4 * g + j
                                for half in range(2):
                                    i = mm(score[32 * j:32 * j + 32, 2 * k + half, 0:288], sel[:, 30 - 2 * g:62 - 2 * g],
                                           unit[:, u % RING, 288 * half:288 * half + 288], start=False, stop=(g == GROUPS - 1),
                                           tile_position=(0, 32 * j), skip_group_check=True)
                            i.then_inc(s_use, 1)
                            if prev:
                                if g == 7:
                                    value_sums(*prev, first and k == 1)
                                if g == 12:
                                    key_sums(*prev)

                def value_sums(it, k, fresh):
                    n = 36 * b + 3 * it + k
                    wait_apart(pe, (s_w, 16 * 9), s_p, n + 1)
                    for c in range(5):
                        rows = 128 if c < 4 else 64
                        mm(acc[0:rows, 64 * c:64 * c + 64], e[:, k, 128 * c:128 * c + rows],
                           vb[:, bass.ds(3 * it + k, 1), 0:S].rearrange("p a n -> p (a n)"), start=(fresh and c == 0), stop=False, skip_group_check=True)
                    for c in range(5):
                        rows = 128 if c < 4 else 64
                        out = turn[:, 128 * c:128 * c + 128] if c < 4 else score[0:64, 2 * k, 288:416]
                        i = nc.tensor.transpose(out, e[:, k, 128 * c:128 * c + rows], ident[:])
                    i.then_inc(s_t, 1)

                def key_sums(it, k):
                    n = 36 * b + 3 * it + k
                    wait_apart(pe, (s_w, 16 * 9), s_ata, n + 1)
                    wait_apart(pe, (s_w, 16 * 9), s_atv, n + 1)
                    for c in range(5):
                        for h in range(2):
                            i = mm(score[0:64, 2 * k + 1, 288:352], at[:, k, c, h:128:2],
                                   vf[:, c, bass.ds((it // 3) * 128 + 64 * h, 64)], start=(c == 0 and h == 0), stop=(c == 4 and h == 1), skip_group_check=True)
                    i.then_inc(s_k, 1)

                def finish(it, k):
                    value_sums(it, k, False)
                    key_sums(it, k)

                trips(pe, b, consume, finish)
                pe.wait_ge(s_acc, 2 * b + 2)
                pe.wait_ge(s_kc, 36 * b + 36)


def fanin_stage(nc, d, res, xn, o_query, o_key, ident):
    PARTS = 4
    W = ROWS // PARTS
    with ExitStack() as ctx:
        def sb(n, shape, dt=F32):
            return ctx.enter_context(nc.sbuf_tensor("fan_" + n, shape, dt))

        def sem(n):
            return ctx.enter_context(nc.semaphore("fan_" + n))

        w = sb("w", [65, S]); ex = sb("ex", [128, ROWS, S]); den = sb("den", [128, ROWS, S]); yt = sb("yt", [65, B, T])
        turned = ctx.enter_context(nc.psum_tensor("fan_turned", [128, 2, 1024], F32))
        out = ctx.enter_context(nc.psum_tensor("fan_out", [128, 2, 512], F32))
        s_w = sem("w"); s_one = sem("one"); s_o = sem("o"); s_e = sem("e"); s_d = sem("d"); s_r = sem("r"); s_y = sem("y")
        s_t = sem("t"); s_yt = sem("yt"); s_out = sem("out"); s_x = sem("x"); s_res = sem("res")
        block = ctx.enter_context(nc.Block())

        @block.sync
        def _(sp):
            sp.dma_start(w[:], d["l1_fan"]).then_inc(s_w, 16)

        @block.gpsimd
        def _(pool):
            nc.gpsimd.memset(yt[S:S + 1, :, :], 1.0).then_inc(s_one, 1)

        @block.vector
        def _(v):
            for p in range(PARTS):
                r = slice(W * p, W * p + W)
                nc.vector.tensor_tensor(o_query[:, r, :], o_query[:, r, :], o_key[:, r, :], ALU.add).then_inc(s_o, 1)
            for p in range(PARTS):
                r = slice(W * p, W * p + W)
                v.wait_ge(s_e, p + 1)
                nc.vector.tensor_scalar(den[:, r, :], ex[:, r, :], 1.0, None, ALU.add).then_inc(s_d, 1)
                v.wait_ge(s_d, p + 1)
                nc.vector.reciprocal(ex[:, r, :], den[:, r, :]).then_inc(s_r, 1)
                v.wait_ge(s_r, p + 1)
                nc.vector.tensor_tensor(o_query[:, r, :], o_query[:, r, :], ex[:, r, :], ALU.mult).then_inc(s_y, 1)
                nc.vector.tensor_tensor(res[:, r, :], res[:, r, :], xn[:, r, 0:S], ALU.add).then_inc(s_x, 1)
            v.wait_ge(s_x, PARTS)
            for b in range(B):
                v.wait_ge(s_out, b + 1)
                nc.vector.tensor_tensor(res[:, 5 * b:5 * b + 4, :], res[:, 5 * b:5 * b + 4, :],
                                        out[:, b % 2, 0:256].rearrange("p (c f) -> p c f", c=4), ALU.add).then_inc(s_res, 1)
                nc.vector.tensor_tensor(res[0:64, 5 * b + 4, :], res[0:64, 5 * b + 4, :], out[0:64, b % 2, 256:320], ALU.add).then_inc(s_res, 1)

        @block.scalar
        def _(act):
            for p in range(PARTS):
                r = slice(W * p, W * p + W)
                act.wait_ge(s_o, p + 1)
                nc.scalar.activation(ex[:, r, :], o_query[:, r, :], ACT.Exp, scale=-1.702).then_inc(s_e, 1)
            for b in range(B):
                act.wait_ge(s_t, b + 1)
                nc.scalar.copy(yt[0:S, b, :], turned[0:S, b % 2, 0:T]).then_inc(s_yt, 1)

        @block.tensor
        def _(pe):
            pe.wait_ge(s_w, 16)
            pe.wait_ge(s_one, 1)
            for b in range(B + 1):
                if b < B:
                    pe.wait_ge(s_y, b // 2 + 1)
                    if b >= 2:
                        pe.wait_ge(s_yt, b - 1)
                    for c in range(5):
                        n = min(128, T - 128 * c)
                        i = nc.tensor.transpose(turned[0:S, b % 2, 128 * c:128 * c + n], o_query[0:n, 5 * b + c, :], ident[0:n, 0:n])
                    i.then_inc(s_t, 1)
                if b >= 1:
                    pe.wait_ge(s_yt, b)
                    if b >= 3:
                        pe.wait_ge(s_res, 2 * (b - 2))
                    for c in range(5):
                        n = min(128, T - 128 * c)
                        i = nc.tensor.matmul(out[0:n, (b - 1) % 2, 64 * c:64 * c + 64], yt[:, b - 1, 128 * c:128 * c + n], w[:], start=True, stop=True)
                    i.then_inc(s_out, 1)


def store_tokens(nc, out, res):
    with ExitStack() as ctx:
        s_out = ctx.enter_context(nc.semaphore("result_stored"))
        r4 = res[:].rearrange("p (b c) f -> p b c f", b=B)
        block = ctx.enter_context(nc.Block())

        @block.sync
        def _(sp):
            for c in range(4):
                sp.dma_start(out[:, 128 * c:128 * c + 128, :].rearrange("b t f -> t b f"), r4[:, :, c, :]).then_inc(s_out, 16)
            sp.dma_start(out[:, 512:576, :].rearrange("b t f -> t b f"), r4[0:64, :, 4, :]).then_inc(s_out, 16)
            sp.wait_ge(s_out, 16 * 5)


def slice_layout(i):
    wx, bx = np.asarray(i["L0_ffn_W_x"]), np.asarray(i["L0_ffn_b_x"])
    wx1 = np.concatenate([wx, bx[None]])
    return {
        "s_wx_t": wx1.reshape(65, 8, S).transpose(2, 1, 0).reshape(S, 8 * 65),
        "s_slice": i["L0_ffn_W_slice"],
        "s_bslice": np.broadcast_to(np.asarray(i["L0_ffn_b_slice"]), (1, 8, S)).reshape(1, 512),
        "s_temp": np.broadcast_to(np.asarray(i["L0_ffn_temperature"]).reshape(1, 8), (65, 8)),
        "s_wfx": np.concatenate([np.asarray(i["L0_ffn_W_fx"]), np.asarray(i["L0_ffn_b_fx"])[None]]),
        "s_wq": i["L0_ffn_W_q"], "s_wk": i["L0_ffn_W_k"],
        "s_wv_t": np.asarray(i["L0_ffn_W_v"]).T,
        "s_wout": np.asarray(i["L0_ffn_W_out"]).reshape(8, S, S).transpose(1, 0, 2).reshape(S, 512),
        "s_bout": np.broadcast_to(np.asarray(i["L0_ffn_b_out"]), (128, S)),
    }


def slice_stage(nc, d, res, xn, xt, ident):
    NAMES = ["logit"] * 5 + ["turn_w"] * 5 + ["pool", "turn_p", "token", "q", "k", "vo", "score", "turn_a", "ow", "out"]
    OWNERS = ["v"] * 5 + ["a"] * 5 + ["v", "a", "v", "a", "v", "a", "v", "a", "v", "v"]
    ring = BankRing(OWNERS, 5)
    FIRST = {n: NAMES.index(n) for n in NAMES}
    NF = len(NAMES)
    with ExitStack() as ctx:
        def sb(n, shape, dt=F32):
            return ctx.enter_context(nc.sbuf_tensor("sl_" + n, shape, dt))

        def sem(n):
            return ctx.enter_context(nc.semaphore("sl_" + n))

        wx_t = sb("wx_t", [S, 8 * 65]); wslice = sb("wslice", [S, S]); bslice = sb("bslice", [65, 512]); temp = sb("temp", [65, 8])
        wfx = sb("wfx", [65, 512]); wq = sb("wq", [S, S]); wk = sb("wk", [S, S]); wv_t = sb("wv_t", [S, S]); wout = sb("wout", [S, 512])
        bout = sb("bout", [128, S]); rtemp = sb("rtemp", [65, 8]); wxs = sb("wxs", [65, 512]); wvo = sb("wvo", [S, 512])
        xs = sb("xs", [65, T]); mx = sb("mx", [128, 5, 8]); w = sb("w", [128, 5, 512]); sm = sb("sm", [128, 5, 8]); rs = sb("rs", [128, 5, 8])
        wt = sb("wt", [128, 4, T])
        nrm = sb("nrm", [128, 4]); rn = sb("rn", [128, 4]); pooled = sb("pooled", [128, 4, 65]); pt = sb("pt", [65, 512])
        tok = sb("tok", [S, 512]); qt = sb("qt", [S, 512]); kt = sb("kt", [S, 512]); vo = sb("vo", [S, 512])
        amx = sb("amx", [S, 8]); att = sb("att", [S, 512]); asm = sb("asm", [S, 8]); ars = sb("ars", [S, 8]); att_t = sb("att_t", [S, 512])
        ow = sb("ow", [128, 256])
        bank = ctx.enter_context(nc.psum_tensor("sl_bank", [128, 5, 512], F32))

        s_w = sem("weights"); s_pre = sem("pre_pe"); s_pv = sem("pre_v"); s_xs = sem("xs"); s_full = sem("full")
        s_ev = sem("emptied_v"); s_ea = sem("emptied_a"); s_mx = sem("max"); s_exp = sem("exp"); s_sum = sem("sum"); s_rs = sem("rsum")
        s_prob = sem("slice_weights"); s_nrm = sem("norm"); s_amx = sem("att_max"); s_cen = sem("att_centred"); s_aexp = sem("att_exp")
        s_asum = sem("att_sum"); s_att = sem("att"); s_res = sem("res")
        emptied_sem = {"v": s_ev, "a": s_ea}

        NW = 16 * (9 + 1)

        def emptied(eng, b, *fills):
            for who, count in ring.latest(fills):
                wait_apart(eng, (s_w, NW), emptied_sem[who], b * ring.per[who] + count)

        block = ctx.enter_context(nc.Block())
        loads = [(wx_t, "s_wx_t"), (wslice, "s_slice"), (temp, "s_temp"), (wfx, "s_wfx"), (wq, "s_wq"), (wk, "s_wk"), (wv_t, "s_wv_t"),
                 (wout, "s_wout"), (bout, "s_bout")]

        @block.sync
        def _(sp):
            for t, name in loads:
                sp.dma_start(t[:], d[name]).then_inc(s_w, 16)
            sp.dma_start(bslice[S:S + 1, :], d["s_bslice"]).then_inc(s_w, 16)

        @block.vector
        def _(v):
            v.wait_ge(s_w, NW)
            nc.vector.tensor_scalar(temp[:], temp[:], 0.1, 5.0, ALU.max, ALU.min).then_inc(s_pv, 1)
            v.wait_ge(s_pv, 1)
            nc.vector.reciprocal(rtemp[:], temp[:]).then_inc(s_pv, 1)
            v.wait_ge(s_pre, 1)
            nc.vector.tensor_copy(wxs[:], bank[0:65, 0, :]).then_inc(s_pv, 1)
            v.wait_ge(s_pv, 3)
            nc.vector.tensor_tensor(wxs[S:S + 1, :], wxs[S:S + 1, :], bslice[S:S + 1, :], ALU.add).then_inc(s_pv, 1)
            v.wait_ge(s_pv, 4)
            w3 = wxs[:].rearrange("p (h g) -> p h g", h=8)
            nc.vector.tensor_tensor(w3, w3, rtemp[:, :, None].broadcast_to([65, 8, S]), ALU.mult).then_inc(s_pv, 1)
            v.wait_ge(s_pre, 2)
            nc.vector.tensor_copy(wvo[:], bank[0:S, 1, :]).then_inc(s_pv, 1)
            nc.vector.tensor_tensor(res[:], res[:], bout[:, None, :].broadcast_to([128, ROWS, S]), ALU.add).then_inc(s_pv, 1)
            v.wait_ge(s_pv, 7)
            with v.Fori(0, B) as b:
                nc.vector.tensor_copy(xs[:], xt[:, bass.ds(b, 1), :].rearrange("p a t -> p (a t)")).then_inc(s_xs, 1)

                def got(name, k=0):
                    n = FIRST[name] + k
                    v.wait_ge(s_full, NF * b + n + 1)
                    return bank[:, n % ring.size, :]

                def heads(ap):
                    return ap.rearrange("p (h g) -> p h g", h=8)

                for c in range(5):
                    rows = 128 if c < 4 else 64
                    src = heads(got("logit", c)[0:rows, :])
                    nc.vector.tensor_reduce(mx[0:rows, c, :], src, AX, ALU.max).then_inc(s_mx, 1)
                    v.wait_ge(s_mx, 5 * b + c + 1)
                    nc.vector.tensor_tensor(heads(w[0:rows, c, :]), src, mx[0:rows, c, :, None].broadcast_to([rows, 8, S]), ALU.subtract).then_inc(s_ev, 1)
                for c in range(5):
                    rows = 128 if c < 4 else 64
                    v.wait_ge(s_exp, 5 * b + c + 1)
                    nc.vector.tensor_reduce(sm[0:rows, c, :], heads(w[0:rows, c, :]), AX, ALU.add).then_inc(s_sum, 1)
                    v.wait_ge(s_sum, 5 * b + c + 1)
                    nc.vector.reciprocal(rs[0:rows, c, :], sm[0:rows, c, :]).then_inc(s_rs, 1)
                    v.wait_ge(s_rs, 5 * b + c + 1)
                    nc.vector.tensor_tensor(heads(w[0:rows, c, :]), heads(w[0:rows, c, :]), rs[0:rows, c, :, None].broadcast_to([rows, 8, S]),
                                            ALU.mult).then_inc(s_prob, 1)
                src = got("pool")[:, 0:260].rearrange("p (a n) -> p a n", a=4)
                nc.vector.tensor_scalar(nrm[:], src[:, :, S], 1e-5, None, ALU.add).then_inc(s_nrm, 1)
                v.wait_ge(s_nrm, 2 * b + 1)
                nc.vector.reciprocal(rn[:], nrm[:]).then_inc(s_nrm, 1)
                v.wait_ge(s_nrm, 2 * b + 2)
                nc.vector.tensor_tensor(pooled[:], src, rn[:, :, None].broadcast_to([128, 4, 65]), ALU.mult).then_inc(s_ev, 1)
                nc.vector.tensor_copy(tok[:], got("token")[0:S, :]).then_inc(s_ev, 1)
                nc.vector.tensor_copy(kt[:], got("k")[0:S, :]).then_inc(s_ev, 1)
                src = heads(got("score")[0:S, :])
                nc.vector.tensor_reduce(amx[:], src, AX, ALU.max).then_inc(s_amx, 1)
                v.wait_ge(s_amx, b + 1)
                nc.vector.tensor_tensor(heads(att[:]), src, amx[:, :, None].broadcast_to([S, 8, S]), ALU.subtract).then_inc(s_ev, 1)
                v.wait_ge(s_aexp, b + 1)
                nc.vector.tensor_reduce(asm[:], heads(att[:]), AX, ALU.add).then_inc(s_asum, 1)
                v.wait_ge(s_asum, 2 * b + 1)
                nc.vector.reciprocal(ars[:], asm[:]).then_inc(s_asum, 1)
                v.wait_ge(s_asum, 2 * b + 2)
                nc.vector.tensor_tensor(heads(att[:]), heads(att[:]), ars[:, :, None].broadcast_to([S, 8, S]), ALU.mult).then_inc(s_att, 1)
                nc.vector.tensor_copy(ow[:], got("ow")[:, 0:256]).then_inc(s_ev, 1)
                src = got("out")
                r = res[:, bass.ds(5 * b, 4), :]
                nc.vector.tensor_tensor(r, r, src[:, 0:256].rearrange("p (c f) -> p c f", c=4), ALU.add).then_inc(s_res, 1)
                r = res[0:64, bass.ds(5 * b + 4, 1), :].rearrange("p c f -> p (c f)")
                nc.vector.tensor_tensor(r, r, src[0:64, 256:320], ALU.add).then_inc(s_ev, 1)

        @block.scalar
        def _(act):
            with act.Fori(0, B) as b:
                def got(name, k=0):
                    n = FIRST[name] + k
                    act.wait_ge(s_full, NF * b + n + 1)
                    return bank[:, n % ring.size, :]

                for c in range(5):
                    rows = 128 if c < 4 else 64
                    act.wait_ge(s_ev, ring.per["v"] * b + c + 1)
                    nc.scalar.activation(w[0:rows, c, :], w[0:rows, c, :], ACT.Exp).then_inc(s_exp, 1)
                for c in range(5):
                    rows = 128 if c < 4 else 64
                    nc.scalar.copy(wt[:, :, 128 * c:128 * c + rows], got("turn_w", c).rearrange("p (a r) -> p a r", a=4)[:, :, 0:rows]).then_inc(s_ea, 1)
                nc.scalar.copy(pt[:], got("turn_p")[0:65, :]).then_inc(s_ea, 1)
                nc.scalar.copy(qt[:], got("q")[0:S, :]).then_inc(s_ea, 1)
                nc.scalar.copy(vo[:], got("vo")[0:S, :]).then_inc(s_ea, 1)
                who, count = ring.emptied(FIRST["score"])
                act.wait_ge(s_ev, ring.per["v"] * b + count)
                nc.scalar.activation(att[:], att[:], ACT.Exp, scale=1.0 / 8.0).then_inc(s_aexp, 1)
                nc.scalar.copy(att_t[:], got("turn_a")[0:S, :]).then_inc(s_ea, 1)

        @block.tensor
        def _(pe):
            mm, turn = nc.tensor.matmul, nc.tensor.transpose
            pe.wait_ge(s_w, NW)
            for h in range(8):
                i = mm(bank[0:65, 0, 64 * h:64 * h + 64], wx_t[:, 65 * h:65 * h + 65], wslice[:], start=True, stop=True)
            i.then_inc(s_pre, 1)
            mm(bank[0:S, 1, :], wv_t[:], wout[:], start=True, stop=True).then_inc(s_pre, 1)
            pe.wait_ge(s_pv, 7)
            with pe.Fori(0, B) as b:
                def fill(name, k=0, reads=()):
                    n = FIRST[name] + k
                    emptied(pe, b, *[FIRST[r] for r in reads], *([n - ring.size] if n >= ring.size else []))
                    return bank[:, n % ring.size, :]

                wait_apart(pe, (s_w, NW), s_xs, b + 1)
                for c in range(5):
                    rows = 128 if c < 4 else 64
                    mm(fill("logit", c)[0:rows, :], xs[:, 128 * c:128 * c + rows], wxs[:], start=True, stop=True).then_inc(s_full, 1)
                for c in range(5):
                    rows = 128 if c < 4 else 64
                    wait_apart(pe, (s_w, NW), s_prob, 5 * b + c + 1)
                    out = fill("turn_w", c)
                    for hp in range(4):
                        i = turn(out[:, 128 * hp:128 * hp + rows], w[0:rows, c, 128 * hp:128 * hp + 128], ident[0:rows, 0:rows])
                    i.then_inc(s_full, 1)
                out = fill("pool")
                for hp in range(4):
                    for c in range(5):
                        rows = 128 if c < 4 else 64
                        i = mm(out[:, 65 * hp:65 * hp + 65], w[0:rows, c, 128 * hp:128 * hp + 128],
                               xn[0:rows, bass.ds(5 * b + c, 1), :].rearrange("p a n -> p (a n)"), start=(c == 0), stop=(c == 4))
                i.then_inc(s_full, 1)
                out = fill("turn_p", reads=["pool"])
                for hp in range(4):
                    i = turn(out[0:65, 128 * hp:128 * hp + 128], pooled[:, hp, :], ident[:])
                i.then_inc(s_full, 1)
                out = fill("token", reads=["turn_p"])
                for h in range(8):
                    i = mm(out[0:S, 64 * h:64 * h + 64], wfx[:, 64 * h:64 * h + 64], pt[:, 64 * h:64 * h + 64], start=True, stop=True)
                i.then_inc(s_full, 1)
                mm(fill("q", reads=["token"])[0:S, :], wq[:], tok[:], start=True, stop=True).then_inc(s_full, 1)
                mm(fill("k")[0:S, :], wk[:], tok[:], start=True, stop=True).then_inc(s_full, 1)
                out = fill("vo")
                for h in range(8):
                    i = mm(out[0:S, 64 * h:64 * h + 64], tok[:, 64 * h:64 * h + 64], wvo[:, 64 * h:64 * h + 64], start=True, stop=True)
                i.then_inc(s_full, 1)
                out = fill("score", reads=["q", "k"])
                for h in range(8):
                    i = mm(out[0:S, 64 * h:64 * h + 64], qt[:, 64 * h:64 * h + 64], kt[:, 64 * h:64 * h + 64], start=True, stop=True)
                i.then_inc(s_full, 1)
                wait_apart(pe, (s_w, NW), s_att, b + 1)
                out = fill("turn_a")
                for h in range(8):
                    i = turn(out[0:S, 64 * h:64 * h + 64], att[:, 64 * h:64 * h + 64], ident[0:S, 0:S])
                i.then_inc(s_full, 1)
                out = fill("ow", reads=["turn_a", "vo"])
                for h in range(8):
                    p0 = 64 * (h % 2)
                    i = mm(out[p0:p0 + 64, 64 * (h // 2):64 * (h // 2) + 64], att_t[:, 64 * h:64 * h + 64], vo[:, 64 * h:64 * h + 64],
                           start=True, stop=True, tile_position=(0, p0))
                i.then_inc(s_full, 1)
                out = fill("out", reads=["ow"])
                for c in range(5):
                    rows = 128 if c < 4 else 64
                    for hp in range(4):
                        i = mm(out[0:rows, 64 * c:64 * c + 64], wt[:, hp, 128 * c:128 * c + rows], ow[:, 64 * hp:64 * hp + 64],
                               start=(hp == 0), stop=(hp == 3))
                i.then_inc(s_full, 1)


def mqa_layout(i):
    wq, wo = np.asarray(i["L1_attn_Wq"]), np.asarray(i["L1_attn_Wo"])
    wv = np.asarray(i["L1_attn_Wv"]).T
    return {"m_wq": wq.T, "m_wk": np.asarray(i["L1_attn_Wk"]).T, "m_wv": np.concatenate([wv, wv], 1),
            "m_wo": wo.T.reshape(4, 128, S).transpose(1, 0, 2).reshape(128, 256)}


def mqa_stage(nc, d, xt, ctx_dram, max_dram, ident):
    SCALE = 1.0 / np.sqrt(8.0)
    OWNERS = ["v", "v"] + ["a", "v", "a", "v"] + ["v"] * 40 + ["a"] + ["a"] * 40
    K, V, Q, SCORE, TURN, PROB = 0, 1, 2, 6, 46, 47
    ring = BankRing(OWNERS, 3)
    NF = len(OWNERS)
    with ExitStack() as ctx:
        def sb(n, shape, dt=F32):
            return ctx.enter_context(nc.sbuf_tensor("mq_" + n, shape, dt))

        def sem(n):
            return ctx.enter_context(nc.semaphore("mq_" + n))

        wq = sb("wq", [S, 512]); wk = sb("wk", [S, S]); wv = sb("wv", [S, 128])
        xs = sb("xs", [S, T]); k1 = sb("k1", [65, 9, S]); q1 = sb("q1", [65, 8, T]); vals = sb("vals", [128, 5, 65])
        mx = sb("mx", [128, 8, 5]); nmx = sb("nmx", [128, 8, 5]); mrow = sb("mrow", [40, 128])
        p = sb("p", [128, 2, 5, T]); rz = sb("rz", [128, 2, 5]); c_out = sb("c_out", [128, 5, 512])
        wide = ctx.enter_context(nc.psum_tensor("mq_wide", [128, 3, 2, 512], F32))
        cx = ctx.enter_context(nc.psum_tensor("mq_cx", [128, 2, 512], F32))
        s_w = sem("weights"); s_init = sem("init"); s_xs = sem("xs"); s_full = sem("full"); s_ev = sem("emptied_v"); s_ea = sem("emptied_a")
        s_nmx = sem("minus_max"); s_mo = sem("max_out"); s_mi = sem("max_in"); s_cx = sem("context"); s_rz = sem("rz"); s_cn = sem("context_normed")
        s_store = sem("context_stored"); s_vp = sem("values_part"); s_qp = sem("q_part_a"); s_qv = sem("q_part_v")
        emptied_sem = {"v": s_ev, "a": s_ea}

        def emptied(eng, b, *fills):
            for who, count in ring.latest(fills):
                wait_apart(eng, (s_w, 48), emptied_sem[who], b * ring.per[who] + count)

        block = ctx.enter_context(nc.Block())

        @block.sync
        def _(sp):
            for t, name in ((wq, "m_wq"), (wk, "m_wk"), (wv, "m_wv")):
                sp.dma_start(t[:], d[name]).then_inc(s_w, 16)
            with sp.Fori(0, B) as b:
                emptied(sp, b, TURN)
                sp.dma_start(max_dram, mrow[:]).then_inc(s_mo, 16)
                sp.wait_ge(s_mo, 16 * (b + 1))
                sp.dma_start(q1[S:S + 1, :, :], max_dram.rearrange("(a h c) n -> a h (c n)", a=1, c=5)[:, :, 0:T]).then_inc(s_mi, 16)
                sp.wait_ge(s_cn, 8 * b + 8)
                sp.dma_start(ctx_dram[bass.ds(b, 1), 0:512, :].rearrange("a (c p) n -> p (a c) n", p=128), c_out[:, 0:4, :]).then_inc(s_store, 16)
                sp.dma_start(ctx_dram[bass.ds(b, 1), 512:576, :].rearrange("a p n -> p (a n)"), c_out[0:64, 4, :]).then_inc(s_store, 16)
            sp.wait_ge(s_store, 32 * B)

        @block.gpsimd
        def _(pool):
            nc.gpsimd.memset(k1[S:S + 1, :, :], 1.0).then_inc(s_init, 1)
            pool.wait_ge(s_init, 1)
            nc.gpsimd.memset(vals[:, :, S:S + 1], 1.0).then_inc(s_init, 1)
            pool.wait_ge(s_init, 2)
            nc.gpsimd.memset(mx[:], 0.0).then_inc(s_init, 1)

        @block.vector
        def _(v):
            v.wait_ge(s_init, 3)
            with v.Fori(0, B) as b:
                nc.vector.tensor_copy(xs[:], xt[0:S, bass.ds(b, 1), :].rearrange("p a t -> p (a t)")).then_inc(s_xs, 1)

                def got(n):
                    v.wait_ge(s_full, NF * b + n + 1)
                    return wide[:, n % 3, :, :]

                nc.vector.tensor_copy(k1[0:S, :, :].rearrange("p j (a o) -> p a j o", a=2)[:, 0], got(K)[0:S, 0, 0:288].rearrange("p (o j) -> p j o", j=9)).then_inc(s_vp, 1)
                nc.vector.tensor_copy(k1[0:S, :, :].rearrange("p j (a o) -> p a j o", a=2)[:, 1], got(K)[0:S, 1, 0:288].rearrange("p (o j) -> p j o", j=9)).then_inc(s_ev, 1)
                src = got(V)
                a = src[:, 0, 0:320].rearrange("p (j f) -> p j f", j=5)
                c = src[:, 1, 0:256].rearrange("p (j f) -> p j f", j=4)
                nc.vector.tensor_copy(vals[0:64, 0:3, 0:S], a[0:64, 0:5:2, :]).then_inc(s_vp, 1)
                nc.vector.tensor_copy(vals[64:128, 0:2, 0:S], a[64:128, 1:5:2, :]).then_inc(s_vp, 1)
                nc.vector.tensor_copy(vals[0:64, 3:5, 0:S], c[0:64, 1:4:2, :]).then_inc(s_vp, 1)
                nc.vector.tensor_copy(vals[64:128, 2:4, 0:S], c[64:128, 0:4:2, :]).then_inc(s_ev, 1)
                for hp in (1, 3):
                    src = got(Q + hp)
                    q3 = q1[0:S, 2 * hp:2 * hp + 2, :].rearrange("p h (a t) -> p h a t", a=2)
                    nc.vector.tensor_copy(q3[:, 0], src[0:64, :, 0:288]).then_inc(s_qv, 1)
                    nc.vector.tensor_copy(q3[:, 1], src[64:128, :, 0:288]).then_inc(s_ev, 1)
                for n in range(40):
                    h, c = divmod(n, 5)
                    rows = 128 if c < 4 else 64
                    nc.vector.tensor_reduce(mx[0:rows, h, c:c + 1], got(SCORE + n)[0:rows, :, 0:288], mybir.AxisListType.XY, ALU.max).then_inc(s_ev, 1)
                v.wait_ge(s_ev, ring.per["v"] * (b + 1))
                nc.vector.tensor_scalar(nmx[:], mx[:], -1.0, None, ALU.mult).then_inc(s_nmx, 1)
                for h in range(8):
                    v.wait_ge(s_cx, 8 * b + h + 1)
                    src = cx[:, h % 2, 0:325].rearrange("p (c n) -> p c n", c=5)
                    nc.vector.reciprocal(rz[:, h % 2, 0:4], src[:, 0:4, S]).then_inc(s_rz, 1)
                    nc.vector.reciprocal(rz[0:64, h % 2, 4:5], src[0:64, 4, S:S + 1]).then_inc(s_rz, 1)
                    v.wait_ge(s_rz, 24 * b + 3 * h + 2)
                    nc.vector.tensor_tensor(c_out[:, 0:4, 64 * h:64 * h + 64], src[:, 0:4, 0:S], rz[:, h % 2, 0:4, None].broadcast_to([128, 4, S]), ALU.mult).then_inc(s_rz, 1)
                    nc.vector.tensor_scalar(c_out[0:64, 4, 64 * h:64 * h + 64], src[0:64, 4, 0:S], rz[0:64, h % 2, 4:5], None, ALU.mult).then_inc(s_cn, 1)
                v.wait_ge(s_store, 32 * b + 32)

        @block.scalar
        def _(act):
            with act.Fori(0, B) as b:
                def got(n):
                    act.wait_ge(s_full, NF * b + n + 1)
                    return wide[:, n % 3, :, :]

                for hp in (0, 2):
                    src = got(Q + hp)
                    q3 = q1[0:S, 2 * hp:2 * hp + 2, :].rearrange("p h (a t) -> p h a t", a=2)
                    nc.scalar.copy(q3[:, 0], src[0:64, :, 0:288]).then_inc(s_qp, 1)
                    nc.scalar.copy(q3[:, 1], src[64:128, :, 0:288]).then_inc(s_ea, 1)
                nc.scalar.copy(mrow[:], got(TURN)[0:40, 0, 0:128]).then_inc(s_ea, 1)
                for n in range(40):
                    h, j = divmod(n, 5)
                    rows = 128 if j < 4 else 64
                    nc.scalar.activation(p[0:rows, h % 2, j, :].rearrange("p (a t) -> p a t", a=2), got(PROB + n)[0:rows, :, 0:288], ACT.Exp,
                                         scale=float(SCALE)).then_inc(s_ea, 1)

        @block.tensor
        def _(pe):
            mm = nc.tensor.matmul
            pe.wait_ge(s_w, 48)
            pe.wait_ge(s_init, 3)
            with pe.Fori(0, B) as b:
                def fill(n, reads=()):
                    emptied(pe, b, *reads, *([n - 3] if n >= 3 else []))
                    return wide[:, n % 3, :, :]

                def halves(out, lhs, rhs):
                    for a in range(2):
                        i = mm(out[:, a, 0:288], lhs, rhs[:, 288 * a:288 * a + 288], start=True, stop=True)
                    i.then_inc(s_full, 1)

                wait_apart(pe, (s_w, 48), s_xs, b + 1)
                halves(fill(K)[0:S], wk[:], xs[:])
                out = fill(V)
                mm(out[:, 0, 0:320], wv[:], xs[:, 0:320], start=True, stop=True)
                mm(out[:, 1, 0:256], wv[:], xs[:, 320:576], start=True, stop=True).then_inc(s_full, 1)
                for hp in range(4):
                    halves(fill(Q + hp), wq[:, 128 * hp:128 * hp + 128], xs[:])
                keys = k1[:].rearrange("p j o -> p (j o)")
                for n in range(40):
                    h, c = divmod(n, 5)
                    reads = ([K] if n == 0 else []) + ([Q + h // 2] if c == 0 and h % 2 == 0 else [])
                    rows = 128 if c < 4 else 64
                    halves(fill(SCORE + n, reads)[0:rows], q1[0:S, h, 128 * c:128 * c + rows], keys[0:S, :])
                out = fill(TURN)
                wait_apart(pe, (s_w, 48), s_nmx, b + 1)
                nc.tensor.transpose(out[0:40, 0, 0:128], nmx[:].rearrange("p h c -> p (h c)"), ident[:]).then_inc(s_full, 1)
                wait_apart(pe, (s_w, 48), s_mi, 16 * (b + 1))

                def context(h):
                    emptied(pe, b, PROB + 5 * h + 4, V)
                    if h >= 2:
                        wait_apart(pe, (s_w, 48), s_cn, 8 * b + h - 1)
                    for c in range(5):
                        rows = 128 if c < 4 else 64
                        for j in range(5):
                            keys_n = 128 if j < 4 else 64
                            i = mm(cx[0:rows, h % 2, 65 * c:65 * c + 65], p[0:keys_n, h % 2, j, 128 * c:128 * c + rows], vals[0:keys_n, j, :],
                                   start=(j == 0), stop=(j == 4))
                    i.then_inc(s_cx, 1)

                for n in range(40):
                    h, j = divmod(n, 5)
                    rows = 128 if j < 4 else 64
                    halves(fill(PROB + n)[0:rows], keys[:, 128 * j:128 * j + rows], q1[:, h, :])
                    if j == 1 and h >= 1:
                        context(h - 1)
                context(7)


def mqa_out_stage(nc, d, ctx_dram, res):
    with ExitStack() as ctx:
        def sem(n):
            return ctx.enter_context(nc.semaphore("mo_" + n))

        wo = ctx.enter_context(nc.sbuf_tensor("mo_wo", [128, 256], F32))
        cr = ctx.enter_context(nc.sbuf_tensor("mo_cr", [128, 2, 4, T], F32))
        out = ctx.enter_context(nc.psum_tensor("mo_out", [128, 2, 512], F32))
        s_w = sem("weights"); s_c = [sem("context0"), sem("context1")]; s_out = sem("out"); s_res = sem("res")
        view = ctx_dram.rearrange("b s n -> b (s n)").rearrange("b (i p t) -> b p i t", p=128, t=T)
        block = ctx.enter_context(nc.Block())

        @block.sync
        def _(sp):
            sp.dma_start(wo[:], d["m_wo"]).then_inc(s_w, 16)
            for k in range(2):
                sp.dma_start(cr[:, k], view[k]).then_inc(s_c[k], 16)
            with sp.Fori(1, B // 2) as n:
                for k in range(2):
                    sp.wait_ge(s_out, 2 * n + k - 1)
                    sp.dma_start(cr[:, k], view[bass.ds(2 * n + k, 1)].rearrange("a p i t -> p (a i) t")).then_inc(s_c[k], 16)

        @block.vector
        def _(v):
            with v.Fori(0, B // 2) as n:
                for k in range(2):
                    v.wait_ge(s_out, 2 * n + k + 1)
                    r = res[:, bass.ds(10 * n + 5 * k, 4), :]
                    nc.vector.tensor_tensor(r, r, out[:, k, 0:256].rearrange("p (c f) -> p c f", c=4), ALU.add).then_inc(s_res, 1)
                    r = res[0:64, bass.ds(10 * n + 5 * k + 4, 1), :].rearrange("p c f -> p (c f)")
                    nc.vector.tensor_tensor(r, r, out[0:64, k, 256:320], ALU.add).then_inc(s_res, 1)

        @block.tensor
        def _(pe):
            pe.wait_ge(s_w, 16)

            def pair(n, first):
                for k in range(2):
                    pe.wait_ge(s_c[k], 16 * (n + 1))
                    if not first:
                        pe.wait_ge(s_res, 4 * n + 2 * k - 2)
                    for c in range(5):
                        rows = 128 if c < 4 else 64
                        for i4 in range(4):
                            i = nc.tensor.matmul(out[0:rows, k, 64 * c:64 * c + 64], cr[:, k, i4, 128 * c:128 * c + rows],
                                                 wo[:, 64 * i4:64 * i4 + 64], start=(i4 == 0), stop=(i4 == 3))
                    i.then_inc(s_out, 1)

            pair(0, True)
            with pe.Fori(1, B // 2) as n:
                pair(n, False)


def moe_layout(i):
    a = {"e_sw1": i["L1_ffn_sW1"], "e_sw2": i["L1_ffn_sW2"], "e_sw3": i["L1_ffn_sW3"]}
    a["e_sb1"] = np.asarray(i["L1_ffn_sb1"])[:, None]
    a["e_sb2"] = np.asarray(i["L1_ffn_sb2"])[:, None]
    a["e_sb3"] = np.broadcast_to(np.asarray(i["L1_ffn_sb3"]), (128, S))
    a["e_w1"] = np.asarray(i["L1_ffn_eW1"]).transpose(1, 0, 2).reshape(S, 512)
    a["e_b1"] = np.asarray(i["L1_ffn_eb1"]).T
    a["e_w2"] = np.asarray(i["L1_ffn_eW2"]).transpose(1, 0, 2).reshape(128, 256)
    a["e_b2"] = np.asarray(i["L1_ffn_eb2"]).T
    w3 = np.concatenate([np.asarray(i["L1_ffn_eW3"]), np.asarray(i["L1_ffn_eb3"])[:, None]], 1)
    a["e_w3"] = w3.transpose(1, 0, 2).reshape(65, 256)
    a["e_gate"] = np.concatenate([np.asarray(i["L1_ffn_gW"]), np.asarray(i["L1_ffn_gb"])[None]])
    return a


def moe_constants():
    return {"c_before": np.broadcast_to(np.tril(np.ones((4, 4)), -1).reshape(1, 16), (128, 16)).astype(np.float32)}


def moe_stage(nc, d, res, xt):
    OWNERS = ["a", "v"] + ["a", "v"] * 4 + ["v", "v", "v", "v", "v", "v"]
    S1, S2, GATE, OUT = 0, 1, 10, 11
    ring = BankRing(OWNERS, 4)
    NF = len(OWNERS)
    with ExitStack() as ctx:
        def sb(n, shape, dt=F32):
            return ctx.enter_context(nc.sbuf_tensor("me_" + n, shape, dt))

        def sem(n):
            return ctx.enter_context(nc.semaphore("me_" + n))

        sw1 = sb("sw1", [S, S]); sw2 = sb("sw2", [S, 128]); sw3 = sb("sw3", [128, S]); sb1 = sb("sb1", [S, 1]); sb2 = sb("sb2", [128, 1])
        sb3 = sb("sb3", [128, S]); w1 = sb("w1", [S, 512]); b1 = sb("b1", [128, 4]); w2 = sb("w2", [128, 256]); b2 = sb("b2", [S, 4])
        w3 = sb("w3", [65, 256]); gate = sb("gate", [65, 4]); before = sb("before", [128, 4, 4])
        xs = sb("xs", [65, T]); h1 = sb("h1", [S, T]); h2 = sb("h2", [128, T]); g1 = sb("g1", [128, 2, T]); g2 = sb("g2", [65, 4, T])
        gl = sb("gl", [128, 5, 4]); gm = sb("gm", [128, 5]); gc = sb("gc", [128, 5, 4]); ge = sb("ge", [128, 5, 4]); gs = sb("gs", [128, 5])
        gr = sb("gr", [128, 5]); gp = sb("gp", [128, 5, 4]); eq = sb("eq", [128, 5, 4, 4]); gt = sb("gt", [128, 5, 4, 4])
        rank = sb("rank", [128, 5, 4]); top = sb("top", [128, 5, 4]); tm = sb("tm", [128, 5]); tc = sb("tc", [128, 5, 4]); te = sb("te", [128, 5, 4])
        ts = sb("ts", [128, 5]); tr = sb("tr", [128, 5]); tw = sb("tw", [128, 5, 4])
        mixed = sb("mixed", [128, 2, 4, S]); sh = sb("sh", [128, 2, S]); msum = sb("msum", [128, 2, S])
        wide = ctx.enter_context(nc.psum_tensor("me_wide", [128, 4, 2, 512], F32))
        s_w = sem("weights"); s_one = sem("ones"); s_xs = sem("xs"); s_full = sem("full"); s_ev = sem("emptied_v"); s_ea = sem("emptied_a")
        s_g = sem("gates_v"); s_ga = sem("gates_a"); s_mix = sem("mix"); s_res = sem("res")
        emptied_sem = {"v": s_ev, "a": s_ea}

        NW = 16 * 13

        def emptied(eng, b, *fills):
            for who, count in ring.latest(fills):
                wait_apart(eng, (s_w, NW), emptied_sem[who], b * ring.per[who] + count)

        block = ctx.enter_context(nc.Block())
        loads = [(sw1, "e_sw1"), (sw2, "e_sw2"), (sw3, "e_sw3"), (sb1, "e_sb1"), (sb2, "e_sb2"), (sb3, "e_sb3"), (w1, "e_w1"), (b1, "e_b1"),
                 (w2, "e_w2"), (b2, "e_b2"), (w3, "e_w3"), (gate, "e_gate")]
        assert NW == 16 * (len(loads) + 1)

        @block.sync
        def _(sp):
            for t, name in loads:
                sp.dma_start(t[:], d[name]).then_inc(s_w, 16)
            sp.dma_start(before[:], d["c_before"].rearrange("p (i j) -> p i j", i=4)).then_inc(s_w, 16)

        @block.gpsimd
        def _(pool):
            nc.gpsimd.memset(g2[S:S + 1, :, :], 1.0).then_inc(s_one, 1)
            pool.wait_ge(s_one, 1)
            nc.gpsimd.memset(gl[:], 0.0).then_inc(s_one, 1)

        @block.vector
        def _(v):
            v.wait_ge(s_w, NW)
            v.wait_ge(s_one, 2)
            nc.vector.tensor_tensor(res[:], res[:], sb3[:, None, :].broadcast_to([128, ROWS, S]), ALU.add).then_inc(s_res, 1)
            v.wait_ge(s_res, 1)
            with v.Fori(0, B) as b:
                nc.vector.tensor_copy(xs[:], xt[:, bass.ds(b, 1), :].rearrange("p a t -> p (a t)")).then_inc(s_xs, 1)
                GSTEPS = 18
                step = [0]

                def done(i):
                    i.then_inc(s_g, 1)
                    step[0] += 1
                    v.wait_ge(s_g, GSTEPS * b + step[0])

                def got(n):
                    v.wait_ge(s_full, NF * b + n + 1)
                    return wide[:, n % 4, :, :]

                def gates():
                    src = got(GATE)
                    done(nc.vector.tensor_copy(gl[:, 0:4, :], src[:, 0, 0:16].rearrange("p (c e) -> p c e", c=4)))
                    nc.vector.tensor_copy(gl[0:64, 4, :], src[0:64, 0, 16:20]).then_inc(s_ev, 1)
                    emptied(v, b, GATE)
                    done(nc.vector.tensor_reduce(gm[:], gl[:], AX, ALU.max))
                    done(nc.vector.tensor_tensor(gc[:], gl[:], gm[:, :, None].broadcast_to([128, 5, 4]), ALU.subtract))
                    v.wait_ge(s_ga, 2 * b + 1)
                    done(nc.vector.tensor_reduce(gs[:], ge[:], AX, ALU.add))
                    done(nc.vector.reciprocal(gr[:], gs[:]))
                    done(nc.vector.tensor_tensor(gp[:], ge[:], gr[:, :, None].broadcast_to([128, 5, 4]), ALU.mult))
                    mine, other = gp[:, :, :, None].broadcast_to([128, 5, 4, 4]), gp[:, :, None, :].broadcast_to([128, 5, 4, 4])
                    done(nc.vector.tensor_tensor(gt[:], other, mine, ALU.is_gt))
                    done(nc.vector.tensor_tensor(eq[:], other, mine, ALU.is_equal))
                    done(nc.vector.tensor_tensor(eq[:], eq[:], before[:, None, :, :].broadcast_to([128, 5, 4, 4]), ALU.mult))
                    done(nc.vector.tensor_tensor(gt[:], gt[:], eq[:], ALU.add))
                    done(nc.vector.tensor_reduce(rank[:], gt[:], AX, ALU.add))
                    done(nc.vector.tensor_scalar(top[:], rank[:], 1.5, None, ALU.is_lt))
                    done(nc.vector.tensor_reduce(tm[:], gp[:], AX, ALU.max))
                    done(nc.vector.tensor_tensor(tc[:], gp[:], tm[:, :, None].broadcast_to([128, 5, 4]), ALU.subtract))
                    v.wait_ge(s_ga, 2 * b + 2)
                    done(nc.vector.tensor_tensor(te[:], te[:], top[:], ALU.mult))
                    done(nc.vector.tensor_reduce(ts[:], te[:], AX, ALU.add))
                    done(nc.vector.reciprocal(tr[:], ts[:]))
                    done(nc.vector.tensor_tensor(tw[:], te[:], tr[:, :, None].broadcast_to([128, 5, 4]), ALU.mult))
                    assert step[0] == GSTEPS

                def hidden(n, out, bias):
                    rows = out.shape[0]
                    nc.vector.tensor_scalar(out.rearrange("p (a t) -> p a t", a=2), got(n)[0:rows, :, 0:288], bias, 0.0, ALU.add, ALU.max).then_inc(s_ev, 1)

                hidden(S2, h2[:], sb2[:, 0:1])
                for x in range(4):
                    hidden(3 + 2 * x, g2[0:S, x, :], b2[:, x:x + 1])
                gates()
                for c in range(5):
                    rows = 128 if c < 4 else 64
                    src = got(OUT + c)
                    m = mixed[0:rows, c % 2]
                    nc.vector.tensor_tensor(m, src[0:rows, 1, 0:256].rearrange("p (e f) -> p e f", e=4), tw[0:rows, c, :, None].broadcast_to([rows, 4, S]), ALU.mult).then_inc(s_mix, 1)
                    v.wait_ge(s_mix, 10 * b + 2 * c + 1)
                    nc.vector.tensor_reduce(msum[0:rows, c % 2, :], m.rearrange("p e f -> p f e"), AX, ALU.add).then_inc(s_mix, 1)
                    r = res[0:rows, bass.ds(5 * b + c, 1), :].rearrange("p c f -> p (c f)")
                    nc.vector.tensor_tensor(r, r, src[0:rows, 0, 0:S], ALU.add).then_inc(s_ev, 1)
                    emptied(v, b, OUT + c)
                    v.wait_ge(s_mix, 10 * b + 2 * c + 2)
                    nc.vector.tensor_tensor(r, r, msum[0:rows, c % 2, :], ALU.add).then_inc(s_res, 1)

        @block.scalar
        def _(act):
            act.wait_ge(s_w, NW)
            with act.Fori(0, B) as b:
                def hidden(n, out, bias):
                    act.wait_ge(s_full, NF * b + n + 1)
                    rows = out.shape[0]
                    nc.scalar.activation(out.rearrange("p (a t) -> p a t", a=2), wide[0:rows, n % 4, :, 0:288], ACT.Relu, bias=bias, scale=1.0).then_inc(s_ea, 1)

                hidden(S1, h1[:], sb1[:, 0:1])
                for x in range(4):
                    if x >= 2:
                        emptied(act, b, 3 + 2 * (x - 2))
                    hidden(2 + 2 * x, g1[:, x % 2, :], b1[:, x:x + 1])
                act.wait_ge(s_g, 18 * b + 3)
                nc.scalar.activation(ge[:], gc[:], ACT.Exp).then_inc(s_ga, 1)
                act.wait_ge(s_g, 18 * b + 14)
                nc.scalar.activation(te[:], tc[:], ACT.Exp).then_inc(s_ga, 1)

        @block.tensor
        def _(pe):
            mm = nc.tensor.matmul
            pe.wait_ge(s_w, NW)
            pe.wait_ge(s_one, 2)
            with pe.Fori(0, B) as b:
                def fill(n, reads=()):
                    emptied(pe, b, *reads, *([n - 4] if n >= 4 else []))
                    return wide[:, n % 4, :, :]

                def layer(n, rows, lhs, rhs, reads=()):
                    out = fill(n, reads)
                    for a in range(2):
                        i = mm(out[0:rows, a, 0:288], lhs, rhs[:, 288 * a:288 * a + 288], start=True, stop=True)
                    i.then_inc(s_full, 1)

                wait_apart(pe, (s_w, NW), s_xs, b + 1)
                layer(S1, S, sw1[:], xs[0:S, :])
                layer(S2, 128, sw2[:], h1[:], [S1])
                for x in range(4):
                    layer(2 + 2 * x, 128, w1[:, 128 * x:128 * x + 128], xs[0:S, :])
                    layer(3 + 2 * x, S, w2[:, 64 * x:64 * x + 64], g1[:, x % 2, :], [2 + 2 * x])
                out = fill(GATE)
                for c in range(5):
                    rows = 128 if c < 4 else 64
                    i = mm(out[0:rows, 0, 4 * c:4 * c + 4], xs[:, 128 * c:128 * c + rows], gate[:], start=True, stop=True)
                i.then_inc(s_full, 1)
                for c in range(5):
                    rows = 128 if c < 4 else 64
                    out = fill(OUT + c, [S2, 3, 5, 7, 9] if c == 0 else [])
                    mm(out[0:rows, 0, 0:S], h2[:, 128 * c:128 * c + rows], sw3[:], start=True, stop=True)
                    for x in range(4):
                        i = mm(out[0:rows, 1, 64 * x:64 * x + 64], g2[:, x, 128 * c:128 * c + rows], w3[:, 64 * x:64 * x + 64], start=True, stop=True)
                    i.then_inc(s_full, 1)


def early_fusion_kernel(nc, d, out, ctx_dram, max_dram, h_spatial):
    fno_stage(nc, d, h_spatial)
    with ExitStack() as ctx:
        def sb(n, shape):
            return ctx.enter_context(nc.sbuf_tensor(n, shape, F32))

        res = sb("res", [128, ROWS, S])
        xn = sb("xn", [128, ROWS, S + 1])
        xt = sb("xt", [S + 1, B, T])
        ident = sb("ident", [128, 128])
        s_id = ctx.enter_context(nc.semaphore("ident_loaded"))
        with nc.Block() as block:
            @block.sync
            def _(sp):
                sp.dma_start(ident[:], d["c_ident"]).then_inc(s_id, 16)
                sp.wait_ge(s_id, 16)
        load_tokens(nc, d, h_spatial, res)
        norm_stage(nc, "n1", res, xn, xt, ident)
        with ExitStack() as inner:
            o_query = inner.enter_context(nc.sbuf_tensor("o_query", [128, ROWS, S], F32))
            o_key = inner.enter_context(nc.sbuf_tensor("o_key", [128, ROWS, S], F32))
            l1_stage(nc, d, xt, o_query, o_key, ident)
            fanin_stage(nc, d, res, xn, o_query, o_key, ident)
        norm_stage(nc, "n2", res, xn, xt, ident)
        slice_stage(nc, d, res, xn, xt, ident)
        norm_stage(nc, "n3", res, xn, xt, ident)
        mqa_stage(nc, d, xt, ctx_dram, max_dram, ident)
        mqa_out_stage(nc, d, ctx_dram, res)
        norm_stage(nc, "n4", res, xn, xt, ident)
        moe_stage(nc, d, res, xt)
        store_tokens(nc, out, res)


def kernel(**inputs):
    import concourse.bacc as bacc
    from concourse.bass_utils import run_bass_kernel_spmd

    nc = bacc.Bacc("TRN2", target_bir_lowering=False, num_devices=1)
    constants = {**fno_constants(), **l1_constants(), **moe_constants()}
    laid = {**constants, **fno_layout(inputs, constants), **l1_layout(inputs), **slice_layout(inputs), **mqa_layout(inputs),
            **moe_layout(inputs), "txt": inputs["txt"]}
    arrays, d = {}, {}
    for name, a in laid.items():
        a = np.ascontiguousarray(a)
        arrays["in_" + name] = a
        d[name] = nc.dram_tensor("in_" + name, a.shape, mybir.dt.from_np(a.dtype), kind="ExternalInput").ap()
    out = nc.dram_tensor("out_0_dram", (B, T, S), F32, kind="ExternalOutput").ap()
    ctx_dram = nc.dram_tensor("ctx_scratch", (B, T, 512), F32, kind="Internal").ap()
    max_dram = nc.dram_tensor("max_scratch", (40, 128), F32, kind="Internal").ap()
    h_spatial = nc.dram_tensor("h_scratch", (B, S, S), F32, kind="Internal").ap()
    early_fusion_kernel(nc, d, out, ctx_dram, max_dram, h_spatial)
    r = run_bass_kernel_spmd(nc, [arrays], core_ids=[0])
    return r.results[0]["out_0_dram"]
```

```python
from contextlib import ExitStack

import numpy as np

import concourse.bass as bass
from concourse import mybir

F32 = mybir.dt.float32
ALU = mybir.AluOpType
ACT = mybir.ActivationFunctionType
AX = mybir.AxisListType.X

B = 8
S = 64
CH = 32
LAYERS = 4
MODES_Y = 12
MODES_X = 24
MID = 4
NIMG = B + 3

T = 576
ROWS = 5 * B
EPS = 1e-5

def fno_constants():
    y = np.arange(S)
    ky = np.arange(MODES_Y)
    kx = np.concatenate([np.arange(MODES_Y), np.arange(S - MODES_Y, S)])
    x = np.arange(S)
    norm = 1.0 / np.sqrt(S)
    ay = 2 * np.pi * np.outer(y, ky) / S
    ax = 2 * np.pi * np.outer(x, kx) / S
    fy = np.zeros((2, S, 2, MODES_Y, 2))
    for r in range(2):
        fy[r, :, r, :, 0] = np.cos(ay) * norm
        fy[r, :, r, :, 1] = -np.sin(ay) * norm
    fx = np.zeros((S, 2, MODES_X, 2))
    fx[:, 0, :, 0] = np.cos(ax) * norm
    fx[:, 0, :, 1] = -np.sin(ax) * norm
    fx[:, 1, :, 0] = np.sin(ax) * norm
    fx[:, 1, :, 1] = np.cos(ax) * norm
    bx = np.zeros((MODES_X, 2, S, 2))
    bx[:, 0, :, 0] = np.cos(ax).T * norm
    bx[:, 0, :, 1] = np.sin(ax).T * norm
    bx[:, 1, :, 0] = -np.sin(ax).T * norm
    bx[:, 1, :, 1] = np.cos(ax).T * norm
    wy = np.where(ky == 0, 1.0, 2.0)[:, None]
    by = np.zeros((4, MODES_Y, 2, 2, 2, S))
    for r in range(4):
        by[r, :, 0, r // 2, r % 2, :] = wy * np.cos(ay).T * norm
        by[r, :, 1, r // 2, r % 2, :] = -wy * np.sin(ay).T * norm
    g = np.linspace(0.0, 1.0, S, dtype=np.float32)
    grid = np.stack([np.broadcast_to(g[:, None], (S, S)), np.broadcast_to(g[None, :], (S, S)), np.ones((S, S))])
    f32 = np.float32
    return {
        "c_fy": fy.reshape(128, 48).astype(f32),
        "c_fx": fx.reshape(128, 48).astype(f32),
        "c_bx": bx.reshape(48, 128).astype(f32),
        "c_by": by.reshape(96, 2 * 128).astype(f32),
        "c_grid": grid.astype(f32),
        "c_ident": np.eye(128, dtype=f32),
    }


def fno_layout(i, c):
    f32 = np.float32
    x = np.asarray(i["x"])[..., 0]
    img = np.concatenate([x, c["c_grid"]])
    a = {}
    a["f_img_pix"] = img.reshape(NIMG, 32, 128).transpose(2, 1, 0)
    a["f_img_row"] = img.reshape(NIMG, 32 * 128)
    pw, pb = np.asarray(i["L0_tok_p_w"]), np.asarray(i["L0_tok_p_b"])
    lift = np.zeros((NIMG, B, CH), f32)
    for b in range(B):
        lift[b, b] = pw[:, 0]
        lift[B, b] = pw[:, 1]
        lift[B + 1, b] = pw[:, 2]
        lift[B + 2, b] = pb
    a["f_lift"] = lift.reshape(NIMG, B * CH)
    a["f_lift_t"] = lift.reshape(NIMG, 2, 128).transpose(2, 1, 0)
    fw = np.asarray(i["L0_tok_fw"])
    a["f_modes"] = fw.transpose(0, 6, 2, 5, 1, 4, 3).reshape(LAYERS, 64, 288 * CH)
    w1, w2 = np.asarray(i["L0_tok_w1_w"]), np.asarray(i["L0_tok_w2_w"])
    a["f_w1t"] = np.tile(w1.transpose(0, 2, 1), (1, 4, 1))
    w2n = np.zeros((LAYERS, 4, CH, 4, CH), f32)
    w2t = np.zeros((LAYERS, 4, CH, 4, CH), f32)
    q1 = np.zeros((4, CH, 4, MID), f32)
    for b in range(4):
        w2n[:, b, :, b, :] = w2
        w2t[:, b, :, b, :] = w2.transpose(0, 2, 1)
        q1[b, :, b, :] = np.asarray(i["L0_tok_q1_w"]).T
    a["f_w2n"] = w2n.reshape(LAYERS, 128, 128)
    a["f_w2t"] = w2t.reshape(LAYERS, 128, 128)
    a["f_q1"] = q1.reshape(128, 16)
    a["f_b1"] = np.tile(np.asarray(i["L0_tok_w1_b"]), (1, B)).reshape(LAYERS, 1, B * CH)
    a["f_b2"] = np.tile(np.asarray(i["L0_tok_w2_b"]), (1, 4)).T
    a["f_q1b"] = np.broadcast_to(np.asarray(i["L0_tok_q1_b"]), (128, MID))
    a["f_q2"] = np.broadcast_to(np.asarray(i["L0_tok_q2_w"]).reshape(-1), (128, MID))
    a["f_q2b"] = np.broadcast_to(np.asarray(i["L0_tok_q2_b"]), (128, 1))
    return a


class BankRing:

    def __init__(self, owners, size):
        self.owners, self.size = owners, size
        self.per = {e: owners.count(e) for e in ("v", "a")}

    def emptied(self, n):
        return self.owners[n], self.owners[:n + 1].count(self.owners[n])

    def latest(self, fills):
        need = {}
        for n in fills:
            who, count = self.emptied(n % len(self.owners))
            if n < 0:
                count -= self.per[who]
            need[who] = max(need.get(who, count), count)
        return sorted(need.items())


def fno_steps():
    steps = [("proj", 1), ("modes", 3), ("mix1", 12), ("inv_x", 6), ("turn_y", 8), ("inv_y", 16), ("turn_r", 16),
             ("fwd_y", 8), ("turn_x", 6), ("fwd_x", 4), ("mix2", 4)]
    first, owners = {}, []
    for name, n in steps:
        first[name] = len(owners)
        owners += ["v"] * n if name in ("mix2", "proj") else ["va"[k % 2] for k in range(n)]
    return first, owners


def fno_stage(nc, d, h_spatial):
    FIRST, OWNERS = fno_steps()
    ring = BankRing(OWNERS, 6)
    NG = len(OWNERS)
    assert NG % ring.size == 0
    with ExitStack() as ctx:
        def sb(n, shape, dt=F32):
            return ctx.enter_context(nc.sbuf_tensor("fno_" + n, shape, dt))

        def sem(n):
            return ctx.enter_context(nc.semaphore("fno_" + n))

        mid = ctx.enter_context(nc.psum_tensor("fno_mid", [128, 2, 512], F32))
        bank = ctx.enter_context(nc.psum_tensor("fno_bank", [128, 6, 512], F32))

        fy = sb("fy", [128, 48]); fx = sb("fx", [128, 48]); bx = sb("bx", [48, 128]); by = sb("by", [96, 2, 128])
        ident = sb("ident", [128, 128])
        img_pix = sb("img_pix", [128, 32, NIMG]); img_row = sb("img_row", [NIMG, 32, 128])
        lift = sb("lift", [NIMG, 2, 128]); lift_t = sb("lift_t", [128, 2, NIMG])
        q1 = sb("q1", [128, 16]); q1b = sb("q1b", [128, MID]); q2 = sb("q2", [128, MID]); q2b = sb("q2b", [128, 1])
        b2 = sb("b2", [128, LAYERS]); b2s = sb("b2s", [128, 1])
        w_modes = sb("w_modes", [64, 288, CH])
        w1t = sb("w1t", [128, LAYERS, CH]); w2n = sb("w2n", [128, LAYERS, 128]); w2t = sb("w2t", [128, LAYERS, 128])
        b1 = sb("b1", [1, LAYERS, B * CH]); b1c = sb("b1c", [1, B * CH])
        w1c = sb("w1c", [128, CH]); w2c = sb("w2c", [128, 2, 128])
        spec = sb("spec", [128, 3, 2, 288])
        lhs = sb("lhs", [64, 2, B, 288])
        y_out = sb("y_out", [128, 3, MODES_X, 2, B])
        v_in = sb("v_in", [128, MODES_Y, B * CH])
        t_x = sb("t_x", [128, 2, S, MODES_Y, 2])
        t_y = sb("t_y", [96, 16, B * CH])
        relu_u = sb("relu_u", [128, 32, B * CH])
        proj = sb("proj", [128, 16])
        r_t = sb("r_t", [128, 8, 512])
        g_y = t_x[:].rearrange("p g x k c -> p (g x k c)").rearrange("p (g k x c) -> p g k x c", g=2, k=MODES_Y, c=2)
        g_x = v_in[:].rearrange("p k n -> p (k n)").rearrange("p (t n) -> p t n", n=128)
        p_x = sb("p_x", [128, 2, 576])
        img_y = sb("img_y", [NIMG, MODES_Y, S, 2]); img_t = sb("img_t", [128, MODES_Y, NIMG]); img_x = sb("img_x", [NIMG, 576])
        q0 = sb("q0", [NIMG, 2, 16])
        hid = sb("hid", [128, 32, B, MID]); feat = sb("feat", [128, 32, B]); feat_r = sb("feat_r", [128, 2, 4, 32])
        tok = sb("tok", [128, 2, 128])

        s_const = sem("const"); s_wm = sem("w_modes"); s_wd = sem("modes_used")
        s_full = sem("bank_full"); s_ev = sem("emptied_v"); s_ea = sem("emptied_a")
        s_wc = sem("layer_weights"); s_b1 = sem("bias1_added"); s_spec = sem("spectrum"); s_dc = sem("constant_term")
        s_lhs = sem("lhs_loaded"); s_fin = sem("tail_v"); s_pre = sem("pre_pe")
        s_pv = sem("pre_v"); s_layer = sem("layer_projected"); s_turn = sem("tail_pe"); s_tok = sem("tok_out");
        emptied_sem = {"v": s_ev, "a": s_ea}

        def emptied(eng, l, n):
            who, count = ring.emptied(n)
            eng.wait_ge(emptied_sem[who], l * ring.per[who] + count)

        def step_in_sbuf(eng, l, name, n):
            last = {}
            for k in range(FIRST[name], FIRST[name] + n):
                last[OWNERS[k]] = k
            for k in last.values():
                emptied(eng, l, k)

        block = ctx.enter_context(nc.Block())
        loads = [(fy, "c_fy"), (fx, "c_fx"), (bx, "c_bx"), (ident, "c_ident"), (q1, "f_q1"), (q1b, "f_q1b"),
                 (q2, "f_q2"), (q2b, "f_q2b"), (b2, "f_b2"), (img_pix, "f_img_pix"), (lift_t, "f_lift_t")]
        NCONST = 16 * (len(loads) + 7)

        @block.sync
        def _(sp):
            for t, name in loads:
                sp.dma_start(t[:], d[name]).then_inc(s_const, 16)
            sp.dma_start(by[:], d["c_by"].rearrange("p (s n) -> p s n", s=2)).then_inc(s_const, 16)
            sp.dma_start(img_row[:], d["f_img_row"].rearrange("p (s n) -> p s n", s=32)).then_inc(s_const, 16)
            sp.dma_start(lift[:], d["f_lift"].rearrange("p (s n) -> p s n", s=2)).then_inc(s_const, 16)
            sp.dma_start(w1t[:], d["f_w1t"].rearrange("l p n -> p l n")).then_inc(s_const, 16)
            sp.dma_start(w2n[:], d["f_w2n"].rearrange("l p n -> p l n")).then_inc(s_const, 16)
            sp.dma_start(w2t[:], d["f_w2t"].rearrange("l p n -> p l n")).then_inc(s_const, 16)
            sp.dma_start(b1[:], d["f_b1"].rearrange("l p n -> p l n")).then_inc(s_const, 16)

            def gather(l):
                sp.wait_ge(s_spec, l + 1)
                for c2, plane in ((0, (0, 1)), (1, (2, 0))):
                    for c in range(2):
                        for b4 in range(4):
                            sp.dma_start(lhs[32 * c2:32 * c2 + 32, c, :, :].rearrange("p (g b) m -> p g b m", g=2)[:, :, b4, :],
                                         spec[32 * b4:32 * b4 + 32, plane[c], :, :]).then_inc(s_lhs, 16)

            gather(0)
            with sp.Fori(1, LAYERS) as l:
                gather(l)
            for g in range(2):
                for b4 in range(4):
                    if g == 0 and b4 == 0:
                        sp.wait_ge(s_fin, 6)
                    sp.dma_start(h_spatial[4 * g + b4].rearrange("(a r) y -> a (r y)", r=2),
                                 tok[32 * b4:32 * b4 + 32, g, :]).then_inc(s_tok, 16)
            sp.wait_ge(s_tok, 16 * 8)

        @block.gpsimd
        def _(pool):
            pool.dma_start(w_modes[:], d["f_modes"][0].rearrange("p (m o) -> p m o", o=CH)).then_inc(s_wm, 16)
            with pool.Fori(1, LAYERS) as l:
                pool.wait_ge(s_full, (l - 1) * NG + 4)
                pool.dma_start(w_modes[:], d["f_modes"][bass.ds(l, 1)].rearrange("a p (m o) -> p (a m) o", o=CH)).then_inc(s_wm, 16)

        def add_spectrum(src, g, half, first):
            for c in range(2):
                dst = spec[:, c, g, 144 * half:144 * half + 144]
                if first:
                    i = nc.vector.tensor_copy(dst, src[:, c:288:2])
                else:
                    i = nc.vector.tensor_tensor(dst, dst, src[:, c:288:2], ALU.add)
            return i

        def empty_banks(eng, l, me):
            done = emptied_sem[me]

            def move(out, in_):
                return nc.vector.tensor_copy(out, in_) if me == "v" else nc.scalar.copy(out, in_)

            def mine(name, n):
                for k in range(n):
                    at = FIRST[name] + k
                    if OWNERS[at] == me:
                        eng.wait_ge(s_full, l * NG + at + 1)
                        yield k, bank[:, at % ring.size, :]

            for _, src in mine("proj", 1):
                move(proj[:], src[:, 0:16]).then_inc(done, 1)
            for r, src in mine("modes", 3):
                move(y_out[:, r].rearrange("p k c b -> p (k c b)"), src[:, 0:384]).then_inc(done, 1)
            for ky, src in mine("mix1", 12):
                i = move(v_in[0:48, ky, :], src[0:48, 0:256])
                if ky:
                    i.then_inc(done, 1)
                    continue
                i.then_inc(s_b1, 1)
                eng.wait_ge(s_b1, l + 1)
                nc.vector.scalar_tensor_tensor(out=v_in[0:1, 0, :], in0=b1c[:, :], scalar=float(S), in1=v_in[0:1, 0, :],
                                               op0=ALU.mult, op1=ALU.add).then_inc(done, 1)
            for k, src in mine("inv_x", 6):
                g, ky = divmod(4 * k, 12)
                move(t_x[:, g, :, ky:ky + 4, :].rearrange("p x k c -> p k x c"),
                     src.rearrange("p (k x c) -> p k x c", k=4, c=2)).then_inc(done, 1)
            for k, src in mine("turn_y", 8):
                move(t_y[:, 2 * k:2 * k + 2, :].rearrange("p a n -> p (a n)"), src[0:96, :]).then_inc(done, 1)
            for k, src in mine("inv_y", 16):
                out = relu_u[:, 2 * k:2 * k + 2, :].rearrange("p a n -> p (a n)")
                if me == "v":
                    nc.vector.tensor_scalar(out, src, 0.0, None, ALU.max).then_inc(done, 1)
                else:
                    nc.scalar.activation(out, src, ACT.Relu).then_inc(done, 1)
            for k, src in mine("turn_r", 16):
                move(r_t[:, k % 8, :], src).then_inc(done, 1)
            for k, src in mine("fwd_y", 8):
                g, x0 = k // 4, 16 * (k % 4)
                move(g_y[:, g, :, x0:x0 + 16, :].rearrange("p k x c -> p x k c"),
                     src[:, 0:384].rearrange("p (x k c) -> p x k c", x=16, c=2)).then_inc(done, 1)
            for k, src in mine("turn_x", 6):
                move(g_x[:, 4 * k:4 * k + 4, :].rearrange("p t n -> p (t n)"), src).then_inc(done, 1)
            for k, src in mine("fwd_x", 4):
                move(p_x[:, k // 2, 288 * (k % 2):288 * (k % 2) + 288], src[:, 0:288]).then_inc(done, 1)
            for k, src in mine("mix2", 4):
                add_spectrum(src, k // 2, k % 2, False).then_inc(done, 1)

        @block.scalar
        def _(act):
            with act.Fori(0, LAYERS) as l:
                empty_banks(act, l, "a")

        @block.vector
        def _(v):
            v.wait_ge(s_const, NCONST)
            nc.vector.tensor_reduce(b2s[:], b2[:], AX, ALU.add).then_inc(s_pv, 1)
            v.wait_ge(s_pv, 1)
            for g in range(2):
                nc.vector.tensor_tensor(lift_t[:, g, NIMG - 1:NIMG], lift_t[:, g, NIMG - 1:NIMG], b2s[:], ALU.add).then_inc(s_pv, 1)
            for k in range(4):
                v.wait_ge(s_pre, k + 1)
                nc.vector.tensor_copy(img_y[:, :, 16 * k:16 * k + 16, :].rearrange("p k x c -> p x k c"),
                                      bank[0:NIMG, k, 0:384].rearrange("p (x k c) -> p x k c", x=16, c=2)).then_inc(s_pv, 1)
            v.wait_ge(s_pre, 5)
            nc.vector.tensor_copy(img_t[:].rearrange("p k n -> p (k n)"), bank[:, 4, 0:12 * NIMG]).then_inc(s_pv, 1)
            v.wait_ge(s_pre, 6)
            nc.vector.tensor_copy(q0[:].rearrange("p g n -> p (g n)"), bank[0:NIMG, 5, 0:32]).then_inc(s_pv, 1)
            for k in range(2):
                v.wait_ge(s_pre, 7 + k)
                nc.vector.tensor_copy(img_x[:, 288 * k:288 * k + 288], bank[0:NIMG, k, 0:288]).then_inc(s_pv, 1)
            for k in range(4):
                v.wait_ge(s_pre, 9 + k)
                add_spectrum(bank[:, 2 + k, :], k // 2, k % 2, True).then_inc(s_pv, 1)
            v.wait_ge(s_pv, 15)
            nc.vector.tensor_scalar(spec[:, 2, :, :], spec[:, 1, :, :], -1.0, None, ALU.mult).then_inc(s_spec, 1)

            with v.Fori(0, LAYERS) as l:
                nc.vector.tensor_copy(w1c[:], w1t[:, bass.ds(l, 1), :].rearrange("p a n -> p (a n)")).then_inc(s_wc, 1)
                nc.vector.tensor_copy(w2c[:, 0, :], w2n[:, bass.ds(l, 1), :].rearrange("p a n -> p (a n)")).then_inc(s_wc, 1)
                nc.vector.tensor_copy(w2c[:, 1, :], w2t[:, bass.ds(l, 1), :].rearrange("p a n -> p (a n)")).then_inc(s_wc, 1)
                nc.vector.tensor_copy(b1c[:], b1[:, bass.ds(l, 1), :].rearrange("p a n -> p (a n)")).then_inc(s_wc, 1)
                empty_banks(v, l, "v")
                v.wait_ge(s_ev, (l + 1) * ring.per["v"])
                for g in range(2):
                    nc.vector.scalar_tensor_tensor(out=spec[:, 0, g, 0:1], in0=b2[:, bass.ds(l, 1)], scalar=float(S),
                                                   in1=spec[:, 0, g, 0:1], op0=ALU.mult, op1=ALU.add).then_inc(s_dc, 1)
                v.wait_ge(s_dc, l * 2 + 2)
                nc.vector.tensor_scalar(spec[:, 2, :, :], spec[:, 1, :, :], -1.0, None, ALU.mult).then_inc(s_spec, 1)

            v.wait_ge(s_layer, LAYERS)
            h3 = hid[:].rearrange("p x b j -> p (x b) j")
            nc.vector.tensor_tensor(h3, mid[:].rearrange("p k (n j) -> p (k n) j", j=MID),
                                    q1b[:, None, :].broadcast_to([128, 256, MID]), ALU.add).then_inc(s_fin, 1)
            v.wait_ge(s_fin, 1)
            nc.vector.scalar_tensor_tensor(out=h3, in0=h3, scalar=0.0, in1=q2[:, None, :].broadcast_to([128, 256, MID]),
                                           op0=ALU.max, op1=ALU.mult).then_inc(s_fin, 1)
            v.wait_ge(s_fin, 2)
            nc.vector.tensor_reduce(feat[:].rearrange("p x b -> p (x b)"), h3, AX, ALU.add).then_inc(s_fin, 1)
            v.wait_ge(s_fin, 3)
            nc.vector.tensor_scalar(feat_r[:].rearrange("p g b x -> p (g b) x"), feat[:].rearrange("p x b -> p b x"),
                                    q2b[:, 0:1], None, ALU.add).then_inc(s_fin, 1)
            for g in range(2):
                v.wait_ge(s_turn, g + 1)
                nc.vector.tensor_copy(tok[:, g, :], bank[:, g, 0:128]).then_inc(s_fin, 1)

        @block.tensor
        def _(pe):
            mm = nc.tensor.matmul
            pe.wait_ge(s_const, NCONST)
            for xh in range(32):
                i = mm(bank[0:NIMG, xh // 8, 48 * (xh % 8):48 * (xh % 8) + 48], img_pix[:, xh, :], fy[:], start=True, stop=True)
                if xh % 8 == 7:
                    i.then_inc(s_pre, 1)
            pe.wait_ge(s_pv, 7)
            for ky in range(12):
                i = nc.tensor.transpose(bank[:, 4, NIMG * ky:NIMG * ky + NIMG], img_y[:, ky, :, :].rearrange("p x c -> p (x c)"),
                                        ident[0:NIMG, 0:NIMG])
            i.then_inc(s_pre, 1)
            for g in range(2):
                i = mm(bank[0:NIMG, 5, 16 * g:16 * g + 16], lift_t[:, g, :], q1[:], start=True, stop=True)
            i.then_inc(s_pre, 1)
            pe.wait_ge(s_pv, 8)
            for ky in range(12):
                i = mm(bank[0:NIMG, ky // 6, 48 * (ky % 6):48 * (ky % 6) + 48], img_t[:, ky, :], fx[:], start=True, stop=True)
                if ky % 6 == 5:
                    i.then_inc(s_pre, 1)
            pe.wait_ge(s_pv, 11)
            for k in range(4):
                mm(bank[:, 2 + k, 0:288], lift[:, k // 2, :], img_x[:, 288 * (k % 2):288 * (k % 2) + 288], start=True, stop=True).then_inc(s_pre, 1)
            for xh in range(32):
                mm(mid[:, xh // 16, 32 * (xh % 16):32 * (xh % 16) + 32], img_row[:, xh, :], q0[:].rearrange("p g n -> p (g n)"),
                   start=(xh % 16 == 0), stop=False, skip_group_check=True)

            with pe.Fori(0, LAYERS) as l:
                def fill(name, k):
                    n = FIRST[name] + k
                    if n >= ring.size:
                        emptied(pe, l, n - ring.size)
                    return bank[:, n % ring.size, :]

                pe.wait_ge(s_lhs, 16 * 16 * (l + 1))
                pe.wait_ge(s_wm, 16 * (l + 1))
                pe.wait_ge(s_wc, 4 * (l + 1))
                out = fill("proj", 0)
                mm(out[:, 0:16], w2c[:, 0, :], q1[:], start=True, stop=True).then_inc(s_full, 1)
                for r in range(3):
                    out = fill("modes", r)
                    for kx in range(MODES_X):
                        for q in range(4):
                            m = (4 * r + q) * MODES_X + kx
                            i = mm(out[32 * q:32 * q + 32, 16 * kx:16 * kx + 16], w_modes[:, m, :], lhs[:, :, :, m],
                                   start=True, stop=True, tile_position=(0, 32 * q))
                    i.then_inc(s_full, 1)
                for ky in range(12):
                    r, q = divmod(ky, 4)
                    if q == 0:
                        emptied(pe, l, FIRST["modes"] + r)
                    out = fill("mix1", ky)
                    for b in range(B):
                        i = mm(out[0:48, 32 * b:32 * b + 32], y_out[32 * q:32 * q + 32, r, :, :, b].rearrange("p k c -> p (k c)"),
                               w1c[32 * q:32 * q + 32, :], start=True, stop=True, tile_position=(32 * q, 0))
                    i.then_inc(s_full, 1)
                step_in_sbuf(pe, l, "mix1", 12)
                for k in range(6):
                    out = fill("inv_x", k)
                    for j in range(4):
                        g, ky = divmod(4 * k + j, 12)
                        i = mm(out[:, 128 * j:128 * j + 128], v_in[0:48, ky, 128 * g:128 * g + 128], bx[:], start=True, stop=True)
                    i.then_inc(s_full, 1)
                step_in_sbuf(pe, l, "inv_x", 6)
                for k in range(8):
                    out = fill("turn_y", k)
                    for j in range(4):
                        x4, g = 2 * k + j // 2, j % 2
                        i = nc.tensor.transpose(out[0:96, 128 * j:128 * j + 128],
                                                t_x[:, g, 4 * x4:4 * x4 + 4, :, :].rearrange("p x k c -> p (x k c)"), ident[:])
                    i.then_inc(s_full, 1)
                for k in range(16):
                    emptied(pe, l, FIRST["turn_y"] + k // 2)
                    out = fill("inv_y", k)
                    for j in range(2):
                        i = mm(out[:, 256 * j:256 * j + 256], by[:, j, :], t_y[:, k, :], start=True, stop=True)
                    i.then_inc(s_full, 1)
                def project(k):
                    emptied(pe, l, FIRST["turn_r"] + k)
                    for j in range(4):
                        xh, g = 2 * k + j // 2, j % 2
                        at = 32 * (xh % 16) + 16 * g
                        i = mm(mid[:, xh // 16, at:at + 16], r_t[:, k % 8, 128 * j:128 * j + 128], proj[:],
                               start=False, stop=False, skip_group_check=True)
                    return i

                for k in range(16):
                    emptied(pe, l, FIRST["inv_y"] + k)
                    out = fill("turn_r", k)
                    for j in range(4):
                        xh, g = 2 * k + j // 2, j % 2
                        i = nc.tensor.transpose(out[:, 128 * j:128 * j + 128], relu_u[:, xh, 128 * g:128 * g + 128], ident[:])
                    i.then_inc(s_full, 1)
                    if k >= 2:
                        project(k - 2)
                project(14)
                project(15).then_inc(s_layer, 1)
                for k in range(8):
                    out = fill("fwd_y", k)
                    for j in range(8):
                        g, xh = k // 4, 8 * (k % 4) + j
                        i = mm(out[:, 48 * j:48 * j + 48], relu_u[:, xh, 128 * g:128 * g + 128], fy[:], start=True, stop=True)
                    i.then_inc(s_full, 1)
                step_in_sbuf(pe, l, "fwd_y", 8)
                for k in range(6):
                    out = fill("turn_x", k)
                    for j in range(4):
                        g, ky = divmod(4 * k + j, 12)
                        i = nc.tensor.transpose(out[:, 128 * j:128 * j + 128], g_y[:, g, ky, :, :].rearrange("p x c -> p (x c)"), ident[:])
                    i.then_inc(s_full, 1)
                step_in_sbuf(pe, l, "turn_x", 6)
                for k in range(4):
                    out = fill("fwd_x", k)
                    for j in range(6):
                        i = mm(out[:, 48 * j:48 * j + 48], g_x[:, 6 * k + j, :], fx[:], start=True, stop=True)
                    i.then_inc(s_full, 1)
                for k in range(4):
                    emptied(pe, l, FIRST["fwd_x"] + k)
                    out = fill("mix2", k)
                    mm(out[:, 0:288], w2c[:, 1, :], p_x[:, k // 2, 288 * (k % 2):288 * (k % 2) + 288], start=True, stop=True).then_inc(s_full, 1)

            pe.wait_ge(s_fin, 4)
            for g in range(2):
                nc.tensor.transpose(bank[:, g, 0:128], feat_r[:, g, :, :].rearrange("p b x -> p (b x)"), ident[:]).then_inc(s_turn, 1)


def wait_apart(eng, met, sem, value):
    if not isinstance(value, int):
        value = eng.to_reg(value)
    eng.wait_ge(*met)
    eng.wait_ge(sem, value)


def load_tokens(nc, d, h_spatial, res):
    with ExitStack() as ctx:
        s_in = ctx.enter_context(nc.semaphore("tok_loaded"))
        s_pad = ctx.enter_context(nc.semaphore("tok_pad"))
        r4 = res[:].rearrange("p (b c) f -> p b c f", b=B)
        block = ctx.enter_context(nc.Block())

        @block.sync
        def _(sp):
            txt = d["txt"]
            sp.dma_start(r4[0:64, :, 0, :], h_spatial.rearrange("b t f -> t b f")).then_inc(s_in, 16)
            sp.dma_start(r4[64:128, :, 0, :], txt[:, 0:64, :].rearrange("b t f -> t b f")).then_inc(s_in, 16)
            for c in range(1, 4):
                sp.dma_start(r4[:, :, c, :], txt[:, 128 * c - 64:128 * c + 64, :].rearrange("b t f -> t b f")).then_inc(s_in, 16)
            sp.dma_start(r4[0:64, :, 4, :], txt[:, 448:512, :].rearrange("b t f -> t b f")).then_inc(s_in, 16)
            sp.wait_ge(s_in, 16 * 6)

        @block.gpsimd
        def _(pool):
            nc.gpsimd.memset(r4[64:128, :, 4, :], 0.0).then_inc(s_pad, 1)
            pool.wait_ge(s_pad, 1)


def norm_stage(nc, tag, res, xn, xt, ident):
    PARTS = 4
    W = ROWS // PARTS
    with ExitStack() as ctx:
        def sb(n, shape, dt=F32):
            return ctx.enter_context(nc.sbuf_tensor(f"{tag}_{n}", shape, dt))

        def sem(n):
            return ctx.enter_context(nc.semaphore(f"{tag}_{n}"))

        sq = sb("sq", [128, ROWS, S])
        total = sb("total", [128, ROWS]); mean = sb("mean", [128, ROWS]); var = sb("var", [128, ROWS])
        std = sb("std", [128, ROWS]); rstd = sb("rstd", [128, ROWS]); eps = sb("eps", [128, 1])
        turned = ctx.enter_context(nc.psum_tensor(f"{tag}_turned", [128, 4, 1024], F32))
        s_one = sem("ones"); s_sum = sem("sum"); s_mean = sem("mean"); s_cen = sem("centred"); s_sq = sem("squares")
        s_var = sem("var"); s_std = sem("std"); s_rstd = sem("rstd"); s_xn = sem("xn"); s_turn = sem("turned"); s_out = sem("xt")
        block = ctx.enter_context(nc.Block())

        @block.gpsimd
        def _(pool):
            nc.gpsimd.memset(eps[:], EPS).then_inc(s_one, 1)
            pool.wait_ge(s_one, 1)
            nc.gpsimd.memset(xn[:, :, S:S + 1], 1.0).then_inc(s_one, 1)
            pool.wait_ge(s_one, 2)
            nc.gpsimd.memset(xt[S:S + 1, :, :], 1.0).then_inc(s_one, 1)
            pool.wait_ge(s_one, 3)

        @block.vector
        def _(v):
            for p in range(PARTS):
                rows = slice(W * p, W * p + W)
                nc.vector.tensor_reduce(total[:, rows], res[:, rows, :], AX, ALU.add).then_inc(s_sum, 1)
            for p in range(PARTS):
                rows = slice(W * p, W * p + W)
                v.wait_ge(s_sum, p + 1)
                nc.vector.tensor_scalar(mean[:, rows], total[:, rows], 1.0 / S, None, ALU.mult).then_inc(s_mean, 1)
            for p in range(PARTS):
                rows = slice(W * p, W * p + W)
                v.wait_ge(s_mean, p + 1)
                nc.vector.tensor_tensor(xn[:, rows, 0:S], res[:, rows, :], mean[:, rows, None].broadcast_to([128, W, S]),
                                        ALU.subtract).then_inc(s_cen, 1)
            for p in range(PARTS):
                rows = slice(W * p, W * p + W)
                v.wait_ge(s_cen, p + 1)
                nc.vector.tensor_tensor(sq[:, rows, :], xn[:, rows, 0:S], xn[:, rows, 0:S], ALU.mult).then_inc(s_sq, 1)
                v.wait_ge(s_sq, p + 1)
                nc.vector.tensor_reduce(var[:, rows], sq[:, rows, :], AX, ALU.add).then_inc(s_var, 1)
            for p in range(PARTS):
                rows = slice(W * p, W * p + W)
                v.wait_ge(s_std, p + 1)
                nc.vector.reciprocal(rstd[:, rows], std[:, rows]).then_inc(s_rstd, 1)
                v.wait_ge(s_rstd, p + 1)
                nc.vector.tensor_tensor(xn[:, rows, 0:S], xn[:, rows, 0:S], rstd[:, rows, None].broadcast_to([128, W, S]),
                                        ALU.mult).then_inc(s_xn, 1)

        @block.scalar
        def _(act):
            act.wait_ge(s_one, 3)
            for p in range(PARTS):
                rows = slice(W * p, W * p + W)
                act.wait_ge(s_var, p + 1)
                nc.scalar.activation(std[:, rows], var[:, rows], ACT.Sqrt, bias=eps[:, 0:1], scale=1.0 / S).then_inc(s_std, 1)
            for b in range(B):
                act.wait_ge(s_turn, b + 1)
                nc.scalar.copy(xt[0:S, b, :], turned[0:S, b % 4, 0:T]).then_inc(s_out, 1)

        @block.tensor
        def _(pe):
            for b in range(B):
                if b % 2 == 0:
                    pe.wait_ge(s_xn, b // 2 + 1)
                if b >= 4:
                    pe.wait_ge(s_out, b - 3)
                for c in range(5):
                    n = min(128, T - 128 * c)
                    i = nc.tensor.transpose(turned[0:S, b % 4, 128 * c:128 * c + n], xn[0:n, 5 * b + c, 0:S], ident[0:n, 0:n])
                i.then_inc(s_turn, 1)


def l1_layout(i):
    f32 = np.float32
    w, bias = np.asarray(i["L0_attn_wqv_w"]), np.asarray(i["L0_attn_wqv_b"])
    wt = np.concatenate([w.T, bias[None]])
    wk = np.asarray(i["L0_attn_wk"])
    a = {"l1_wq": padded(wt[:, :512]), "l1_wvf": padded(wt[:, 512:1024])}
    wb = w[1024:].reshape(4, 2, S, S)
    both = np.zeros((2, S, 4, S + 1), f32)
    both[:, :, :, :S] = wb.transpose(1, 3, 0, 2)
    both[:, :, :, S] = wk.reshape(4, 2, S).transpose(1, 2, 0)
    a["l1_wvb"] = both.reshape(128, 4 * 65)
    bb = np.zeros((2, 4, S + 1), f32)
    bb[:, :, :S] = bias[1024:].reshape(4, 2, S).transpose(1, 0, 2)
    a["l1_bvb"] = padded(bb.reshape(2, 4 * 65))
    a["l1_wk"] = wk.reshape(4, 128).T
    a["l1_fan"] = np.concatenate([np.asarray(i["L0_attn_fanin_w"]).T, np.asarray(i["L0_attn_fanin_b"])[None]])
    return a


def l1_constants():
    f32 = np.float32
    dup = np.concatenate([np.eye(S), np.eye(S)], 1)
    sel = np.zeros((128, 62))
    sel[:64, 30] = 2.0
    sel[64:, 31] = 2.0
    neg = np.zeros((2, S, S, 2))
    par = np.zeros((2, S, 2))
    for h in range(2):
        neg[h, :, :, h] = -1.0
        par[h, :, h] = 1.0
    return {"c_dup": padded(dup).astype(f32), "c_sel": sel.astype(f32), "c_neg": neg.reshape(128, 128).astype(f32),
            "c_par": padded(par.reshape(2, 128)).astype(f32)}


def l1_stage(nc, d, xt, o_query, o_key, ident):
    RING = 16
    GROUPS = 16
    SCALE = 1.0 / 8.0
    FILLS = ["v"] * 2 + ["va"[k % 2] for k in range(22)]
    fills = BankRing(FILLS, 6)
    with ExitStack() as ctx:
        def sb(n, shape, dt=F32):
            return ctx.enter_context(nc.sbuf_tensor("l1_" + n, shape, dt))

        def sem(n):
            return ctx.enter_context(nc.semaphore("l1_" + n))

        wq = sb("wq", [128, 512]); wvf = sb("wvf", [128, 512]); wvb = sb("wvb", [128, 4, 65]); bvb = sb("bvb", [128, 4 * 65])
        wk = sb("wk", [128, 4]); nwk = sb("nwk", [128, 4])
        dup = sb("dup", [128, 128]); sel = sb("sel", [128, 62]); neg = sb("neg", [128, 128]); par = sb("par", [128, 128])
        xs = sb("xs", [128, T]); xdup = sb("xdup", [128, T]); xpar = sb("xpar", [128, T, 2])
        q = sb("q", [128, 4, T]); nk = sb("nk", [128, 36 * 64])
        vf = sb("vf", [128, 5, 512]); vb = sb("vb", [128, 36, 65])
        nks = sb("nks", [128, 3, 64])
        unit = sb("unit", [128, RING, T])
        e = sb("e", [128, 3, T]); z = sb("z", [128, 3]); z1 = sb("z1", [128, 3]); rz = sb("rz", [128, 3])
        at = sb("at", [128, 3, 5, 128])
        okf = sb("okf", [64, 36, S]); oks = sb("oks", [64, 9, S])
        score = ctx.enter_context(nc.psum_tensor("l1_score", [128, 6, 512], F32))
        turn = ctx.enter_context(nc.psum_tensor("l1_turn", [128, 512], F32))
        acc = ctx.enter_context(nc.psum_tensor("l1_acc", [128, 512], F32))

        s_w = sem("weights"); s_init = sem("init"); s_xs = sem("xs"); s_fill = sem("fill"); s_fv = sem("fill_emptied_v")
        s_fa = sem("fill_emptied_a"); s_xp = sem("x_by_parity"); s_nk = sem("minus_k"); s_nks = sem("minus_k_staged")
        s_uv = sem("units_v"); s_ua = sem("units_a"); s_use = sem("units_summed"); s_e = sem("exp")
        s_z1 = sem("z1"); s_rz = sem("rz"); s_p = sem("probs"); s_t = sem("turned"); s_ata = sem("at_a"); s_atv = sem("at_v")
        s_k = sem("key_out"); s_kc = sem("key_out_copied"); s_acc = sem("acc_copied"); s_add = sem("key_out_summed"); s_od = sem("o_key_moved")
        filled = {"v": s_fv, "a": s_fa}
        by_vector = [[True, False, True, g % 2 == 1] for g in range(GROUPS)]

        def emptied(eng, b, n):
            who, count = fills.emptied(n)
            eng.wait_ge(filled[who], b * fills.per[who] + count)

        block = ctx.enter_context(nc.Block())

        @block.sync
        def _(sp):
            for t, name in ((wq, "l1_wq"), (wvf, "l1_wvf"), (bvb, "l1_bvb"), (wk, "l1_wk"), (dup, "c_dup"), (sel, "c_sel"),
                            (neg, "c_neg"), (par, "c_par")):
                sp.dma_start(t[:], d[name]).then_inc(s_w, 16)
            sp.dma_start(wvb[:], d["l1_wvb"].rearrange("p (a n) -> p a n", a=4)).then_inc(s_w, 16)
            with sp.Fori(0, B) as b:
                sp.wait_ge(s_add, 3 * b + 3)
                sp.dma_start(o_key[0:64, bass.ds(5 * b, 5), :], oks[:, 0:9:2, :]).then_inc(s_od, 16)
                sp.dma_start(o_key[64:128, bass.ds(5 * b, 4), :], oks[:, 1:9:2, :]).then_inc(s_od, 16)

        def tiles(b, it, first):
            for k in range(3):
                prev = None if first and k == 0 else ((it - 1, 2) if k == 0 else (it, k - 1))
                yield k, prev

        def trips(eng, b, body, last):
            body(0, True)
            with eng.Fori(1, 12) as it:
                body(it, False)
            last(11, 2)

        @block.gpsimd
        def _(pool):
            for n, t in enumerate((xpar, vf, at, o_key, o_query)):
                if n:
                    pool.wait_ge(s_init, n)
                nc.gpsimd.memset(t[:], 0.0).then_inc(s_init, 1)
            with pool.Fori(0, B) as b:
                def stage(it, first):
                    for k in range(3):
                        n = 36 * b + 3 * it + k
                        if k == 0 and first:
                            wait_apart(pool, (s_w, 16 * 9), s_nk, 4 * b + 4)
                        if not first:
                            wait_apart(pool, (s_w, 16 * 9), s_uv, (n - 2) * GROUPS)
                            wait_apart(pool, (s_w, 16 * 9), s_ua, (n - 2) * GROUPS)
                        nc.gpsimd.tensor_copy(nks[:, k, :], nk[:, bass.ds(192 * it + 64 * k, 64)]).then_inc(s_nks, 1)

                stage(0, True)
                with pool.Fori(1, 12) as it:
                    stage(it, False)

        def empty_fills(me, got):
            def move(out, in_):
                i = nc.vector.tensor_copy(out, in_) if me == "v" else nc.scalar.copy(out, in_)
                i.then_inc(filled[me], 1)

            for n in range(2, 24):
                if FILLS[n] != me:
                    continue
                src = got(n)
                if n < 10:
                    hp, half = divmod(n - 2, 2)
                    move(q[:, hp, 288 * half:288 * half + 288], src[:, 0:288])
                elif n < 15:
                    rows = 128 if n < 14 else 64
                    move(vf[0:rows, n - 10, :], src[0:rows, :])
                else:
                    move(vb[:, n - 15:36:9, :], src[:, 0:260].rearrange("p (a n) -> p a n", a=4))

        @block.vector
        def _(v):
            v.wait_ge(s_w, 16 * 9)
            v.wait_ge(s_init, 5)
            nc.vector.tensor_scalar(nwk[:], wk[:], -1.0, None, ALU.mult).then_inc(s_z1, 1)
            nc.vector.tensor_scalar(wvb[:, :, S:S + 1], wvb[:, :, S:S + 1], -SCALE, None, ALU.mult).then_inc(s_z1, 1)
            with v.Fori(0, B) as b:
                nc.vector.tensor_copy(xs[:], xt[:, bass.ds(b, 1), :].rearrange("p a t -> p (a t)")).then_inc(s_xs, 1)

                def got(n):
                    v.wait_ge(s_fill, 24 * b + n + 1)
                    return score[:, n % 6, :]

                for n in range(2):
                    nc.vector.tensor_copy(xdup[:, 288 * n:288 * n + 288], got(n)[:, 0:288]).then_inc(s_fv, 1)
                v.wait_ge(s_fv, fills.per["v"] * b + 2)
                for h in range(2):
                    half = slice(64 * h, 64 * h + 64)
                    nc.vector.tensor_copy(xpar[half, :, h], xdup[half, :]).then_inc(s_xp, 1)
                v.wait_ge(s_z1, 36 * b + 2)
                for hp in range(4):
                    nc.vector.tensor_scalar(nk[:, T * hp:T * hp + T], xdup[:], nwk[:, hp:hp + 1], None, ALU.mult).then_inc(s_nk, 1)
                empty_fills("v", got)

                def produce(it, first):
                    for k, prev in tiles(b, it, first):
                        n = 36 * b + 3 * it + k
                        v.wait_ge(s_nks, n + 1)
                        for g in range(GROUPS):
                            if not (first and k == 0 and g < 4):
                                v.wait_ge(s_use, n * GROUPS + g - 3)
                            for j in range(4):
                                if by_vector[g][j]:
                                    u = 4 * g + j
                                    i = nc.vector.tensor_scalar(unit[:, u % RING, :], q[:, bass.ds(it // 3, 1), :].rearrange("p a t -> p (a t)"),
                                                                nks[:, k, 16 * j + g:16 * j + g + 1], 0.0, ALU.add, ALU.max)
                            i.then_inc(s_uv, 1)
                            if prev:
                                if g == 6:
                                    normalise(*prev)
                                if g == 10:
                                    last_chunk(*prev)

                def normalise(it, k):
                    n = 36 * b + 3 * it + k
                    v.wait_ge(s_e, n + 1)
                    nc.vector.tensor_scalar(z1[:, k:k + 1], z[:, k:k + 1], 1.0, None, ALU.add).then_inc(s_z1, 1)
                    v.wait_ge(s_z1, n + 3)
                    nc.vector.reciprocal(rz[:, k:k + 1], z1[:, k:k + 1]).then_inc(s_rz, 1)
                    v.wait_ge(s_rz, n + 1)
                    nc.vector.tensor_scalar(e[:, k, :], e[:, k, :], rz[:, k:k + 1], None, ALU.mult).then_inc(s_p, 1)

                def last_chunk(it, k):
                    n = 36 * b + 3 * it + k
                    v.wait_ge(s_t, n + 1)
                    nc.vector.tensor_copy(at[0:64, k, 4, :], score[0:64, 2 * k, 288:416]).then_inc(s_atv, 1)

                def finish(it, k):
                    normalise(it, k)
                    last_chunk(it, k)

                trips(v, b, produce, finish)
                v.wait_ge(s_kc, 36 * b + 36)
                nc.vector.tensor_tensor(oks[:], okf[:, 0:9, :], okf[:, 9:18, :], ALU.add).then_inc(s_add, 1)
                v.wait_ge(s_add, 3 * b + 1)
                nc.vector.tensor_tensor(oks[:], oks[:], okf[:, 18:27, :], ALU.add).then_inc(s_add, 1)
                v.wait_ge(s_add, 3 * b + 2)
                nc.vector.tensor_tensor(oks[:], oks[:], okf[:, 27:36, :], ALU.add).then_inc(s_add, 1)
                v.wait_ge(s_od, 32 * b + 32)

        @block.scalar
        def _(act):
            act.wait_ge(s_init, 5)
            with act.Fori(0, B) as b:
                def got(n):
                    act.wait_ge(s_fill, 24 * b + n + 1)
                    return score[:, n % 6, :]

                empty_fills("a", got)
                act.wait_ge(s_fv, (b + 1) * fills.per["v"])

                def produce(it, first):
                    for k, prev in tiles(b, it, first):
                        n = 36 * b + 3 * it + k
                        wait_apart(act, (s_w, 16 * 9), s_nks, n + 1)
                        for g in range(GROUPS):
                            if not (first and k == 0 and g < 4):
                                wait_apart(act, (s_w, 16 * 9), s_use, n * GROUPS + g - 3)
                            for j in range(4):
                                if not by_vector[g][j]:
                                    u = 4 * g + j
                                    i = nc.scalar.activation(unit[:, u % RING, :], q[:, bass.ds(it // 3, 1), :].rearrange("p a t -> p (a t)"), ACT.Relu,
                                                             bias=nks[:, k, 16 * j + g:16 * j + g + 1], scale=1.0)
                            i.then_inc(s_ua, 1)
                            if prev:
                                if g == 4:
                                    exp(*prev)
                                if g == 10:
                                    chunks(*prev)
                                if g == 14:
                                    key_out(*prev)

                def exp(it, k):
                    n = 36 * b + 3 * it + k
                    wait_apart(act, (s_w, 16 * 9), s_use, (n + 1) * GROUPS)
                    nc.scalar.activation(e[:, k, :].rearrange("p (a t) -> p a t", a=2), score[:, 2 * k:2 * k + 2, 0:288], ACT.Exp,
                                         bias=vb[:, bass.ds(3 * it + k, 1), S:S + 1].rearrange("p a n -> p (a n)"), scale=-SCALE,
                                         accum_out=z[:, k:k + 1]).then_inc(s_e, 1)

                def chunks(it, k):
                    n = 36 * b + 3 * it + k
                    act.wait_ge(s_t, n + 1)
                    nc.scalar.copy(at[:, k, 0:4, :].rearrange("p c r -> p (c r)"), turn[:]).then_inc(s_ata, 1)

                def key_out(it, k):
                    n = 36 * b + 3 * it + k
                    wait_apart(act, (s_w, 16 * 9), s_k, n + 1)
                    nc.scalar.copy(okf[:, bass.ds(3 * it + k, 1), :].rearrange("p a n -> p (a n)"), score[0:64, 2 * k + 1, 288:352]).then_inc(s_kc, 1)

                def finish(it, k):
                    exp(it, k)
                    chunks(it, k)
                    key_out(it, k)

                trips(act, b, produce, finish)
                nc.scalar.copy(o_query[:, bass.ds(5 * b, 4), :].rearrange("p c f -> p (c f)"), acc[:, 0:256]).then_inc(s_acc, 1)
                nc.scalar.copy(o_query[0:64, bass.ds(5 * b + 4, 1), :].rearrange("p c f -> p (c f)"), acc[0:64, 256:320]).then_inc(s_acc, 1)

        @block.tensor
        def _(pe):
            mm = nc.tensor.matmul
            pe.wait_ge(s_w, 16 * 9)
            pe.wait_ge(s_z1, 2)
            with pe.Fori(0, B) as b:
                def fill(n):
                    if n >= 6:
                        emptied(pe, b, n - 6)
                    return score[:, n % 6, :]

                pe.wait_ge(s_xs, b + 1)
                for n in range(2):
                    mm(fill(n)[:, 0:288], dup[:], xs[:, 288 * n:288 * n + 288], start=True, stop=True).then_inc(s_fill, 1)
                for n in range(2, 10):
                    hp, half = divmod(n - 2, 2)
                    mm(fill(n)[:, 0:288], wq[:, 128 * hp:128 * hp + 128], xs[:, 288 * half:288 * half + 288], start=True, stop=True).then_inc(s_fill, 1)
                for n in range(10, 15):
                    c = n - 10
                    rows = 128 if c < 4 else 64
                    mm(fill(n)[0:rows, :], xs[:, 128 * c:128 * c + rows], wvf[:], start=True, stop=True).then_inc(s_fill, 1)
                pe.wait_ge(s_xp, 2 * b + 2)
                for n in range(15, 24):
                    t0 = 64 * (n - 15)
                    out = fill(n)[:, 0:260]
                    mm(out, xpar[:, t0:t0 + 64, :].rearrange("p t h -> p (t h)"), wvb[:].rearrange("p a n -> p (a n)"), start=True, stop=False)
                    mm(out, par[:], bvb[:], start=False, stop=True).then_inc(s_fill, 1)
                for n in range(18, 24):
                    emptied(pe, b, n)

                def consume(it, first):
                    for k, prev in tiles(b, it, first):
                        n = 36 * b + 3 * it + k
                        if not first:
                            pe.wait_ge(s_kc, n - 2)
                        for half in range(2):
                            mm(score[:, 2 * k + half, 0:288], neg[:], q[:, bass.ds(it // 3, 1), 288 * half:288 * half + 288].rearrange("p a t -> p (a t)"),
                               start=True, stop=False, skip_group_check=True)
                        for g in range(GROUPS):
                            pe.wait_ge(s_uv, n * GROUPS + g + 1)
                            pe.wait_ge(s_ua, n * GROUPS + g + 1)
                            for j in range(4):
                                u = 4 * g + j
                                for half in range(2):
                                    i = mm(score[32 * j:32 * j + 32, 2 * k + half, 0:288], sel[:, 30 - 2 * g:62 - 2 * g],
                                           unit[:, u % RING, 288 * half:288 * half + 288], start=False, stop=(g == GROUPS - 1),
                                           tile_position=(0, 32 * j), skip_group_check=True)
                            i.then_inc(s_use, 1)
                            if prev:
                                if g == 7:
                                    value_sums(*prev, first and k == 1)
                                if g == 12:
                                    key_sums(*prev)

                def value_sums(it, k, fresh):
                    n = 36 * b + 3 * it + k
                    wait_apart(pe, (s_w, 16 * 9), s_p, n + 1)
                    for c in range(5):
                        rows = 128 if c < 4 else 64
                        mm(acc[0:rows, 64 * c:64 * c + 64], e[:, k, 128 * c:128 * c + rows],
                           vb[:, bass.ds(3 * it + k, 1), 0:S].rearrange("p a n -> p (a n)"), start=(fresh and c == 0), stop=False, skip_group_check=True)
                    for c in range(5):
                        rows = 128 if c < 4 else 64
                        out = turn[:, 128 * c:128 * c + 128] if c < 4 else score[0:64, 2 * k, 288:416]
                        i = nc.tensor.transpose(out, e[:, k, 128 * c:128 * c + rows], ident[:])
                    i.then_inc(s_t, 1)

                def key_sums(it, k):
                    n = 36 * b + 3 * it + k
                    wait_apart(pe, (s_w, 16 * 9), s_ata, n + 1)
                    wait_apart(pe, (s_w, 16 * 9), s_atv, n + 1)
                    for c in range(5):
                        for h in range(2):
                            i = mm(score[0:64, 2 * k + 1, 288:352], at[:, k, c, h:128:2],
                                   vf[:, c, bass.ds((it // 3) * 128 + 64 * h, 64)], start=(c == 0 and h == 0), stop=(c == 4 and h == 1), skip_group_check=True)
                    i.then_inc(s_k, 1)

                def finish(it, k):
                    value_sums(it, k, False)
                    key_sums(it, k)

                trips(pe, b, consume, finish)
                pe.wait_ge(s_acc, 2 * b + 2)
                pe.wait_ge(s_kc, 36 * b + 36)


def fanin_stage(nc, d, res, xn, o_query, o_key, ident):
    PARTS = 4
    W = ROWS // PARTS
    with ExitStack() as ctx:
        def sb(n, shape, dt=F32):
            return ctx.enter_context(nc.sbuf_tensor("fan_" + n, shape, dt))

        def sem(n):
            return ctx.enter_context(nc.semaphore("fan_" + n))

        w = sb("w", [65, S]); ex = sb("ex", [128, ROWS, S]); den = sb("den", [128, ROWS, S]); yt = sb("yt", [65, B, T])
        turned = ctx.enter_context(nc.psum_tensor("fan_turned", [128, 2, 1024], F32))
        out = ctx.enter_context(nc.psum_tensor("fan_out", [128, 2, 512], F32))
        s_w = sem("w"); s_one = sem("one"); s_o = sem("o"); s_e = sem("e"); s_d = sem("d"); s_r = sem("r"); s_y = sem("y")
        s_t = sem("t"); s_yt = sem("yt"); s_out = sem("out"); s_x = sem("x"); s_res = sem("res")
        block = ctx.enter_context(nc.Block())

        @block.sync
        def _(sp):
            sp.dma_start(w[:], d["l1_fan"]).then_inc(s_w, 16)

        @block.gpsimd
        def _(pool):
            nc.gpsimd.memset(yt[S:S + 1, :, :], 1.0).then_inc(s_one, 1)

        @block.vector
        def _(v):
            for p in range(PARTS):
                r = slice(W * p, W * p + W)
                nc.vector.tensor_tensor(o_query[:, r, :], o_query[:, r, :], o_key[:, r, :], ALU.add).then_inc(s_o, 1)
            for p in range(PARTS):
                r = slice(W * p, W * p + W)
                v.wait_ge(s_e, p + 1)
                nc.vector.tensor_scalar(den[:, r, :], ex[:, r, :], 1.0, None, ALU.add).then_inc(s_d, 1)
                v.wait_ge(s_d, p + 1)
                nc.vector.reciprocal(ex[:, r, :], den[:, r, :]).then_inc(s_r, 1)
                v.wait_ge(s_r, p + 1)
                nc.vector.tensor_tensor(o_query[:, r, :], o_query[:, r, :], ex[:, r, :], ALU.mult).then_inc(s_y, 1)
                nc.vector.tensor_tensor(res[:, r, :], res[:, r, :], xn[:, r, 0:S], ALU.add).then_inc(s_x, 1)
            v.wait_ge(s_x, PARTS)
            for b in range(B):
                v.wait_ge(s_out, b + 1)
                nc.vector.tensor_tensor(res[:, 5 * b:5 * b + 4, :], res[:, 5 * b:5 * b + 4, :],
                                        out[:, b % 2, 0:256].rearrange("p (c f) -> p c f", c=4), ALU.add).then_inc(s_res, 1)
                nc.vector.tensor_tensor(res[0:64, 5 * b + 4, :], res[0:64, 5 * b + 4, :], out[0:64, b % 2, 256:320], ALU.add).then_inc(s_res, 1)

        @block.scalar
        def _(act):
            for p in range(PARTS):
                r = slice(W * p, W * p + W)
                act.wait_ge(s_o, p + 1)
                nc.scalar.activation(ex[:, r, :], o_query[:, r, :], ACT.Exp, scale=-1.702).then_inc(s_e, 1)
            for b in range(B):
                act.wait_ge(s_t, b + 1)
                nc.scalar.copy(yt[0:S, b, :], turned[0:S, b % 2, 0:T]).then_inc(s_yt, 1)

        @block.tensor
        def _(pe):
            pe.wait_ge(s_w, 16)
            pe.wait_ge(s_one, 1)
            for b in range(B + 1):
                if b < B:
                    pe.wait_ge(s_y, b // 2 + 1)
                    if b >= 2:
                        pe.wait_ge(s_yt, b - 1)
                    for c in range(5):
                        n = min(128, T - 128 * c)
                        i = nc.tensor.transpose(turned[0:S, b % 2, 128 * c:128 * c + n], o_query[0:n, 5 * b + c, :], ident[0:n, 0:n])
                    i.then_inc(s_t, 1)
                if b >= 1:
                    pe.wait_ge(s_yt, b)
                    if b >= 3:
                        pe.wait_ge(s_res, 2 * (b - 2))
                    for c in range(5):
                        n = min(128, T - 128 * c)
                        i = nc.tensor.matmul(out[0:n, (b - 1) % 2, 64 * c:64 * c + 64], yt[:, b - 1, 128 * c:128 * c + n], w[:], start=True, stop=True)
                    i.then_inc(s_out, 1)


def store_tokens(nc, out, res):
    with ExitStack() as ctx:
        s_out = ctx.enter_context(nc.semaphore("result_stored"))
        r4 = res[:].rearrange("p (b c) f -> p b c f", b=B)
        block = ctx.enter_context(nc.Block())

        @block.sync
        def _(sp):
            for c in range(4):
                sp.dma_start(out[:, 128 * c:128 * c + 128, :].rearrange("b t f -> t b f"), r4[:, :, c, :]).then_inc(s_out, 16)
            sp.dma_start(out[:, 512:576, :].rearrange("b t f -> t b f"), r4[0:64, :, 4, :]).then_inc(s_out, 16)
            sp.wait_ge(s_out, 16 * 5)


def padded(a):
    a = np.asarray(a)
    return np.concatenate([a, np.zeros((128 - a.shape[0], a.shape[1]), a.dtype)])


def slice_layout(i):
    wx, bx = np.asarray(i["L0_ffn_W_x"]), np.asarray(i["L0_ffn_b_x"])
    wx1 = np.concatenate([wx, bx[None]])
    return {
        "s_wx_t": wx1.reshape(65, 8, S).transpose(2, 1, 0).reshape(S, 8 * 65),
        "s_slice": i["L0_ffn_W_slice"],
        "s_bslice": np.broadcast_to(np.asarray(i["L0_ffn_b_slice"]), (1, 8, S)).reshape(1, 512),
        "s_temp": np.broadcast_to(np.asarray(i["L0_ffn_temperature"]).reshape(1, 8), (65, 8)),
        "s_wfx": np.concatenate([np.asarray(i["L0_ffn_W_fx"]), np.asarray(i["L0_ffn_b_fx"])[None]]),
        "s_wq": padded(i["L0_ffn_W_q"]), "s_wk": padded(i["L0_ffn_W_k"]),
        "s_wv_t": np.asarray(i["L0_ffn_W_v"]).T,
        "s_wout": np.asarray(i["L0_ffn_W_out"]).reshape(8, S, S).transpose(1, 0, 2).reshape(S, 512),
        "s_bout": np.broadcast_to(np.asarray(i["L0_ffn_b_out"]), (128, S)),
    }


def slice_stage(nc, d, res, xn, xt, ident):
    NAMES = ["logit"] * 5 + ["turn_w"] * 5 + ["pool", "turn_p", "token", "q", "k", "vo", "score", "turn_a", "ow", "out"]
    OWNERS = ["v"] * 5 + ["a"] * 5 + ["v", "a", "v", "a", "v", "a", "v", "a", "v", "v"]
    ring = BankRing(OWNERS, 5)
    FIRST = {n: NAMES.index(n) for n in NAMES}
    NF = len(NAMES)
    with ExitStack() as ctx:
        def sb(n, shape, dt=F32):
            return ctx.enter_context(nc.sbuf_tensor("sl_" + n, shape, dt))

        def sem(n):
            return ctx.enter_context(nc.semaphore("sl_" + n))

        wx_t = sb("wx_t", [S, 8 * 65]); wslice = sb("wslice", [S, S]); bslice = sb("bslice", [65, 512]); temp = sb("temp", [65, 8])
        wfx = sb("wfx", [65, 512]); wq = sb("wq", [128, S]); wk = sb("wk", [128, S]); wv_t = sb("wv_t", [S, S]); wout = sb("wout", [S, 512])
        bout = sb("bout", [128, S]); rtemp = sb("rtemp", [65, 8]); wxs = sb("wxs", [128, 512]); wvo = sb("wvo", [S, 512])
        xs = sb("xs", [128, T]); mx = sb("mx", [128, 5, 8]); w = sb("w", [128, 5, 512]); sm = sb("sm", [128, 5, 8]); rs = sb("rs", [128, 5, 8])
        wt = sb("wt", [128, 4, T])
        nrm = sb("nrm", [128, 4]); rn = sb("rn", [128, 4]); pooled = sb("pooled", [128, 4, 65]); pt = sb("pt", [65, 512])
        tok = sb("tok", [128, 512]); qt = sb("qt", [S, 512]); kt = sb("kt", [S, 512]); vo = sb("vo", [S, 512])
        amx = sb("amx", [S, 8]); att = sb("att", [S, 512]); asm = sb("asm", [S, 8]); ars = sb("ars", [S, 8]); att_t = sb("att_t", [S, 512])
        ow = sb("ow", [128, 256])
        bank = ctx.enter_context(nc.psum_tensor("sl_bank", [128, 5, 512], F32))

        s_w = sem("weights"); s_zero = sem("padding"); s_pre = sem("pre_pe"); s_pv = sem("pre_v"); s_xs = sem("xs"); s_full = sem("full")
        s_ev = sem("emptied_v"); s_ea = sem("emptied_a"); s_mx = sem("max"); s_exp = sem("exp"); s_sum = sem("sum"); s_rs = sem("rsum")
        s_prob = sem("slice_weights"); s_nrm = sem("norm"); s_amx = sem("att_max"); s_cen = sem("att_centred"); s_aexp = sem("att_exp")
        s_asum = sem("att_sum"); s_att = sem("att"); s_res = sem("res")
        emptied_sem = {"v": s_ev, "a": s_ea}

        NW = 16 * (9 + 1)

        def emptied(eng, b, *fills):
            for who, count in ring.latest(fills):
                wait_apart(eng, (s_w, NW), emptied_sem[who], b * ring.per[who] + count)

        block = ctx.enter_context(nc.Block())
        loads = [(wx_t, "s_wx_t"), (wslice, "s_slice"), (temp, "s_temp"), (wfx, "s_wfx"), (wq, "s_wq"), (wk, "s_wk"), (wv_t, "s_wv_t"),
                 (wout, "s_wout"), (bout, "s_bout")]

        @block.sync
        def _(sp):
            for t, name in loads:
                sp.dma_start(t[:], d[name]).then_inc(s_w, 16)
            sp.dma_start(bslice[S:S + 1, :], d["s_bslice"]).then_inc(s_w, 16)

        @block.gpsimd
        def _(pool):
            nc.gpsimd.memset(wxs[S:128, :], 0.0).then_inc(s_zero, 1)
            pool.wait_ge(s_zero, 1)
            nc.gpsimd.memset(tok[S:128, :], 0.0).then_inc(s_zero, 1)

        @block.vector
        def _(v):
            v.wait_ge(s_w, NW)
            v.wait_ge(s_zero, 2)
            nc.vector.tensor_scalar(temp[:], temp[:], 0.1, 5.0, ALU.max, ALU.min).then_inc(s_pv, 1)
            v.wait_ge(s_pv, 1)
            nc.vector.reciprocal(rtemp[:], temp[:]).then_inc(s_pv, 1)
            v.wait_ge(s_pre, 1)
            nc.vector.tensor_copy(wxs[0:65, :], bank[0:65, 0, :]).then_inc(s_pv, 1)
            v.wait_ge(s_pv, 3)
            nc.vector.tensor_tensor(wxs[S:S + 1, :], wxs[S:S + 1, :], bslice[S:S + 1, :], ALU.add).then_inc(s_pv, 1)
            v.wait_ge(s_pv, 4)
            w3 = wxs[0:65, :].rearrange("p (h g) -> p h g", h=8)
            nc.vector.tensor_tensor(w3, w3, rtemp[:, :, None].broadcast_to([65, 8, S]), ALU.mult).then_inc(s_pv, 1)
            v.wait_ge(s_pre, 2)
            nc.vector.tensor_copy(wvo[:], bank[0:S, 1, :]).then_inc(s_pv, 1)
            nc.vector.tensor_tensor(res[:], res[:], bout[:, None, :].broadcast_to([128, ROWS, S]), ALU.add).then_inc(s_pv, 1)
            v.wait_ge(s_pv, 7)
            with v.Fori(0, B) as b:
                nc.vector.tensor_copy(xs[:], xt[:, bass.ds(b, 1), :].rearrange("p a t -> p (a t)")).then_inc(s_xs, 1)

                def got(name, k=0):
                    n = FIRST[name] + k
                    v.wait_ge(s_full, NF * b + n + 1)
                    return bank[:, n % ring.size, :]

                def heads(ap):
                    return ap.rearrange("p (h g) -> p h g", h=8)

                for c in range(5):
                    rows = 128 if c < 4 else 64
                    src = heads(got("logit", c)[0:rows, :])
                    nc.vector.tensor_reduce(mx[0:rows, c, :], src, AX, ALU.max).then_inc(s_mx, 1)
                    v.wait_ge(s_mx, 5 * b + c + 1)
                    nc.vector.tensor_tensor(heads(w[0:rows, c, :]), src, mx[0:rows, c, :, None].broadcast_to([rows, 8, S]), ALU.subtract).then_inc(s_ev, 1)
                for c in range(5):
                    rows = 128 if c < 4 else 64
                    v.wait_ge(s_exp, 5 * b + c + 1)
                    nc.vector.tensor_reduce(sm[0:rows, c, :], heads(w[0:rows, c, :]), AX, ALU.add).then_inc(s_sum, 1)
                    v.wait_ge(s_sum, 5 * b + c + 1)
                    nc.vector.reciprocal(rs[0:rows, c, :], sm[0:rows, c, :]).then_inc(s_rs, 1)
                    v.wait_ge(s_rs, 5 * b + c + 1)
                    nc.vector.tensor_tensor(heads(w[0:rows, c, :]), heads(w[0:rows, c, :]), rs[0:rows, c, :, None].broadcast_to([rows, 8, S]),
                                            ALU.mult).then_inc(s_prob, 1)
                src = got("pool")[:, 0:260].rearrange("p (a n) -> p a n", a=4)
                nc.vector.tensor_scalar(nrm[:], src[:, :, S], 1e-5, None, ALU.add).then_inc(s_nrm, 1)
                v.wait_ge(s_nrm, 2 * b + 1)
                nc.vector.reciprocal(rn[:], nrm[:]).then_inc(s_nrm, 1)
                v.wait_ge(s_nrm, 2 * b + 2)
                nc.vector.tensor_tensor(pooled[:], src, rn[:, :, None].broadcast_to([128, 4, 65]), ALU.mult).then_inc(s_ev, 1)
                nc.vector.tensor_copy(tok[0:S, :], got("token")[0:S, :]).then_inc(s_ev, 1)
                nc.vector.tensor_copy(kt[:], got("k")[0:S, :]).then_inc(s_ev, 1)
                src = heads(got("score")[0:S, :])
                nc.vector.tensor_reduce(amx[:], src, AX, ALU.max).then_inc(s_amx, 1)
                v.wait_ge(s_amx, b + 1)
                nc.vector.tensor_tensor(heads(att[:]), src, amx[:, :, None].broadcast_to([S, 8, S]), ALU.subtract).then_inc(s_ev, 1)
                v.wait_ge(s_aexp, b + 1)
                nc.vector.tensor_reduce(asm[:], heads(att[:]), AX, ALU.add).then_inc(s_asum, 1)
                v.wait_ge(s_asum, 2 * b + 1)
                nc.vector.reciprocal(ars[:], asm[:]).then_inc(s_asum, 1)
                v.wait_ge(s_asum, 2 * b + 2)
                nc.vector.tensor_tensor(heads(att[:]), heads(att[:]), ars[:, :, None].broadcast_to([S, 8, S]), ALU.mult).then_inc(s_att, 1)
                nc.vector.tensor_copy(ow[:], got("ow")[:, 0:256]).then_inc(s_ev, 1)
                src = got("out")
                r = res[:, bass.ds(5 * b, 4), :]
                nc.vector.tensor_tensor(r, r, src[:, 0:256].rearrange("p (c f) -> p c f", c=4), ALU.add).then_inc(s_res, 1)
                r = res[0:64, bass.ds(5 * b + 4, 1), :].rearrange("p c f -> p (c f)")
                nc.vector.tensor_tensor(r, r, src[0:64, 256:320], ALU.add).then_inc(s_ev, 1)

        @block.scalar
        def _(act):
            with act.Fori(0, B) as b:
                def got(name, k=0):
                    n = FIRST[name] + k
                    act.wait_ge(s_full, NF * b + n + 1)
                    return bank[:, n % ring.size, :]

                for c in range(5):
                    rows = 128 if c < 4 else 64
                    act.wait_ge(s_ev, ring.per["v"] * b + c + 1)
                    nc.scalar.activation(w[0:rows, c, :], w[0:rows, c, :], ACT.Exp).then_inc(s_exp, 1)
                for c in range(5):
                    rows = 128 if c < 4 else 64
                    nc.scalar.copy(wt[:, :, 128 * c:128 * c + rows], got("turn_w", c).rearrange("p (a r) -> p a r", a=4)[:, :, 0:rows]).then_inc(s_ea, 1)
                nc.scalar.copy(pt[:], got("turn_p")[0:65, :]).then_inc(s_ea, 1)
                nc.scalar.copy(qt[:], got("q")[0:S, :]).then_inc(s_ea, 1)
                nc.scalar.copy(vo[:], got("vo")[0:S, :]).then_inc(s_ea, 1)
                who, count = ring.emptied(FIRST["score"])
                act.wait_ge(s_ev, ring.per["v"] * b + count)
                nc.scalar.activation(att[:], att[:], ACT.Exp, scale=1.0 / 8.0).then_inc(s_aexp, 1)
                nc.scalar.copy(att_t[:], got("turn_a")[0:S, :]).then_inc(s_ea, 1)

        @block.tensor
        def _(pe):
            mm, turn = nc.tensor.matmul, nc.tensor.transpose
            pe.wait_ge(s_w, NW)
            for h in range(8):
                i = mm(bank[0:65, 0, 64 * h:64 * h + 64], wx_t[:, 65 * h:65 * h + 65], wslice[:], start=True, stop=True)
            i.then_inc(s_pre, 1)
            mm(bank[0:S, 1, :], wv_t[:], wout[:], start=True, stop=True).then_inc(s_pre, 1)
            pe.wait_ge(s_pv, 7)
            with pe.Fori(0, B) as b:
                def fill(name, k=0, reads=()):
                    n = FIRST[name] + k
                    emptied(pe, b, *[FIRST[r] for r in reads], *([n - ring.size] if n >= ring.size else []))
                    return bank[:, n % ring.size, :]

                wait_apart(pe, (s_w, NW), s_xs, b + 1)
                for c in range(5):
                    rows = 128 if c < 4 else 64
                    mm(fill("logit", c)[0:rows, :], xs[:, 128 * c:128 * c + rows], wxs[:], start=True, stop=True).then_inc(s_full, 1)
                for c in range(5):
                    rows = 128 if c < 4 else 64
                    wait_apart(pe, (s_w, NW), s_prob, 5 * b + c + 1)
                    out = fill("turn_w", c)
                    for hp in range(4):
                        i = turn(out[:, 128 * hp:128 * hp + rows], w[0:rows, c, 128 * hp:128 * hp + 128], ident[0:rows, 0:rows])
                    i.then_inc(s_full, 1)
                out = fill("pool")
                for hp in range(4):
                    for c in range(5):
                        rows = 128 if c < 4 else 64
                        i = mm(out[:, 65 * hp:65 * hp + 65], w[0:rows, c, 128 * hp:128 * hp + 128],
                               xn[0:rows, bass.ds(5 * b + c, 1), :].rearrange("p a n -> p (a n)"), start=(c == 0), stop=(c == 4))
                i.then_inc(s_full, 1)
                out = fill("turn_p", reads=["pool"])
                for hp in range(4):
                    i = turn(out[0:65, 128 * hp:128 * hp + 128], pooled[:, hp, :], ident[:])
                i.then_inc(s_full, 1)
                out = fill("token", reads=["turn_p"])
                for h in range(8):
                    i = mm(out[0:S, 64 * h:64 * h + 64], wfx[:, 64 * h:64 * h + 64], pt[:, 64 * h:64 * h + 64], start=True, stop=True)
                i.then_inc(s_full, 1)
                mm(fill("q", reads=["token"])[0:S, :], wq[:], tok[:], start=True, stop=True).then_inc(s_full, 1)
                mm(fill("k")[0:S, :], wk[:], tok[:], start=True, stop=True).then_inc(s_full, 1)
                out = fill("vo")
                for h in range(8):
                    i = mm(out[0:S, 64 * h:64 * h + 64], tok[0:S, 64 * h:64 * h + 64], wvo[:, 64 * h:64 * h + 64], start=True, stop=True)
                i.then_inc(s_full, 1)
                out = fill("score", reads=["q", "k"])
                for h in range(8):
                    i = mm(out[0:S, 64 * h:64 * h + 64], qt[:, 64 * h:64 * h + 64], kt[:, 64 * h:64 * h + 64], start=True, stop=True)
                i.then_inc(s_full, 1)
                wait_apart(pe, (s_w, NW), s_att, b + 1)
                out = fill("turn_a")
                for h in range(8):
                    i = turn(out[0:S, 64 * h:64 * h + 64], att[:, 64 * h:64 * h + 64], ident[0:S, 0:S])
                i.then_inc(s_full, 1)
                out = fill("ow", reads=["turn_a", "vo"])
                for h in range(8):
                    p0 = 64 * (h % 2)
                    i = mm(out[p0:p0 + 64, 64 * (h // 2):64 * (h // 2) + 64], att_t[:, 64 * h:64 * h + 64], vo[:, 64 * h:64 * h + 64],
                           start=True, stop=True, tile_position=(0, p0))
                i.then_inc(s_full, 1)
                out = fill("out", reads=["ow"])
                for c in range(5):
                    rows = 128 if c < 4 else 64
                    for hp in range(4):
                        i = mm(out[0:rows, 64 * c:64 * c + 64], wt[:, hp, 128 * c:128 * c + rows], ow[:, 64 * hp:64 * hp + 64],
                               start=(hp == 0), stop=(hp == 3))
                i.then_inc(s_full, 1)


def mqa_layout(i):
    wv = np.asarray(i["L1_attn_Wv"]).T
    return {"m_wq": padded(np.asarray(i["L1_attn_Wq"]).T), "m_wk": padded(np.asarray(i["L1_attn_Wk"]).T),
            "m_wv": padded(np.concatenate([wv, wv], 1)),
            "m_wo": np.asarray(i["L1_attn_Wo"]).T.reshape(4, 128, S).transpose(1, 0, 2).reshape(128, 256)}


def mqa_stage(nc, d, xt, ctx_dram, ident):
    SCALE = 1.0 / np.sqrt(8.0)
    UNITS = 40
    OWNERS = ["v", "v"] + ["a", "v", "a", "v"] + ["a"] * UNITS
    K, V, Q, SCORE = 0, 1, 2, 6
    ring = BankRing(OWNERS, 2)
    NF = len(OWNERS)
    TURN_LAG, CTX_LAG, NORM_LAG = 2, 3, 4
    with ExitStack() as ctx:
        def sb(n, shape, dt=F32):
            return ctx.enter_context(nc.sbuf_tensor("mq_" + n, shape, dt))

        def sem(n):
            return ctx.enter_context(nc.semaphore("mq_" + n))

        wq = sb("wq", [128, 512]); wk = sb("wk", [128, S]); wv = sb("wv", [128, 128])
        keys = sb("keys", [128, 9, S]); q = sb("q", [128, 8, T]); vals = sb("vals", [128, 5, S])
        mx = sb("mx", [128, UNITS]); nmx = sb("nmx", [128, UNITS]); z = sb("z", [128, UNITS]); rz = sb("rz", [128, UNITS])
        p = sb("p", [128, 3, T]); pt = sb("pt", [128, 2, 5, 128]); c_out = sb("c_out", [128, 5, 512])
        wide = ctx.enter_context(nc.psum_tensor("mq_wide", [128, 2, 2, 512], F32))
        turned = ctx.enter_context(nc.psum_tensor("mq_turned", [128, 2, 512], F32))
        cx = ctx.enter_context(nc.psum_tensor("mq_cx", [128, 2, 512], F32))
        s_w = sem("weights"); s_init = sem("init"); s_full = sem("full"); s_ev = sem("emptied_v"); s_ea = sem("emptied_a")
        s_part = sem("part_v"); s_qp = sem("q_part_a"); s_mx = sem("max"); s_nmx = sem("minus_max"); s_turn = sem("probs_turned")
        s_pa = sem("pt_a"); s_pv = sem("pt_v"); s_cx = sem("context"); s_rz = sem("rz"); s_cn = sem("context_normed")
        s_store = sem("context_stored")
        emptied_sem = {"v": s_ev, "a": s_ea}

        def emptied(eng, b, *fills):
            for who, count in ring.latest(fills):
                wait_apart(eng, (s_w, 48), emptied_sem[who], b * ring.per[who] + count)

        def rows_of(c):
            return 128 if c < 4 else 64

        block = ctx.enter_context(nc.Block())

        @block.sync
        def _(sp):
            for t, name in ((wq, "m_wq"), (wk, "m_wk"), (wv, "m_wv")):
                sp.dma_start(t[:], d[name]).then_inc(s_w, 16)
            with sp.Fori(0, B) as b:
                sp.wait_ge(s_cn, 8 * b + 8)
                sp.dma_start(ctx_dram[bass.ds(b, 1), 0:512, :].rearrange("a (c p) n -> p (a c) n", p=128), c_out[:, 0:4, :]).then_inc(s_store, 16)
                sp.dma_start(ctx_dram[bass.ds(b, 1), 512:576, :].rearrange("a p n -> p (a n)"), c_out[0:64, 4, :]).then_inc(s_store, 16)
            sp.wait_ge(s_store, 32 * B + 16)

        @block.gpsimd
        def _(pool):
            for n, t in enumerate((keys[S:128, :, :], q[S:128, :, :])):
                if n:
                    pool.wait_ge(s_init, n)
                nc.gpsimd.memset(t, 0.0).then_inc(s_init, 1)
            pool.wait_ge(s_init, 2)
            nc.gpsimd.memset(z[:], 1.0).then_inc(s_init, 1)
            pool.wait_ge(s_init, 3)
            nc.gpsimd.memset(c_out[:, 0, 0:1], 0.0).then_inc(s_store, 16)

        @block.vector
        def _(v):
            v.wait_ge(s_init, 3)
            with v.Fori(0, B) as b:
                def got(n):
                    v.wait_ge(s_full, NF * b + n + 1)
                    return wide[:, n % 2, :, :]

                k4 = keys[0:S, :, :].rearrange("p j (a o) -> p a j o", a=2)
                src = got(K)
                nc.vector.tensor_copy(k4[:, 0], src[0:S, 0, 0:288].rearrange("p (o j) -> p j o", j=9)).then_inc(s_part, 1)
                nc.vector.tensor_copy(k4[:, 1], src[0:S, 1, 0:288].rearrange("p (o j) -> p j o", j=9)).then_inc(s_ev, 1)
                src = got(V)
                a = src[:, 0, 0:320].rearrange("p (j f) -> p j f", j=5)
                c = src[:, 1, 0:256].rearrange("p (j f) -> p j f", j=4)
                nc.vector.tensor_copy(vals[0:64, 0:3, :], a[0:64, 0:5:2, :]).then_inc(s_part, 1)
                nc.vector.tensor_copy(vals[64:128, 0:2, :], a[64:128, 1:5:2, :]).then_inc(s_part, 1)
                nc.vector.tensor_copy(vals[0:64, 3:5, :], c[0:64, 1:4:2, :]).then_inc(s_part, 1)
                nc.vector.tensor_copy(vals[64:128, 2:4, :], c[64:128, 0:4:2, :]).then_inc(s_ev, 1)
                for hp in (1, 3):
                    src = got(Q + hp)
                    q3 = q[0:S, 2 * hp:2 * hp + 2, :].rearrange("p h (a t) -> p h a t", a=2)
                    nc.vector.tensor_copy(q3[:, 0], src[0:64, :, 0:288]).then_inc(s_part, 1)
                    nc.vector.tensor_copy(q3[:, 1], src[64:128, :, 0:288]).then_inc(s_ev, 1)

                for n in range(UNITS + NORM_LAG):
                    if n < UNITS:
                        r = rows_of(n % 5)
                        nc.vector.tensor_reduce(mx[0:r, n:n + 1], got(SCORE + n)[0:r, :, 0:288], mybir.AxisListType.XY, ALU.max).then_inc(s_mx, 1)
                        v.wait_ge(s_mx, UNITS * b + n + 1)
                        nc.vector.tensor_scalar(nmx[0:r, n:n + 1], mx[0:r, n:n + 1], -float(SCALE), None, ALU.mult).then_inc(s_nmx, 1)
                    m = n - TURN_LAG
                    if 0 <= m < UNITS:
                        r = rows_of(m % 5)
                        v.wait_ge(s_turn, UNITS * b + m + 1)
                        nc.vector.tensor_copy(pt[0:64, m % 2, 4, 0:r], turned[0:64, 1, 0:r]).then_inc(s_pv, 1)
                    h, c = divmod(n - NORM_LAG, 5)
                    if h >= 0 and c == 4:
                        if h == 0:
                            v.wait_ge(s_store, 32 * b + 16)
                        v.wait_ge(s_cx, UNITS * b + 5 * h + 5)
                        nc.vector.reciprocal(rz[:, 5 * h:5 * h + 5], z[:, 5 * h:5 * h + 5]).then_inc(s_rz, 1)
                        v.wait_ge(s_rz, 16 * b + 2 * h + 1)
                        src = cx[:, h % 2, 0:320].rearrange("p (c n) -> p c n", c=5)
                        nc.vector.tensor_tensor(c_out[:, 0:4, 64 * h:64 * h + 64], src[:, 0:4, :], rz[:, 5 * h:5 * h + 4, None].broadcast_to([128, 4, S]), ALU.mult).then_inc(s_rz, 1)
                        nc.vector.tensor_scalar(c_out[0:64, 4, 64 * h:64 * h + 64], src[0:64, 4, :], rz[0:64, 5 * h + 4:5 * h + 5], None, ALU.mult).then_inc(s_cn, 1)

        @block.scalar
        def _(act):
            act.wait_ge(s_init, 3)
            with act.Fori(0, B) as b:
                def got(n):
                    act.wait_ge(s_full, NF * b + n + 1)
                    return wide[:, n % 2, :, :]

                for hp in (0, 2):
                    src = got(Q + hp)
                    q3 = q[0:S, 2 * hp:2 * hp + 2, :].rearrange("p h (a t) -> p h a t", a=2)
                    nc.scalar.copy(q3[:, 0], src[0:64, :, 0:288]).then_inc(s_qp, 1)
                    nc.scalar.copy(q3[:, 1], src[64:128, :, 0:288]).then_inc(s_ea, 1)
                for n in range(UNITS + TURN_LAG):
                    if n < UNITS:
                        r = rows_of(n % 5)
                        if n >= 3:
                            wait_apart(act, (s_w, 48), s_turn, UNITS * b + n - 2)
                        act.wait_ge(s_nmx, UNITS * b + n + 1)
                        nc.scalar.activation(p[0:r, n % 3, :].rearrange("p (a t) -> p a t", a=2), wide[0:r, (SCORE + n) % 2, :, 0:288], ACT.Exp,
                                             bias=nmx[0:r, n:n + 1], scale=float(SCALE), accum_out=z[0:r, n:n + 1]).then_inc(s_ea, 1)
                    m = n - TURN_LAG
                    if m >= 0:
                        r = rows_of(m % 5)
                        if m >= 2:
                            wait_apart(act, (s_w, 48), s_cx, UNITS * b + m - 1)
                        act.wait_ge(s_turn, UNITS * b + m + 1)
                        nc.scalar.copy(pt[:, m % 2, 0:4, 0:r], turned[:, 0, :].rearrange("p (j s) -> p j s", j=4)[:, :, 0:r]).then_inc(s_pa, 1)

        @block.tensor
        def _(pe):
            mm = nc.tensor.matmul
            pe.wait_ge(s_w, 48)
            pe.wait_ge(s_init, 3)
            with pe.Fori(0, B) as b:
                def fill(n, reads=()):
                    emptied(pe, b, *reads, *([n - 2] if n >= 2 else []))
                    return wide[:, n % 2, :, :]

                def halves(out, lhs, rhs, cut=288):
                    mm(out[:, 0, 0:cut], lhs, rhs(0, cut), start=True, stop=True)
                    mm(out[:, 1, 0:T - cut], lhs, rhs(cut, T), start=True, stop=True).then_inc(s_full, 1)

                def x(t0, t1):
                    return xt[:, bass.ds(b, 1), t0:t1].rearrange("p a t -> p (a t)")

                halves(fill(K)[0:S], wk[:], x)
                halves(fill(V), wv[:], x, cut=320)
                for hp in range(4):
                    halves(fill(Q + hp), wq[:, 128 * hp:128 * hp + 128], x)
                flat = keys[:].rearrange("p j o -> p (j o)")
                for n in range(UNITS + CTX_LAG):
                    if n < UNITS:
                        h, c = divmod(n, 5)
                        reads = ([K] if n == 0 else []) + ([Q + h // 2] if c == 0 and h % 2 == 0 else [])
                        halves(fill(SCORE + n, reads)[0:rows_of(c)], q[:, h, 128 * c:128 * c + rows_of(c)], lambda t0, t1: flat[:, t0:t1])
                    m = n - TURN_LAG
                    if 0 <= m < UNITS:
                        r = rows_of(m % 5)
                        emptied(pe, b, SCORE + m)
                        if m >= 1:
                            wait_apart(pe, (s_w, 48), s_pa, UNITS * b + m)
                            wait_apart(pe, (s_w, 48), s_pv, UNITS * b + m)
                        for j in range(4):
                            nc.tensor.transpose(turned[:, 0, 128 * j:128 * j + r], p[0:r, m % 3, 128 * j:128 * j + 128], ident[0:r, 0:r])
                        nc.tensor.transpose(turned[0:64, 1, 0:r], p[0:r, m % 3, 512:576], ident[0:r, 0:r]).then_inc(s_turn, 1)
                    m = n - CTX_LAG
                    if m >= 0:
                        h, c = divmod(m, 5)
                        wait_apart(pe, (s_w, 48), s_pa, UNITS * b + m + 1)
                        wait_apart(pe, (s_w, 48), s_pv, UNITS * b + m + 1)
                        if c == 0 and h >= 2:
                            wait_apart(pe, (s_w, 48), s_cn, 8 * b + h - 1)
                        for j in range(5):
                            keys_n = rows_of(j)
                            i = mm(cx[0:rows_of(c), h % 2, 64 * c:64 * c + 64], pt[0:keys_n, m % 2, j, 0:rows_of(c)], vals[0:keys_n, j, :],
                                   start=(j == 0), stop=(j == 4))
                        i.then_inc(s_cx, 1)


def mqa_out_stage(nc, d, ctx_dram, res):
    with ExitStack() as ctx:
        def sem(n):
            return ctx.enter_context(nc.semaphore("mo_" + n))

        wo = ctx.enter_context(nc.sbuf_tensor("mo_wo", [128, 256], F32))
        cr = ctx.enter_context(nc.sbuf_tensor("mo_cr", [128, 2, 4, T], F32))
        out = ctx.enter_context(nc.psum_tensor("mo_out", [128, 2, 512], F32))
        s_w = sem("weights"); s_c = [sem("context0"), sem("context1")]; s_out = sem("out"); s_res = sem("res")
        view = ctx_dram.rearrange("b s n -> b (s n)").rearrange("b (i p t) -> b p i t", p=128, t=T)
        block = ctx.enter_context(nc.Block())

        @block.sync
        def _(sp):
            sp.dma_start(wo[:], d["m_wo"]).then_inc(s_w, 16)
            for k in range(2):
                sp.dma_start(cr[:, k], view[k]).then_inc(s_c[k], 16)
            with sp.Fori(1, B // 2) as n:
                for k in range(2):
                    sp.wait_ge(s_out, 2 * n + k - 1)
                    sp.dma_start(cr[:, k], view[bass.ds(2 * n + k, 1)].rearrange("a p i t -> p (a i) t")).then_inc(s_c[k], 16)

        @block.vector
        def _(v):
            with v.Fori(0, B // 2) as n:
                for k in range(2):
                    v.wait_ge(s_out, 2 * n + k + 1)
                    r = res[:, bass.ds(10 * n + 5 * k, 4), :]
                    nc.vector.tensor_tensor(r, r, out[:, k, 0:256].rearrange("p (c f) -> p c f", c=4), ALU.add).then_inc(s_res, 1)
                    r = res[0:64, bass.ds(10 * n + 5 * k + 4, 1), :].rearrange("p c f -> p (c f)")
                    nc.vector.tensor_tensor(r, r, out[0:64, k, 256:320], ALU.add).then_inc(s_res, 1)

        @block.tensor
        def _(pe):
            pe.wait_ge(s_w, 16)

            def pair(n, first):
                for k in range(2):
                    pe.wait_ge(s_c[k], 16 * (n + 1))
                    if not first:
                        pe.wait_ge(s_res, 4 * n + 2 * k - 2)
                    for c in range(5):
                        rows = 128 if c < 4 else 64
                        for i4 in range(4):
                            i = nc.tensor.matmul(out[0:rows, k, 64 * c:64 * c + 64], cr[:, k, i4, 128 * c:128 * c + rows],
                                                 wo[:, 64 * i4:64 * i4 + 64], start=(i4 == 0), stop=(i4 == 3))
                    i.then_inc(s_out, 1)

            pair(0, True)
            with pe.Fori(1, B // 2) as n:
                pair(n, False)


def moe_layout(i):
    a = {"e_sw1": padded(i["L1_ffn_sW1"]), "e_sw2": padded(i["L1_ffn_sW2"]), "e_sw3": i["L1_ffn_sW3"]}
    a["e_sb1"] = np.asarray(i["L1_ffn_sb1"])[:, None]
    a["e_sb2"] = np.asarray(i["L1_ffn_sb2"])[:, None]
    a["e_sb3"] = np.broadcast_to(np.asarray(i["L1_ffn_sb3"]), (128, S))
    a["e_w1"] = padded(np.asarray(i["L1_ffn_eW1"]).transpose(1, 0, 2).reshape(S, 512))
    a["e_b1"] = np.asarray(i["L1_ffn_eb1"]).T
    a["e_w2"] = np.asarray(i["L1_ffn_eW2"]).transpose(1, 0, 2).reshape(128, 256)
    a["e_b2"] = np.asarray(i["L1_ffn_eb2"]).T
    w3 = np.concatenate([np.asarray(i["L1_ffn_eW3"]), np.asarray(i["L1_ffn_eb3"])[:, None]], 1)
    a["e_w3"] = padded(w3.transpose(1, 0, 2).reshape(65, 256))
    a["e_gate"] = padded(np.concatenate([np.asarray(i["L1_ffn_gW"]), np.asarray(i["L1_ffn_gb"])[None]]))
    return a


def moe_constants():
    return {"c_before": np.broadcast_to(np.tril(np.ones((4, 4)), -1).reshape(1, 16), (128, 16)).astype(np.float32)}


def moe_stage(nc, d, res, xt):
    NAMES = ["shared1", "e1_0", "shared2", "e1_1", "e2_0", "e1_2", "e2_1", "e1_3", "e2_2", "e2_3"] + [f"out{c}" for c in range(5)]
    OWNERS = ["a" if n.startswith("e1") or n == "shared1" else "v" for n in NAMES]
    FILL = {name: n for n, name in enumerate(NAMES)}
    ring = BankRing(OWNERS, 3)
    NF = len(OWNERS)
    assert NF % ring.size == 0
    with ExitStack() as ctx:
        def sb(n, shape, dt=F32):
            return ctx.enter_context(nc.sbuf_tensor("me_" + n, shape, dt))

        def sem(n):
            return ctx.enter_context(nc.semaphore("me_" + n))

        sw1 = sb("sw1", [128, S]); sw2 = sb("sw2", [128, 128]); sw3 = sb("sw3", [128, S]); sb1 = sb("sb1", [S, 1]); sb2 = sb("sb2", [128, 1])
        sb3 = sb("sb3", [128, S]); w1 = sb("w1", [128, 512]); b1 = sb("b1", [128, 4]); w2 = sb("w2", [128, 256]); b2 = sb("b2", [S, 4])
        w3 = sb("w3", [128, 256]); gate = sb("gate", [128, 4]); before = sb("before", [128, 4, 4])
        h1 = sb("h1", [128, T]); h2 = sb("h2", [128, T]); g1 = sb("g1", [128, 2, T]); g2 = sb("g2", [128, 4, T])
        gl = sb("gl", [128, ROWS, 4]); gm = sb("gm", [128, ROWS]); gc = sb("gc", [128, ROWS, 4]); ge = sb("ge", [128, ROWS, 4])
        gs = sb("gs", [128, ROWS]); gr = sb("gr", [128, ROWS]); gp = sb("gp", [128, ROWS, 4])
        eq = sb("eq", [128, ROWS, 4, 4]); gt = sb("gt", [128, ROWS, 4, 4])
        rank = sb("rank", [128, ROWS, 4]); top = sb("top", [128, ROWS, 4]); tm = sb("tm", [128, ROWS]); tc = sb("tc", [128, ROWS, 4])
        te = sb("te", [128, ROWS, 4]); ts = sb("ts", [128, ROWS]); tr = sb("tr", [128, ROWS]); tw = sb("tw", [128, ROWS, 5])
        mixed = sb("mixed", [128, 2, 5, S]); msum = sb("msum", [128, 2, S])
        wide = ctx.enter_context(nc.psum_tensor("me_wide", [128, 3, 2, 512], F32))
        gates = ctx.enter_context(nc.psum_tensor("me_gates", [128, 512], F32))
        s_w = sem("weights"); s_one = sem("ones"); s_full = sem("full"); s_ev = sem("emptied_v"); s_ea = sem("emptied_a")
        s_gf = sem("gates_full"); s_g = sem("gates_v"); s_ga = sem("gates_a"); s_mix = sem("mix"); s_res = sem("res")
        emptied_sem = {"v": s_ev, "a": s_ea}

        NW = 16 * 13

        def emptied(eng, b, *fills):
            for who, count in ring.latest(fills):
                wait_apart(eng, (s_w, NW), emptied_sem[who], b * ring.per[who] + (ring.per[who] + count))

        block = ctx.enter_context(nc.Block())
        loads = [(gate, "e_gate"), (sw1, "e_sw1"), (w1, "e_w1"), (sw2, "e_sw2"), (sw3, "e_sw3"), (sb1, "e_sb1"), (sb2, "e_sb2"),
                 (sb3, "e_sb3"), (b1, "e_b1"), (w2, "e_w2"), (b2, "e_b2"), (w3, "e_w3")]
        assert NW == 16 * (len(loads) + 1)

        @block.sync
        def _(sp):
            for t, name in loads:
                sp.dma_start(t[:], d[name]).then_inc(s_w, 16)
            sp.dma_start(before[:], d["c_before"].rearrange("p (i j) -> p i j", i=4)).then_inc(s_w, 16)

        @block.gpsimd
        def _(pool):
            fills = [(gl[:], 0.0), (h1[S:128, :], 0.0), (g2[S:128, :, :], 0.0), (g2[S:S + 1, :, :], 1.0), (tw[:, :, 0:1], 1.0)]
            for n, (t, value) in enumerate(fills):
                if n:
                    pool.wait_ge(s_one, n)
                nc.gpsimd.memset(t, value).then_inc(s_one, 1)
            pool.wait_ge(s_one, 5)
            nc.gpsimd.memset(msum[:, 0, 0:1], 0.0).then_inc(s_ev, ring.per["v"])
            nc.gpsimd.memset(msum[:, 1, 0:1], 0.0).then_inc(s_ea, ring.per["a"])

        @block.vector
        def _(v):
            v.wait_ge(s_w, NW)
            v.wait_ge(s_one, 5)
            v.wait_ge(s_ea, ring.per["a"])
            nc.vector.tensor_tensor(res[:], res[:], sb3[:, None, :].broadcast_to([128, ROWS, S]), ALU.add).then_inc(s_res, 1)
            step = [0]

            def done(i):
                i.then_inc(s_g, 1)
                step[0] += 1
                v.wait_ge(s_g, step[0])

            def over_experts(a):
                return a[:, :, None].broadcast_to([128, ROWS, 4])

            v.wait_ge(s_gf, 1)
            src = gates[:, 0:4 * ROWS].rearrange("p (b c e) -> p b c e", b=B, e=4)
            g4 = gl[:].rearrange("p (b c) e -> p b c e", b=B)
            done(nc.vector.tensor_copy(g4[:, :, 0:4, :], src[:, :, 0:4, :]))
            done(nc.vector.tensor_copy(g4[0:64, :, 4, :], src[0:64, :, 4, :]))
            done(nc.vector.tensor_reduce(gm[:], gl[:], AX, ALU.max))
            done(nc.vector.tensor_tensor(gc[:], gl[:], over_experts(gm), ALU.subtract))
            CENTRED = step[0]
            v.wait_ge(s_ga, 1)
            done(nc.vector.tensor_reduce(gs[:], ge[:], AX, ALU.add))
            done(nc.vector.reciprocal(gr[:], gs[:]))
            done(nc.vector.tensor_tensor(gp[:], ge[:], over_experts(gr), ALU.mult))
            mine, other = gp[:, :, :, None].broadcast_to([128, ROWS, 4, 4]), gp[:, :, None, :].broadcast_to([128, ROWS, 4, 4])
            done(nc.vector.tensor_tensor(gt[:], other, mine, ALU.is_gt))
            done(nc.vector.tensor_tensor(eq[:], other, mine, ALU.is_equal))
            done(nc.vector.tensor_tensor(eq[:], eq[:], before[:, None, :, :].broadcast_to([128, ROWS, 4, 4]), ALU.mult))
            done(nc.vector.tensor_tensor(gt[:], gt[:], eq[:], ALU.add))
            done(nc.vector.tensor_reduce(rank[:], gt[:], AX, ALU.add))
            done(nc.vector.tensor_scalar(top[:], rank[:], 1.5, None, ALU.is_lt))
            done(nc.vector.tensor_reduce(tm[:], gp[:], AX, ALU.max))
            done(nc.vector.tensor_tensor(tc[:], gp[:], over_experts(tm), ALU.subtract))
            KEPT = step[0]
            v.wait_ge(s_ga, 2)
            done(nc.vector.tensor_tensor(te[:], te[:], top[:], ALU.mult))
            done(nc.vector.tensor_reduce(ts[:], te[:], AX, ALU.add))
            done(nc.vector.reciprocal(tr[:], ts[:]))
            done(nc.vector.tensor_tensor(tw[:, :, 1:5], te[:], over_experts(tr), ALU.mult))
            assert (CENTRED, KEPT) == (4, 15)
            v.wait_ge(s_res, 1)

            with v.Fori(0, B) as b:
                def got(name):
                    v.wait_ge(s_full, NF * b + FILL[name] + 1)
                    return wide[:, FILL[name] % ring.size, :, :]

                def hidden(name, out, bias):
                    rows = out.shape[0]
                    nc.vector.tensor_scalar(out.rearrange("p (a t) -> p a t", a=2), got(name)[0:rows, :, 0:288], bias, 0.0, ALU.add, ALU.max).then_inc(s_ev, 1)

                hidden("shared2", h2[:], sb2[:, 0:1])
                for x in range(4):
                    hidden(f"e2_{x}", g2[0:S, x, :], b2[:, x:x + 1])
                for c in range(5):
                    rows = 128 if c < 4 else 64
                    src = got(f"out{c}")[0:rows, 0, 0:320].rearrange("p (e f) -> p e f", e=5)
                    m = mixed[0:rows, c % 2]
                    weights = tw[0:rows, bass.ds(5 * b + c, 1), :].rearrange("p a e -> p (a e)")[:, :, None].broadcast_to([rows, 5, S])
                    nc.vector.tensor_tensor(m, src, weights, ALU.mult).then_inc(s_ev, 1)
                    v.wait_ge(s_ev, ring.per["v"] * b + (ring.per["v"] + 5 + c + 1))
                    nc.vector.tensor_reduce(msum[0:rows, c % 2, :], m.rearrange("p e f -> p f e"), AX, ALU.add).then_inc(s_mix, 1)
                    v.wait_ge(s_mix, 5 * b + c + 1)
                    r = res[0:rows, bass.ds(5 * b + c, 1), :].rearrange("p c f -> p (c f)")
                    nc.vector.tensor_tensor(r, r, msum[0:rows, c % 2, :], ALU.add).then_inc(s_res, 1)

        @block.scalar
        def _(act):
            act.wait_ge(s_w, NW)
            act.wait_ge(s_g, 4)
            nc.scalar.activation(ge[:], gc[:], ACT.Exp).then_inc(s_ga, 1)
            act.wait_ge(s_g, 15)
            nc.scalar.activation(te[:], tc[:], ACT.Exp).then_inc(s_ga, 1)
            with act.Fori(0, B) as b:
                def hidden(name, out, bias):
                    n = FILL[name]
                    act.wait_ge(s_full, NF * b + n + 1)
                    rows = out.shape[0]
                    nc.scalar.activation(out.rearrange("p (a t) -> p a t", a=2), wide[0:rows, n % ring.size, :, 0:288], ACT.Relu, bias=bias, scale=1.0).then_inc(s_ea, 1)

                hidden("shared1", h1[0:S, :], sb1[:, 0:1])
                for x in range(4):
                    hidden(f"e1_{x}", g1[:, x % 2, :], b1[:, x:x + 1])

        @block.tensor
        def _(pe):
            mm = nc.tensor.matmul
            pe.wait_ge(s_w, NW)
            pe.wait_ge(s_one, 5)
            for b in range(B):
                for c in range(5):
                    rows = 128 if c < 4 else 64
                    at = 4 * (5 * b + c)
                    i = mm(gates[0:rows, at:at + 4], xt[:, b, 128 * c:128 * c + rows], gate[:], start=True, stop=True)
            i.then_inc(s_gf, 1)
            with pe.Fori(0, B) as b:
                def fill(name, *reads):
                    n = FILL[name]
                    emptied(pe, b, n - ring.size, *[FILL[r] for r in reads])
                    return wide[:, n % ring.size, :, :]

                def layer(name, rows, lhs, rhs, *reads):
                    out = fill(name, *reads)
                    for a in range(2):
                        i = mm(out[0:rows, a, 0:288], lhs, rhs(288 * a, 288 * a + 288), start=True, stop=True)
                    i.then_inc(s_full, 1)

                def x_in(t0, t1):
                    return xt[:, bass.ds(b, 1), t0:t1].rearrange("p a t -> p (a t)")

                def first(x):
                    layer(f"e1_{x}", 128, w1[:, 128 * x:128 * x + 128], x_in)

                def second(x):
                    layer(f"e2_{x}", S, w2[:, 64 * x:64 * x + 64], lambda t0, t1: g1[:, x % 2, t0:t1], f"e1_{x}")

                layer("shared1", S, sw1[:], x_in)
                first(0)
                layer("shared2", 128, sw2[:], lambda t0, t1: h1[:, t0:t1], "shared1")
                first(1)
                second(0)
                first(2)
                second(1)
                first(3)
                second(2)
                second(3)
                for c in range(5):
                    rows = 128 if c < 4 else 64
                    out = fill(f"out{c}", "shared2", "e2_3")
                    mm(out[0:rows, 0, 0:S], h2[:, 128 * c:128 * c + rows], sw3[:], start=True, stop=True)
                    for x in range(4):
                        i = mm(out[0:rows, 0, 64 * x + 64:64 * x + 128], g2[:, x, 128 * c:128 * c + rows], w3[:, 64 * x:64 * x + 64], start=True, stop=True)
                    i.then_inc(s_full, 1)


def early_fusion_kernel(nc, d, out, ctx_dram, h_spatial):
    fno_stage(nc, d, h_spatial)
    with ExitStack() as ctx:
        def sb(n, shape):
            return ctx.enter_context(nc.sbuf_tensor(n, shape, F32))

        res = sb("res", [128, ROWS, S])
        xn = sb("xn", [128, ROWS, S + 1])
        xt = sb("xt", [128, B, T])
        ident = sb("ident", [128, 128])
        s_id = ctx.enter_context(nc.semaphore("ident_loaded"))
        s_zero = ctx.enter_context(nc.semaphore("xt_padded"))
        with nc.Block() as block:
            @block.gpsimd
            def _(pool):
                nc.gpsimd.memset(xt[S:128, :, :], 0.0).then_inc(s_zero, 1)
                pool.wait_ge(s_zero, 1)

            @block.sync
            def _(sp):
                sp.dma_start(ident[:], d["c_ident"]).then_inc(s_id, 16)
                sp.wait_ge(s_id, 16)
        load_tokens(nc, d, h_spatial, res)
        norm_stage(nc, "n1", res, xn, xt, ident)
        with ExitStack() as inner:
            o_query = inner.enter_context(nc.sbuf_tensor("o_query", [128, ROWS, S], F32))
            o_key = inner.enter_context(nc.sbuf_tensor("o_key", [128, ROWS, S], F32))
            l1_stage(nc, d, xt, o_query, o_key, ident)
            fanin_stage(nc, d, res, xn, o_query, o_key, ident)
        norm_stage(nc, "n2", res, xn, xt, ident)
        slice_stage(nc, d, res, xn, xt, ident)
        norm_stage(nc, "n3", res, xn, xt, ident)
        mqa_stage(nc, d, xt, ctx_dram, ident)
        mqa_out_stage(nc, d, ctx_dram, res)
        norm_stage(nc, "n4", res, xn, xt, ident)
        moe_stage(nc, d, res, xt)
        store_tokens(nc, out, res)


def kernel(**inputs):
    import concourse.bacc as bacc
    from concourse.bass_utils import run_bass_kernel_spmd

    nc = bacc.Bacc("TRN2", target_bir_lowering=False, num_devices=1)
    constants = {**fno_constants(), **l1_constants(), **moe_constants()}
    laid = {**constants, **fno_layout(inputs, constants), **l1_layout(inputs), **slice_layout(inputs), **mqa_layout(inputs),
            **moe_layout(inputs), "txt": inputs["txt"]}
    arrays, d = {}, {}
    for name, a in laid.items():
        a = np.ascontiguousarray(a)
        arrays["in_" + name] = a
        d[name] = nc.dram_tensor("in_" + name, a.shape, mybir.dt.from_np(a.dtype), kind="ExternalInput").ap()
    out = nc.dram_tensor("out_0_dram", (B, T, S), F32, kind="ExternalOutput").ap()
    ctx_dram = nc.dram_tensor("ctx_scratch", (B, T, 512), F32, kind="Internal").ap()
    h_spatial = nc.dram_tensor("h_scratch", (B, S, S), F32, kind="Internal").ap()
    early_fusion_kernel(nc, d, out, ctx_dram, h_spatial)
    r = run_bass_kernel_spmd(nc, [arrays], core_ids=[0])
    return r.results[0]["out_0_dram"]
```

```python
from contextlib import ExitStack

import numpy as np

import concourse.bass as bass
from concourse import mybir

F32 = mybir.dt.float32
ALU = mybir.AluOpType
ACT = mybir.ActivationFunctionType
AX = mybir.AxisListType.X

B = 8
S = 64
CH = 32
LAYERS = 4
MODES_Y = 12
MODES_X = 24
MID = 4
NIMG = B + 3

T = 576
ROWS = 5 * B
EPS = 1e-5


def padded(a):
    a = np.asarray(a)
    return np.concatenate([a, np.zeros((128 - a.shape[0], a.shape[1]), a.dtype)])


def fno_constants():
    y = np.arange(S)
    ky = np.arange(MODES_Y)
    kx = np.concatenate([np.arange(MODES_Y), np.arange(S - MODES_Y, S)])
    x = np.arange(S)
    norm = 1.0 / np.sqrt(S)
    ay = 2 * np.pi * np.outer(y, ky) / S
    ax = 2 * np.pi * np.outer(x, kx) / S
    fy = np.zeros((2, S, 2, MODES_Y, 2))
    for r in range(2):
        fy[r, :, r, :, 0] = np.cos(ay) * norm
        fy[r, :, r, :, 1] = -np.sin(ay) * norm
    fx = np.zeros((S, 2, MODES_X, 2))
    fx[:, 0, :, 0] = np.cos(ax) * norm
    fx[:, 0, :, 1] = -np.sin(ax) * norm
    fx[:, 1, :, 0] = np.sin(ax) * norm
    fx[:, 1, :, 1] = np.cos(ax) * norm
    bx = np.zeros((MODES_X, 2, S, 2))
    bx[:, 0, :, 0] = np.cos(ax).T * norm
    bx[:, 0, :, 1] = np.sin(ax).T * norm
    bx[:, 1, :, 0] = -np.sin(ax).T * norm
    bx[:, 1, :, 1] = np.cos(ax).T * norm
    wy = np.where(ky == 0, 1.0, 2.0)[:, None]
    by = np.zeros((4, MODES_Y, 2, 2, 2, S))
    for r in range(4):
        by[r, :, 0, r // 2, r % 2, :] = wy * np.cos(ay).T * norm
        by[r, :, 1, r // 2, r % 2, :] = -wy * np.sin(ay).T * norm
    g = np.linspace(0.0, 1.0, S, dtype=np.float32)
    grid = np.stack([np.broadcast_to(g[:, None], (S, S)), np.broadcast_to(g[None, :], (S, S)), np.ones((S, S))])
    f32 = np.float32
    return {
        "c_fy": fy.reshape(128, 48).astype(f32),
        "c_fx": fx.reshape(128, 48).astype(f32),
        "c_bx": bx.reshape(48, 128).astype(f32),
        "c_by": by.reshape(96, 2 * 128).astype(f32),
        "c_grid": grid.astype(f32),
        "c_ident": np.eye(128, dtype=f32),
    }


def fno_layout(i, c):
    f32 = np.float32
    x = np.asarray(i["x"])[..., 0]
    img = np.concatenate([x, c["c_grid"]])
    a = {}
    a["f_img_pix"] = img.reshape(NIMG, 32, 128).transpose(2, 1, 0)
    a["f_img_row"] = img.reshape(NIMG, 32 * 128)
    pw, pb = np.asarray(i["L0_tok_p_w"]), np.asarray(i["L0_tok_p_b"])
    lift = np.zeros((NIMG, B, CH), f32)
    for b in range(B):
        lift[b, b] = pw[:, 0]
        lift[B, b] = pw[:, 1]
        lift[B + 1, b] = pw[:, 2]
        lift[B + 2, b] = pb
    a["f_lift"] = lift.reshape(NIMG, B * CH)
    a["f_lift_t"] = lift.reshape(NIMG, 2, 128).transpose(2, 1, 0)
    fw = np.asarray(i["L0_tok_fw"])
    a["f_modes"] = fw.transpose(0, 6, 2, 5, 1, 4, 3).reshape(LAYERS, 64, 288 * CH)
    w1, w2 = np.asarray(i["L0_tok_w1_w"]), np.asarray(i["L0_tok_w2_w"])
    a["f_w1t"] = np.tile(w1.transpose(0, 2, 1), (1, 4, 1))
    w2n = np.zeros((LAYERS, 4, CH, 4, CH), f32)
    w2t = np.zeros((LAYERS, 4, CH, 4, CH), f32)
    q1 = np.zeros((4, CH, 4, MID), f32)
    for b in range(4):
        w2n[:, b, :, b, :] = w2
        w2t[:, b, :, b, :] = w2.transpose(0, 2, 1)
        q1[b, :, b, :] = np.asarray(i["L0_tok_q1_w"]).T
    a["f_w2n"] = w2n.reshape(LAYERS, 128, 128)
    a["f_w2t"] = w2t.reshape(LAYERS, 128, 128)
    a["f_q1"] = q1.reshape(128, 16)
    a["f_b1"] = np.tile(np.asarray(i["L0_tok_w1_b"]), (1, B)).reshape(LAYERS, 1, B * CH)
    a["f_b2"] = np.tile(np.asarray(i["L0_tok_w2_b"]), (1, 4)).T
    a["f_q1b"] = np.broadcast_to(np.asarray(i["L0_tok_q1_b"]), (128, MID))
    a["f_q2"] = np.broadcast_to(np.asarray(i["L0_tok_q2_w"]).reshape(-1), (128, MID))
    a["f_q2b"] = np.broadcast_to(np.asarray(i["L0_tok_q2_b"]), (128, 1))
    return a


class BankRing:

    def __init__(self, owners, size):
        self.owners, self.size = owners, size
        self.per = {e: owners.count(e) for e in ("v", "a")}

    def emptied(self, n):
        return self.owners[n], self.owners[:n + 1].count(self.owners[n])

    def latest(self, fills):
        need = {}
        for n in fills:
            who, count = self.emptied(n % len(self.owners))
            if n < 0:
                count -= self.per[who]
            need[who] = max(need.get(who, count), count)
        return sorted(need.items())


def fno_steps():
    steps = [("proj", 1), ("modes", 3), ("mix1", 12), ("inv_x", 6), ("turn_y", 8), ("inv_y", 16), ("turn_r", 16),
             ("fwd_y", 8), ("turn_x", 6), ("fwd_x", 4), ("mix2", 4)]
    first, owners = {}, []
    for name, n in steps:
        first[name] = len(owners)
        owners += ["v"] * n if name in ("mix2", "proj") else ["va"[k % 2] for k in range(n)]
    return first, owners


def fno_stage(nc, d, h_spatial):
    FIRST, OWNERS = fno_steps()
    ring = BankRing(OWNERS, 6)
    NG = len(OWNERS)
    assert NG % ring.size == 0
    with ExitStack() as ctx:
        def sb(n, shape, dt=F32):
            return ctx.enter_context(nc.sbuf_tensor("fno_" + n, shape, dt))

        def sem(n):
            return ctx.enter_context(nc.semaphore("fno_" + n))

        mid = ctx.enter_context(nc.psum_tensor("fno_mid", [128, 2, 512], F32))
        bank = ctx.enter_context(nc.psum_tensor("fno_bank", [128, 6, 512], F32))

        fy = sb("fy", [128, 48]); fx = sb("fx", [128, 48]); bx = sb("bx", [48, 128]); by = sb("by", [96, 2, 128])
        ident = sb("ident", [128, 128])
        img_pix = sb("img_pix", [128, 32, NIMG]); img_row = sb("img_row", [NIMG, 32, 128])
        lift = sb("lift", [NIMG, 2, 128]); lift_t = sb("lift_t", [128, 2, NIMG])
        q1 = sb("q1", [128, 16]); q1b = sb("q1b", [128, MID]); q2 = sb("q2", [128, MID]); q2b = sb("q2b", [128, 1])
        b2 = sb("b2", [128, LAYERS]); b2s = sb("b2s", [128, 1])
        w_modes = sb("w_modes", [64, 288, CH])
        w1t = sb("w1t", [128, LAYERS, CH]); w2n = sb("w2n", [128, LAYERS, 128]); w2t = sb("w2t", [128, LAYERS, 128])
        b1 = sb("b1", [1, LAYERS, B * CH]); b1c = sb("b1c", [1, B * CH])
        w1c = sb("w1c", [128, CH]); w2c = sb("w2c", [128, 2, 128])
        spec = sb("spec", [128, 3, 2, 288])
        lhs = sb("lhs", [64, 2, B, 288])
        y_out = sb("y_out", [128, 3, MODES_X, 2, B])
        v_in = sb("v_in", [128, MODES_Y, B * CH])
        t_x = sb("t_x", [128, 2, S, MODES_Y, 2])
        t_y = sb("t_y", [96, 16, B * CH])
        relu_u = sb("relu_u", [128, 32, B * CH])
        proj = sb("proj", [128, 16])
        r_t = sb("r_t", [128, 8, 512])
        g_y = t_x[:].rearrange("p g x k c -> p (g x k c)").rearrange("p (g k x c) -> p g k x c", g=2, k=MODES_Y, c=2)
        g_x = v_in[:].rearrange("p k n -> p (k n)").rearrange("p (t n) -> p t n", n=128)
        p_x = sb("p_x", [128, 2, 576])
        img_y = sb("img_y", [NIMG, MODES_Y, S, 2]); img_t = sb("img_t", [128, MODES_Y, NIMG]); img_x = sb("img_x", [NIMG, 576])
        q0 = sb("q0", [NIMG, 2, 16])
        hid = sb("hid", [128, 32, B, MID]); feat = sb("feat", [128, 32, B]); feat_r = sb("feat_r", [128, 2, 4, 32])
        tok = sb("tok", [128, 2, 128])

        s_const = sem("const"); s_wm = sem("w_modes");
        s_full = sem("bank_full"); s_ev = sem("emptied_v"); s_ea = sem("emptied_a")
        s_wc = sem("layer_weights"); s_b1 = sem("bias1_added"); s_spec = sem("spectrum"); s_dc = sem("constant_term")
        s_lhs = sem("lhs_loaded"); s_fin = sem("tail_v"); s_pre = sem("pre_pe")
        s_pv = sem("pre_v"); s_layer = sem("layer_projected"); s_turn = sem("tail_pe"); s_tok = sem("tok_out")
        emptied_sem = {"v": s_ev, "a": s_ea}

        def emptied(eng, l, n):
            who, count = ring.emptied(n)
            eng.wait_ge(emptied_sem[who], l * ring.per[who] + count)

        def step_in_sbuf(eng, l, name, n):
            last = {}
            for k in range(FIRST[name], FIRST[name] + n):
                last[OWNERS[k]] = k
            for k in last.values():
                emptied(eng, l, k)

        block = ctx.enter_context(nc.Block())
        loads = [(fy, "c_fy"), (fx, "c_fx"), (bx, "c_bx"), (ident, "c_ident"), (q1, "f_q1"), (q1b, "f_q1b"),
                 (q2, "f_q2"), (q2b, "f_q2b"), (b2, "f_b2"), (img_pix, "f_img_pix"), (lift_t, "f_lift_t")]
        NCONST = 16 * (len(loads) + 7)

        @block.sync
        def _(sp):
            for t, name in loads:
                sp.dma_start(t[:], d[name]).then_inc(s_const, 16)
            sp.dma_start(by[:], d["c_by"].rearrange("p (s n) -> p s n", s=2)).then_inc(s_const, 16)
            sp.dma_start(img_row[:], d["f_img_row"].rearrange("p (s n) -> p s n", s=32)).then_inc(s_const, 16)
            sp.dma_start(lift[:], d["f_lift"].rearrange("p (s n) -> p s n", s=2)).then_inc(s_const, 16)
            sp.dma_start(w1t[:], d["f_w1t"].rearrange("l p n -> p l n")).then_inc(s_const, 16)
            sp.dma_start(w2n[:], d["f_w2n"].rearrange("l p n -> p l n")).then_inc(s_const, 16)
            sp.dma_start(w2t[:], d["f_w2t"].rearrange("l p n -> p l n")).then_inc(s_const, 16)
            sp.dma_start(b1[:], d["f_b1"].rearrange("l p n -> p l n")).then_inc(s_const, 16)

            def gather(l):
                sp.wait_ge(s_spec, l + 1)
                for c2, plane in ((0, (0, 1)), (1, (2, 0))):
                    for c in range(2):
                        for b4 in range(4):
                            sp.dma_start(lhs[32 * c2:32 * c2 + 32, c, :, :].rearrange("p (g b) m -> p g b m", g=2)[:, :, b4, :],
                                         spec[32 * b4:32 * b4 + 32, plane[c], :, :]).then_inc(s_lhs, 16)

            gather(0)
            with sp.Fori(1, LAYERS) as l:
                gather(l)
            for g in range(2):
                for b4 in range(4):
                    if g == 0 and b4 == 0:
                        sp.wait_ge(s_fin, 6)
                    sp.dma_start(h_spatial[4 * g + b4].rearrange("(a r) y -> a (r y)", r=2),
                                 tok[32 * b4:32 * b4 + 32, g, :]).then_inc(s_tok, 16)
            sp.wait_ge(s_tok, 16 * 8)

        @block.gpsimd
        def _(pool):
            pool.dma_start(w_modes[:], d["f_modes"][0].rearrange("p (m o) -> p m o", o=CH)).then_inc(s_wm, 16)
            with pool.Fori(1, LAYERS) as l:
                pool.wait_ge(s_full, (l - 1) * NG + 4)
                pool.dma_start(w_modes[:], d["f_modes"][bass.ds(l, 1)].rearrange("a p (m o) -> p (a m) o", o=CH)).then_inc(s_wm, 16)

        def add_spectrum(src, g, half, first):
            for c in range(2):
                dst = spec[:, c, g, 144 * half:144 * half + 144]
                if first:
                    i = nc.vector.tensor_copy(dst, src[:, c:288:2])
                else:
                    i = nc.vector.tensor_tensor(dst, dst, src[:, c:288:2], ALU.add)
            return i

        def layers(eng, body):
            with eng.Fori(0, LAYERS - 1) as l:
                body(l, False)
            body(LAYERS - 1, True)

        def empty_banks(eng, l, me, last):
            done = emptied_sem[me]

            def move(out, in_):
                return nc.vector.tensor_copy(out, in_) if me == "v" else nc.scalar.copy(out, in_)

            def mine(name, n):
                for k in range(n):
                    at = FIRST[name] + k
                    if OWNERS[at] == me:
                        eng.wait_ge(s_full, l * NG + at + 1)
                        yield k, bank[:, at % ring.size, :]

            for _, src in mine("proj", 1):
                move(proj[:], src[:, 0:16]).then_inc(done, 1)
            for r, src in mine("modes", 3):
                move(y_out[:, r].rearrange("p k c b -> p (k c b)"), src[:, 0:384]).then_inc(done, 1)
            for ky, src in mine("mix1", 12):
                i = move(v_in[0:48, ky, :], src[0:48, 0:256])
                if ky:
                    i.then_inc(done, 1)
                    continue
                i.then_inc(s_b1, 1)
                eng.wait_ge(s_b1, l + 1)
                nc.vector.scalar_tensor_tensor(out=v_in[0:1, 0, :], in0=b1c[:, :], scalar=float(S), in1=v_in[0:1, 0, :],
                                               op0=ALU.mult, op1=ALU.add).then_inc(done, 1)
            for k, src in mine("inv_x", 6):
                g, ky = divmod(4 * k, 12)
                move(t_x[:, g, :, ky:ky + 4, :].rearrange("p x k c -> p k x c"),
                     src.rearrange("p (k x c) -> p k x c", k=4, c=2)).then_inc(done, 1)
            for k, src in mine("turn_y", 8):
                move(t_y[:, 2 * k:2 * k + 2, :].rearrange("p a n -> p (a n)"), src[0:96, :]).then_inc(done, 1)
            for k, src in mine("inv_y", 16):
                out = relu_u[:, 2 * k:2 * k + 2, :].rearrange("p a n -> p (a n)")
                if me == "v":
                    nc.vector.tensor_scalar(out, src, 0.0, None, ALU.max).then_inc(done, 1)
                else:
                    nc.scalar.activation(out, src, ACT.Relu).then_inc(done, 1)
            for k, src in mine("turn_r", 16):
                move(r_t[:, k % 8, :], src).then_inc(done, 1)
            if last:
                return
            for k, src in mine("fwd_y", 8):
                g, x0 = k // 4, 16 * (k % 4)
                move(g_y[:, g, :, x0:x0 + 16, :].rearrange("p k x c -> p x k c"),
                     src[:, 0:384].rearrange("p (x k c) -> p x k c", x=16, c=2)).then_inc(done, 1)
            for k, src in mine("turn_x", 6):
                move(g_x[:, 4 * k:4 * k + 4, :].rearrange("p t n -> p (t n)"), src).then_inc(done, 1)
            for k, src in mine("fwd_x", 4):
                move(p_x[:, k // 2, 288 * (k % 2):288 * (k % 2) + 288], src[:, 0:288]).then_inc(done, 1)
            for k, src in mine("mix2", 4):
                add_spectrum(src, k // 2, k % 2, False).then_inc(done, 1)

        @block.scalar
        def _(act):
            layers(act, lambda l, last: empty_banks(act, l, "a", last))

        @block.vector
        def _(v):
            v.wait_ge(s_const, NCONST)
            nc.vector.tensor_reduce(b2s[:], b2[:], AX, ALU.add).then_inc(s_pv, 1)
            v.wait_ge(s_pv, 1)
            for g in range(2):
                nc.vector.tensor_tensor(lift_t[:, g, NIMG - 1:NIMG], lift_t[:, g, NIMG - 1:NIMG], b2s[:], ALU.add).then_inc(s_pv, 1)
            for k in range(4):
                v.wait_ge(s_pre, k + 1)
                nc.vector.tensor_copy(img_y[:, :, 16 * k:16 * k + 16, :].rearrange("p k x c -> p x k c"),
                                      bank[0:NIMG, k, 0:384].rearrange("p (x k c) -> p x k c", x=16, c=2)).then_inc(s_pv, 1)
            v.wait_ge(s_pre, 5)
            nc.vector.tensor_copy(img_t[:].rearrange("p k n -> p (k n)"), bank[:, 4, 0:12 * NIMG]).then_inc(s_pv, 1)
            v.wait_ge(s_pre, 6)
            nc.vector.tensor_copy(q0[:].rearrange("p g n -> p (g n)"), bank[0:NIMG, 5, 0:32]).then_inc(s_pv, 1)
            for k in range(2):
                v.wait_ge(s_pre, 7 + k)
                nc.vector.tensor_copy(img_x[:, 288 * k:288 * k + 288], bank[0:NIMG, k, 0:288]).then_inc(s_pv, 1)
            for k in range(4):
                v.wait_ge(s_pre, 9 + k)
                add_spectrum(bank[:, 2 + k, :], k // 2, k % 2, True).then_inc(s_pv, 1)
            v.wait_ge(s_pv, 15)
            nc.vector.tensor_scalar(spec[:, 2, :, :], spec[:, 1, :, :], -1.0, None, ALU.mult).then_inc(s_spec, 1)

            def layer(l, last):
                nc.vector.tensor_copy(w1c[:], w1t[:, bass.ds(l, 1), :].rearrange("p a n -> p (a n)")).then_inc(s_wc, 1)
                nc.vector.tensor_copy(w2c[:, 0, :], w2n[:, bass.ds(l, 1), :].rearrange("p a n -> p (a n)")).then_inc(s_wc, 1)
                nc.vector.tensor_copy(w2c[:, 1, :], w2t[:, bass.ds(l, 1), :].rearrange("p a n -> p (a n)")).then_inc(s_wc, 1)
                nc.vector.tensor_copy(b1c[:], b1[:, bass.ds(l, 1), :].rearrange("p a n -> p (a n)")).then_inc(s_wc, 1)
                empty_banks(v, l, "v", last)
                if last:
                    return
                v.wait_ge(s_ev, (l + 1) * ring.per["v"])
                for g in range(2):
                    nc.vector.scalar_tensor_tensor(out=spec[:, 0, g, 0:1], in0=b2[:, bass.ds(l, 1)], scalar=float(S),
                                                   in1=spec[:, 0, g, 0:1], op0=ALU.mult, op1=ALU.add).then_inc(s_dc, 1)
                v.wait_ge(s_dc, l * 2 + 2)
                nc.vector.tensor_scalar(spec[:, 2, :, :], spec[:, 1, :, :], -1.0, None, ALU.mult).then_inc(s_spec, 1)

            layers(v, layer)
            v.wait_ge(s_layer, LAYERS)
            h3 = hid[:].rearrange("p x b j -> p (x b) j")
            nc.vector.tensor_tensor(h3, mid[:].rearrange("p k (n j) -> p (k n) j", j=MID),
                                    q1b[:, None, :].broadcast_to([128, 256, MID]), ALU.add).then_inc(s_fin, 1)
            v.wait_ge(s_fin, 1)
            nc.vector.scalar_tensor_tensor(out=h3, in0=h3, scalar=0.0, in1=q2[:, None, :].broadcast_to([128, 256, MID]),
                                           op0=ALU.max, op1=ALU.mult).then_inc(s_fin, 1)
            v.wait_ge(s_fin, 2)
            nc.vector.tensor_reduce(feat[:].rearrange("p x b -> p (x b)"), h3, AX, ALU.add).then_inc(s_fin, 1)
            v.wait_ge(s_fin, 3)
            nc.vector.tensor_scalar(feat_r[:].rearrange("p g b x -> p (g b) x"), feat[:].rearrange("p x b -> p b x"),
                                    q2b[:, 0:1], None, ALU.add).then_inc(s_fin, 1)
            for g in range(2):
                v.wait_ge(s_turn, g + 1)
                nc.vector.tensor_copy(tok[:, g, :], bank[:, g, 0:128]).then_inc(s_fin, 1)

        @block.tensor
        def _(pe):
            mm = nc.tensor.matmul
            pe.wait_ge(s_const, NCONST)
            for xh in range(32):
                i = mm(bank[0:NIMG, xh // 8, 48 * (xh % 8):48 * (xh % 8) + 48], img_pix[:, xh, :], fy[:], start=True, stop=True)
                if xh % 8 == 7:
                    i.then_inc(s_pre, 1)
            pe.wait_ge(s_pv, 7)
            for ky in range(12):
                i = nc.tensor.transpose(bank[:, 4, NIMG * ky:NIMG * ky + NIMG], img_y[:, ky, :, :].rearrange("p x c -> p (x c)"),
                                        ident[0:NIMG, 0:NIMG])
            i.then_inc(s_pre, 1)
            for g in range(2):
                i = mm(bank[0:NIMG, 5, 16 * g:16 * g + 16], lift_t[:, g, :], q1[:], start=True, stop=True)
            i.then_inc(s_pre, 1)
            pe.wait_ge(s_pv, 8)
            for ky in range(12):
                i = mm(bank[0:NIMG, ky // 6, 48 * (ky % 6):48 * (ky % 6) + 48], img_t[:, ky, :], fx[:], start=True, stop=True)
                if ky % 6 == 5:
                    i.then_inc(s_pre, 1)
            pe.wait_ge(s_pv, 11)
            for k in range(4):
                mm(bank[:, 2 + k, 0:288], lift[:, k // 2, :], img_x[:, 288 * (k % 2):288 * (k % 2) + 288], start=True, stop=True).then_inc(s_pre, 1)
            for xh in range(32):
                mm(mid[:, xh // 16, 32 * (xh % 16):32 * (xh % 16) + 32], img_row[:, xh, :], q0[:].rearrange("p g n -> p (g n)"),
                   start=(xh % 16 == 0), stop=False, skip_group_check=True)

            def layer(l, last):
                def fill(name, k):
                    n = FIRST[name] + k
                    if n >= ring.size:
                        emptied(pe, l, n - ring.size)
                    return bank[:, n % ring.size, :]

                pe.wait_ge(s_lhs, 16 * 16 * (l + 1))
                pe.wait_ge(s_wm, 16 * (l + 1))
                pe.wait_ge(s_wc, 4 * (l + 1))
                out = fill("proj", 0)
                mm(out[:, 0:16], w2c[:, 0, :], q1[:], start=True, stop=True).then_inc(s_full, 1)
                for r in range(3):
                    out = fill("modes", r)
                    for kx in range(MODES_X):
                        for q in range(4):
                            m = (4 * r + q) * MODES_X + kx
                            i = mm(out[32 * q:32 * q + 32, 16 * kx:16 * kx + 16], w_modes[:, m, :], lhs[:, :, :, m],
                                   start=True, stop=True, tile_position=(0, 32 * q))
                    i.then_inc(s_full, 1)
                for ky in range(12):
                    r, q = divmod(ky, 4)
                    if q == 0:
                        emptied(pe, l, FIRST["modes"] + r)
                    out = fill("mix1", ky)
                    for b in range(B):
                        i = mm(out[0:48, 32 * b:32 * b + 32], y_out[32 * q:32 * q + 32, r, :, :, b].rearrange("p k c -> p (k c)"),
                               w1c[32 * q:32 * q + 32, :], start=True, stop=True, tile_position=(32 * q, 0))
                    i.then_inc(s_full, 1)
                step_in_sbuf(pe, l, "mix1", 12)
                for k in range(6):
                    out = fill("inv_x", k)
                    for j in range(4):
                        g, ky = divmod(4 * k + j, 12)
                        i = mm(out[:, 128 * j:128 * j + 128], v_in[0:48, ky, 128 * g:128 * g + 128], bx[:], start=True, stop=True)
                    i.then_inc(s_full, 1)
                step_in_sbuf(pe, l, "inv_x", 6)
                for k in range(8):
                    out = fill("turn_y", k)
                    for j in range(4):
                        x4, g = 2 * k + j // 2, j % 2
                        i = nc.tensor.transpose(out[0:96, 128 * j:128 * j + 128],
                                                t_x[:, g, 4 * x4:4 * x4 + 4, :, :].rearrange("p x k c -> p (x k c)"), ident[:])
                    i.then_inc(s_full, 1)
                for k in range(16):
                    emptied(pe, l, FIRST["turn_y"] + k // 2)
                    out = fill("inv_y", k)
                    for j in range(2):
                        i = mm(out[:, 256 * j:256 * j + 256], by[:, j, :], t_y[:, k, :], start=True, stop=True)
                    i.then_inc(s_full, 1)
                def project(k):
                    emptied(pe, l, FIRST["turn_r"] + k)
                    for j in range(4):
                        xh, g = 2 * k + j // 2, j % 2
                        at = 32 * (xh % 16) + 16 * g
                        i = mm(mid[:, xh // 16, at:at + 16], r_t[:, k % 8, 128 * j:128 * j + 128], proj[:],
                               start=False, stop=False, skip_group_check=True)
                    return i

                for k in range(16):
                    emptied(pe, l, FIRST["inv_y"] + k)
                    out = fill("turn_r", k)
                    for j in range(4):
                        xh, g = 2 * k + j // 2, j % 2
                        i = nc.tensor.transpose(out[:, 128 * j:128 * j + 128], relu_u[:, xh, 128 * g:128 * g + 128], ident[:])
                    i.then_inc(s_full, 1)
                    if k >= 2:
                        project(k - 2)
                project(14)
                project(15).then_inc(s_layer, 1)
                if last:
                    return
                for k in range(8):
                    out = fill("fwd_y", k)
                    for j in range(8):
                        g, xh = k // 4, 8 * (k % 4) + j
                        i = mm(out[:, 48 * j:48 * j + 48], relu_u[:, xh, 128 * g:128 * g + 128], fy[:], start=True, stop=True)
                    i.then_inc(s_full, 1)
                step_in_sbuf(pe, l, "fwd_y", 8)
                for k in range(6):
                    out = fill("turn_x", k)
                    for j in range(4):
                        g, ky = divmod(4 * k + j, 12)
                        i = nc.tensor.transpose(out[:, 128 * j:128 * j + 128], g_y[:, g, ky, :, :].rearrange("p x c -> p (x c)"), ident[:])
                    i.then_inc(s_full, 1)
                step_in_sbuf(pe, l, "turn_x", 6)
                for k in range(4):
                    out = fill("fwd_x", k)
                    for j in range(6):
                        i = mm(out[:, 48 * j:48 * j + 48], g_x[:, 6 * k + j, :], fx[:], start=True, stop=True)
                    i.then_inc(s_full, 1)
                for k in range(4):
                    emptied(pe, l, FIRST["fwd_x"] + k)
                    out = fill("mix2", k)
                    mm(out[:, 0:288], w2c[:, 1, :], p_x[:, k // 2, 288 * (k % 2):288 * (k % 2) + 288], start=True, stop=True).then_inc(s_full, 1)

            layers(pe, layer)
            pe.wait_ge(s_fin, 4)
            for g in range(2):
                nc.tensor.transpose(bank[:, g, 0:128], feat_r[:, g, :, :].rearrange("p b x -> p (b x)"), ident[:]).then_inc(s_turn, 1)


def wait_apart(eng, met, sem, value):
    if not isinstance(value, int):
        value = eng.to_reg(value)
    eng.wait_ge(*met)
    eng.wait_ge(sem, value)


def load_tokens(nc, d, h_spatial, res):
    with ExitStack() as ctx:
        s_in = ctx.enter_context(nc.semaphore("tok_loaded"))
        s_pad = ctx.enter_context(nc.semaphore("tok_pad"))
        r4 = res[:].rearrange("p (b c) f -> p b c f", b=B)
        block = ctx.enter_context(nc.Block())

        @block.sync
        def _(sp):
            txt = d["txt"]
            sp.dma_start(r4[0:64, :, 0, :], h_spatial.rearrange("b t f -> t b f")).then_inc(s_in, 16)
            sp.dma_start(r4[64:128, :, 0, :], txt[:, 0:64, :].rearrange("b t f -> t b f")).then_inc(s_in, 16)
            for c in range(1, 4):
                sp.dma_start(r4[:, :, c, :], txt[:, 128 * c - 64:128 * c + 64, :].rearrange("b t f -> t b f")).then_inc(s_in, 16)
            sp.dma_start(r4[0:64, :, 4, :], txt[:, 448:512, :].rearrange("b t f -> t b f")).then_inc(s_in, 16)
            sp.wait_ge(s_in, 16 * 6)

        @block.gpsimd
        def _(pool):
            nc.gpsimd.memset(r4[64:128, :, 4, :], 0.0).then_inc(s_pad, 1)
            pool.wait_ge(s_pad, 1)


def norm_stage(nc, tag, res, xn, xt, ident):
    PARTS = 4
    W = ROWS // PARTS
    with ExitStack() as ctx:
        def sb(n, shape, dt=F32):
            return ctx.enter_context(nc.sbuf_tensor(f"{tag}_{n}", shape, dt))

        def sem(n):
            return ctx.enter_context(nc.semaphore(f"{tag}_{n}"))

        sq = sb("sq", [128, ROWS, S])
        total = sb("total", [128, ROWS]); mean = sb("mean", [128, ROWS]); var = sb("var", [128, ROWS])
        std = sb("std", [128, ROWS]); rstd = sb("rstd", [128, ROWS]); eps = sb("eps", [128, 1])
        turned = ctx.enter_context(nc.psum_tensor(f"{tag}_turned", [128, 4, 1024], F32))
        s_one = sem("ones"); s_sum = sem("sum"); s_mean = sem("mean"); s_cen = sem("centred"); s_sq = sem("squares")
        s_var = sem("var"); s_std = sem("std"); s_rstd = sem("rstd"); s_xn = sem("xn"); s_turn = sem("turned"); s_out = sem("xt")
        block = ctx.enter_context(nc.Block())

        @block.gpsimd
        def _(pool):
            nc.gpsimd.memset(eps[:], EPS).then_inc(s_one, 1)
            pool.wait_ge(s_one, 1)
            nc.gpsimd.memset(xn[:, :, S:S + 1], 1.0).then_inc(s_one, 1)
            pool.wait_ge(s_one, 2)
            nc.gpsimd.memset(xt[S:S + 1, :, :], 1.0).then_inc(s_one, 1)
            pool.wait_ge(s_one, 3)

        @block.vector
        def _(v):
            for p in range(PARTS):
                rows = slice(W * p, W * p + W)
                nc.vector.tensor_reduce(total[:, rows], res[:, rows, :], AX, ALU.add).then_inc(s_sum, 1)
            for p in range(PARTS):
                rows = slice(W * p, W * p + W)
                v.wait_ge(s_sum, p + 1)
                nc.vector.tensor_scalar(mean[:, rows], total[:, rows], 1.0 / S, None, ALU.mult).then_inc(s_mean, 1)
            for p in range(PARTS):
                rows = slice(W * p, W * p + W)
                v.wait_ge(s_mean, p + 1)
                nc.vector.tensor_tensor(xn[:, rows, 0:S], res[:, rows, :], mean[:, rows, None].broadcast_to([128, W, S]),
                                        ALU.subtract).then_inc(s_cen, 1)
            for p in range(PARTS):
                rows = slice(W * p, W * p + W)
                v.wait_ge(s_cen, p + 1)
                nc.vector.tensor_tensor(sq[:, rows, :], xn[:, rows, 0:S], xn[:, rows, 0:S], ALU.mult).then_inc(s_sq, 1)
                v.wait_ge(s_sq, p + 1)
                nc.vector.tensor_reduce(var[:, rows], sq[:, rows, :], AX, ALU.add).then_inc(s_var, 1)
            for p in range(PARTS):
                rows = slice(W * p, W * p + W)
                v.wait_ge(s_std, p + 1)
                nc.vector.reciprocal(rstd[:, rows], std[:, rows]).then_inc(s_rstd, 1)
                v.wait_ge(s_rstd, p + 1)
                nc.vector.tensor_tensor(xn[:, rows, 0:S], xn[:, rows, 0:S], rstd[:, rows, None].broadcast_to([128, W, S]),
                                        ALU.mult).then_inc(s_xn, 1)

        @block.scalar
        def _(act):
            act.wait_ge(s_one, 3)
            for p in range(PARTS):
                rows = slice(W * p, W * p + W)
                act.wait_ge(s_var, p + 1)
                nc.scalar.activation(std[:, rows], var[:, rows], ACT.Sqrt, bias=eps[:, 0:1], scale=1.0 / S).then_inc(s_std, 1)
            for b in range(B):
                act.wait_ge(s_turn, b + 1)
                nc.scalar.copy(xt[0:S, b, :], turned[0:S, b % 4, 0:T]).then_inc(s_out, 1)

        @block.tensor
        def _(pe):
            for b in range(B):
                if b % 2 == 0:
                    pe.wait_ge(s_xn, b // 2 + 1)
                if b >= 4:
                    pe.wait_ge(s_out, b - 3)
                for c in range(5):
                    n = min(128, T - 128 * c)
                    i = nc.tensor.transpose(turned[0:S, b % 4, 128 * c:128 * c + n], xn[0:n, 5 * b + c, 0:S], ident[0:n, 0:n])
                i.then_inc(s_turn, 1)


def l1_layout(i):
    f32 = np.float32
    w, bias = np.asarray(i["L0_attn_wqv_w"]), np.asarray(i["L0_attn_wqv_b"])
    wt = np.concatenate([w.T, bias[None]])
    wk = np.asarray(i["L0_attn_wk"])
    a = {"l1_wq": padded(wt[:, :512]), "l1_wvf": padded(wt[:, 512:1024])}
    wb = w[1024:].reshape(4, 2, S, S)
    both = np.zeros((2, S, 4, S + 1), f32)
    both[:, :, :, :S] = wb.transpose(1, 3, 0, 2)
    both[:, :, :, S] = wk.reshape(4, 2, S).transpose(1, 2, 0)
    a["l1_wvb"] = both.reshape(128, 4 * 65)
    by_head = bias[1024:].reshape(4, 2, S).transpose(1, 0, 2).reshape(1, 2, 256)
    a["l1_bvb"] = np.broadcast_to(by_head, (64, 2, 256)).reshape(128, 256)
    a["l1_wk"] = wk.reshape(4, 128).T
    a["l1_fan"] = np.concatenate([np.asarray(i["L0_attn_fanin_w"]).T, np.asarray(i["L0_attn_fanin_b"])[None]])
    return a


def l1_constants():
    f32 = np.float32
    dup = np.concatenate([np.eye(S), np.eye(S)], 1)
    sel = np.zeros((128, 62))
    sel[:64, 30] = 2.0
    sel[64:, 31] = 2.0
    neg = np.zeros((2, S, S, 2))
    for h in range(2):
        neg[h, :, :, h] = -1.0
    return {"c_dup": padded(dup).astype(f32), "c_fold": dup.T.astype(f32), "c_sel": sel.astype(f32), "c_neg": neg.reshape(128, 128).astype(f32)}


CUT = 320


def l1_stage(nc, d, xt, o_query_t, o_key_t, ident):
    RING = 16
    GROUPS = 16
    SCALE = 1.0 / 8.0
    FILLS = ["v"] * 2 + ["va"[k % 2] for k in range(30)]
    NF = len(FILLS)
    NW = 16 * 8
    QUERY, FORWARD, BACKWARD, QSUM = 2, 10, 15, 24
    fills = BankRing(FILLS, 6)
    with ExitStack() as ctx:
        def sb(n, shape, dt=F32):
            return ctx.enter_context(nc.sbuf_tensor("l1_" + n, shape, dt))

        def sem(n):
            return ctx.enter_context(nc.semaphore("l1_" + n))

        wq = sb("wq", [128, 512]); wvf = sb("wvf", [128, 512]); wvb = sb("wvb", [128, 4, 65]); bvb = sb("bvb", [128, 4 * S])
        wk = sb("wk", [128, 4]); nwk = sb("nwk", [128, 4])
        dup = sb("dup", [128, 128]); sel = sb("sel", [128, 62]); neg = sb("neg", [128, 128])
        xs = sb("xs", [128, T]); xdup = sb("xdup", [128, T]); xpar = sb("xpar", [128, T, 2])
        q = sb("q", [128, 4, T]); nqs = sb("minus_qsum", [128, 4, T]); nk = sb("nk", [128, 36 * 64])
        vf = sb("vf", [128, 5, 512]); vb = sb("vb", [128, 36, 65])
        nks = sb("nks", [128, 3, 64]); vbs = sb("vbs", [128, 3, S]); vfs = sb("vfs", [128, 5, 128])
        unit = sb("unit", [128, RING, T])
        e = sb("e", [128, 3, T]); z = sb("z", [128, 3]); z1 = sb("z1", [128, 3]); rz = sb("rz", [128, 3])
        at = sb("at", [128, 3, 5, 128])
        okt = sb("okt", [128, 4, T])
        score = ctx.enter_context(nc.psum_tensor("l1_score", [128, 6, 512], F32))
        turn = ctx.enter_context(nc.psum_tensor("l1_turn", [128, 512], F32))
        acc = ctx.enter_context(nc.psum_tensor("l1_acc", [128, 512], F32))

        s_w = sem("weights"); s_init = sem("init"); s_xs = sem("xs"); s_fill = sem("fill"); s_fv = sem("fill_emptied_v")
        s_fa = sem("fill_emptied_a"); s_xp = sem("x_by_parity"); s_nk = sem("minus_k"); s_nks = sem("minus_k_staged"); s_vbs = sem("backward_values_staged"); s_vfs = sem("forward_values_staged")
        s_uv = sem("units_v"); s_ua = sem("units_a"); s_use = sem("units_summed"); s_sub = sem("qsum_subtracted"); s_e = sem("exp")
        s_z1 = sem("z1"); s_rz = sem("rz"); s_p = sem("probs"); s_t = sem("turned"); s_ata = sem("at_a"); s_atv = sem("at_v")
        s_k = sem("key_out"); s_kc = sem("key_out_copied"); s_acc = sem("acc_copied"); s_add = sem("key_out_summed")
        filled = {"v": s_fv, "a": s_fa}
        by_vector = [[True, False, True, g % 2 == 1] for g in range(GROUPS)]

        def emptied(eng, b, *ns):
            for who, count in fills.latest(ns):
                eng.wait_ge(filled[who], b * fills.per[who] + count)

        block = ctx.enter_context(nc.Block())

        @block.sync
        def _(sp):
            for t, name in ((wq, "l1_wq"), (wvf, "l1_wvf"), (bvb, "l1_bvb"), (wk, "l1_wk"), (dup, "c_dup"), (sel, "c_sel"),
                            (neg, "c_neg")):
                sp.dma_start(t[:], d[name]).then_inc(s_w, 16)
            sp.dma_start(wvb[:], d["l1_wvb"].rearrange("p (a n) -> p a n", a=4)).then_inc(s_w, 16)

        def tiles(b, it, first):
            for k in range(3):
                prev = None if first and k == 0 else ((it - 1, 2) if k == 0 else (it, k - 1))
                yield k, prev

        def trips(eng, b, body, last):
            body(0, True)
            with eng.Fori(1, 12) as it:
                body(it, False)
            last(11, 2)

        @block.gpsimd
        def _(pool):
            for n, t in enumerate((xpar, vf, at)):
                if n:
                    pool.wait_ge(s_init, n)
                nc.gpsimd.memset(t[:], 0.0).then_inc(s_init, 1)
            with pool.Fori(0, B) as b:
                def stage(it, first):
                    for k in range(3):
                        n = 36 * b + 3 * it + k
                        if k == 0 and first:
                            wait_apart(pool, (s_w, NW), s_nk, 4 * b + 4)
                        if not first:
                            wait_apart(pool, (s_w, NW), s_uv, (n - 2) * GROUPS)
                            wait_apart(pool, (s_w, NW), s_ua, (n - 2) * GROUPS)
                        nc.gpsimd.tensor_copy(nks[:, k, :], nk[:, bass.ds(192 * it + 64 * k, 64)]).then_inc(s_nks, 1)
                    for k in range(3):
                        n = 36 * b + 3 * it + k
                        if k == 0 and first:
                            for me in ("v", "a"):
                                wait_apart(pool, (s_w, NW), filled[me], b * fills.per[me] + fills.per[me])
                        if not first:
                            wait_apart(pool, (s_w, NW), s_t, n - 2)
                        nc.gpsimd.tensor_tensor(vbs[:, k, :], vb[:, bass.ds(3 * it + k, 1), 0:S].rearrange("p a n -> p (a n)"),
                                                bvb[:, bass.ds((it // 3) * S, S)], ALU.add).then_inc(s_vbs, 1)
                    if not first:
                        wait_apart(pool, (s_w, NW), s_k, 12 * b + it)
                    nc.gpsimd.tensor_copy(vfs[:], vf[:, :, bass.ds((it // 3) * 128, 128)]).then_inc(s_vfs, 1)

                stage(0, True)
                with pool.Fori(1, 12) as it:
                    stage(it, False)

        def empty_fills(me, got):
            def move(out, in_):
                i = nc.vector.tensor_copy(out, in_) if me == "v" else nc.scalar.copy(out, in_)
                i.then_inc(filled[me], 1)

            for n in range(2, NF):
                if FILLS[n] != me:
                    continue
                src = got(n)
                if n < FORWARD:
                    hp, half = divmod(n - 2, 2)
                    move(q[:, hp, 288 * half:288 * half + 288], src[:, 0:288])
                elif n < BACKWARD:
                    rows = 128 if n < 14 else 64
                    move(vf[0:rows, n - 10, :], src[0:rows, :])
                elif n >= QSUM:
                    hp, half = divmod(n - QSUM, 2)
                    move(nqs[:, hp, 288 * half:288 * half + 288], src[:, 0:288])
                else:
                    move(vb[:, n - 15:36:9, :], src[:, 0:260].rearrange("p (a n) -> p a n", a=4))

        @block.vector
        def _(v):
            v.wait_ge(s_w, NW)
            v.wait_ge(s_init, 3)
            nc.vector.tensor_scalar(nwk[:], wk[:], -1.0, None, ALU.mult).then_inc(s_z1, 1)
            nc.vector.tensor_scalar(wvb[:, :, S:S + 1], wvb[:, :, S:S + 1], -SCALE, None, ALU.mult).then_inc(s_z1, 1)
            with v.Fori(0, B) as b:
                nc.vector.tensor_copy(xs[:], xt[:, bass.ds(b, 1), :].rearrange("p a t -> p (a t)")).then_inc(s_xs, 1)

                def got(n):
                    v.wait_ge(s_fill, NF * b + n + 1)
                    return score[:, n % 6, :]

                for n in range(2):
                    nc.vector.tensor_copy(xdup[:, 288 * n:288 * n + 288], got(n)[:, 0:288]).then_inc(s_fv, 1)
                v.wait_ge(s_fv, fills.per["v"] * b + 2)
                for h in range(2):
                    half = slice(64 * h, 64 * h + 64)
                    nc.vector.tensor_copy(xpar[half, :, h], xdup[half, :]).then_inc(s_xp, 1)
                v.wait_ge(s_z1, 36 * b + 2)
                for hp in range(4):
                    nc.vector.tensor_scalar(nk[:, T * hp:T * hp + T], xdup[:], nwk[:, hp:hp + 1], None, ALU.mult).then_inc(s_nk, 1)
                empty_fills("v", got)

                def produce(it, first):
                    for k, prev in tiles(b, it, first):
                        n = 36 * b + 3 * it + k
                        v.wait_ge(s_nks, n + 1)
                        for g in range(GROUPS):
                            if not (first and k == 0 and g < 4):
                                v.wait_ge(s_use, n * GROUPS + g - 3)
                            for j in range(4):
                                if by_vector[g][j]:
                                    u = 4 * g + j
                                    i = nc.vector.tensor_scalar(unit[:, u % RING, :], q[:, bass.ds(it // 3, 1), :].rearrange("p a t -> p (a t)"),
                                                                nks[:, k, 16 * j + g:16 * j + g + 1], 0.0, ALU.add, ALU.max)
                            i.then_inc(s_uv, 1)
                            if prev:
                                if g == 4:
                                    subtract(*prev)
                                if g == 8:
                                    normalise(*prev)
                                if g == 12:
                                    last_chunk(*prev)

                def subtract(it, k):
                    n = 36 * b + 3 * it + k
                    v.wait_ge(s_use, (n + 1) * GROUPS)
                    nc.vector.tensor_tensor(e[:, k, :].rearrange("p (a t) -> p a t", a=2), score[:, 2 * k:2 * k + 2, 0:288],
                                            nqs[:, bass.ds(it // 3, 1), :].rearrange("p x (a t) -> p (x a) t", a=2), ALU.add).then_inc(s_sub, 1)

                def normalise(it, k):
                    n = 36 * b + 3 * it + k
                    v.wait_ge(s_e, n + 1)
                    nc.vector.tensor_scalar(z1[:, k:k + 1], z[:, k:k + 1], 1.0, None, ALU.add).then_inc(s_z1, 1)
                    v.wait_ge(s_z1, n + 3)
                    nc.vector.reciprocal(rz[:, k:k + 1], z1[:, k:k + 1]).then_inc(s_rz, 1)
                    v.wait_ge(s_rz, n + 1)
                    nc.vector.tensor_scalar(e[:, k, :], e[:, k, :], rz[:, k:k + 1], None, ALU.mult).then_inc(s_p, 1)

                def last_chunk(it, k):
                    n = 36 * b + 3 * it + k
                    if k == 0 and not isinstance(it, int):
                        v.wait_ge(s_k, 12 * b + it)
                    v.wait_ge(s_t, n + 1)
                    nc.vector.tensor_copy(at[0:64, k, 4, :], score[0:64, 2 * k, 288:416]).then_inc(s_atv, 1)

                o_key_b = o_key_t[:, bass.ds(b, 1), :].rearrange("p a t -> p (a t)")

                def finish(it, k):
                    v.wait_ge(s_kc, 12 * b + 9)
                    nc.vector.tensor_tensor(o_key_b, okt[:, 0, :], okt[:, 1, :], ALU.add).then_inc(s_add, 1)
                    v.wait_ge(s_add, 3 * b + 1)
                    nc.vector.tensor_tensor(o_key_b, o_key_b, okt[:, 2, :], ALU.add).then_inc(s_add, 1)
                    subtract(it, k)
                    normalise(it, k)
                    last_chunk(it, k)

                trips(v, b, produce, finish)
                v.wait_ge(s_kc, 12 * b + 12)
                v.wait_ge(s_add, 3 * b + 2)
                nc.vector.tensor_tensor(o_key_b, o_key_b, okt[:, 3, :], ALU.add).then_inc(s_add, 1)

        @block.scalar
        def _(act):
            act.wait_ge(s_init, 3)
            with act.Fori(0, B) as b:
                def got(n):
                    act.wait_ge(s_fill, NF * b + n + 1)
                    return score[:, n % 6, :]

                empty_fills("a", got)
                act.wait_ge(s_fv, (b + 1) * fills.per["v"])

                def produce(it, first):
                    for k, prev in tiles(b, it, first):
                        n = 36 * b + 3 * it + k
                        wait_apart(act, (s_w, NW), s_nks, n + 1)
                        for g in range(GROUPS):
                            if not (first and k == 0 and g < 4):
                                wait_apart(act, (s_w, NW), s_use, n * GROUPS + g - 3)
                            for j in range(4):
                                if not by_vector[g][j]:
                                    u = 4 * g + j
                                    i = nc.scalar.activation(unit[:, u % RING, :], q[:, bass.ds(it // 3, 1), :].rearrange("p a t -> p (a t)"), ACT.Relu,
                                                             bias=nks[:, k, 16 * j + g:16 * j + g + 1], scale=1.0)
                            i.then_inc(s_ua, 1)
                            if prev:
                                if g == 6:
                                    exp(*prev)
                                if g == 12:
                                    chunks(*prev)
                                if g == 15 and prev[1] == 2:
                                    key_out(prev[0])

                def exp(it, k):
                    n = 36 * b + 3 * it + k
                    wait_apart(act, (s_w, NW), s_sub, n + 1)
                    nc.scalar.activation(e[:, k, :], e[:, k, :], ACT.Exp,
                                         bias=vb[:, bass.ds(3 * it + k, 1), S:S + 1].rearrange("p a n -> p (a n)"), scale=-SCALE,
                                         accum_out=z[:, k:k + 1]).then_inc(s_e, 1)

                def chunks(it, k):
                    n = 36 * b + 3 * it + k
                    act.wait_ge(s_t, n + 1)
                    nc.scalar.copy(at[:, k, 0:4, :].rearrange("p c r -> p (c r)"), turn[:]).then_inc(s_ata, 1)

                def key_out(it):
                    wait_apart(act, (s_w, NW), s_k, 12 * b + it + 1)
                    nc.scalar.copy(okt[:].rearrange("p h t -> p (h t)")[:, bass.ds(192 * it, 192)], score[:, 5, 288:480]).then_inc(s_kc, 1)

                def finish(it, k):
                    exp(it, k)
                    chunks(it, k)
                    key_out(it)

                trips(act, b, produce, finish)
                nc.scalar.copy(o_query_t[0:64, bass.ds(b, 1), 0:CUT].rearrange("p a t -> p (a t)"), acc[0:64, 0:CUT]).then_inc(s_acc, 1)
                nc.scalar.copy(o_query_t[64:128, bass.ds(b, 1), 0:T - CUT].rearrange("p a t -> p (a t)"), acc[64:128, 0:T - CUT]).then_inc(s_acc, 1)

        @block.tensor
        def _(pe):
            mm = nc.tensor.matmul
            pe.wait_ge(s_w, NW)
            pe.wait_ge(s_z1, 2)
            with pe.Fori(0, B) as b:
                def fill(n):
                    if n >= 6:
                        emptied(pe, b, n - 6)
                    return score[:, n % 6, :]

                def fill_after(n, read):
                    emptied(pe, b, n - 6, read)
                    return score[:, n % 6, :]

                pe.wait_ge(s_xs, b + 1)
                for n in range(2):
                    mm(fill(n)[:, 0:288], dup[:], xs[:, 288 * n:288 * n + 288], start=True, stop=True).then_inc(s_fill, 1)
                for n in range(2, 10):
                    hp, half = divmod(n - 2, 2)
                    mm(fill(n)[:, 0:288], wq[:, 128 * hp:128 * hp + 128], xs[:, 288 * half:288 * half + 288], start=True, stop=True).then_inc(s_fill, 1)
                for n in range(10, 15):
                    c = n - 10
                    rows = 128 if c < 4 else 64
                    mm(fill(n)[0:rows, :], xs[:, 128 * c:128 * c + rows], wvf[:], start=True, stop=True).then_inc(s_fill, 1)
                pe.wait_ge(s_xp, 2 * b + 2)
                for n in range(15, 24):
                    t0 = 64 * (n - 15)
                    out = fill(n)[:, 0:260]
                    mm(out, xpar[:, t0:t0 + 64, :].rearrange("p t h -> p (t h)"), wvb[:].rearrange("p a n -> p (a n)"), start=True, stop=True).then_inc(s_fill, 1)
                for n in range(QSUM, NF):
                    hp, half = divmod(n - QSUM, 2)
                    out = fill_after(n, QUERY + n - QSUM)
                    mm(out[:, 0:288], neg[:], q[:, hp, 288 * half:288 * half + 288], start=True, stop=True).then_inc(s_fill, 1)
                emptied(pe, b, *range(NF - 6, NF))

                def consume(it, first):
                    for k, prev in tiles(b, it, first):
                        n = 36 * b + 3 * it + k
                        if not first:
                            if k < 2:
                                pe.wait_ge(s_atv, n - 2)
                            else:
                                pe.wait_ge(s_kc, 12 * b + it)
                        for g in range(GROUPS):
                            pe.wait_ge(s_uv, n * GROUPS + g + 1)
                            pe.wait_ge(s_ua, n * GROUPS + g + 1)
                            for j in range(4):
                                u = 4 * g + j
                                for half in range(2):
                                    i = mm(score[32 * j:32 * j + 32, 2 * k + half, 0:288], sel[:, 30 - 2 * g:62 - 2 * g],
                                           unit[:, u % RING, 288 * half:288 * half + 288], start=(g == 0), stop=(g == GROUPS - 1),
                                           tile_position=(0, 32 * j), skip_group_check=True)
                            i.then_inc(s_use, 1)
                            if prev:
                                if g == 9:
                                    value_sums(*prev, first and k == 1)
                                if g == 13 and prev[1] == 2:
                                    key_sums(prev[0])

                def value_sums(it, k, fresh):
                    n = 36 * b + 3 * it + k
                    wait_apart(pe, (s_w, NW), s_vbs, n + 1)
                    wait_apart(pe, (s_w, NW), s_p, n + 1)
                    for p0, t0, t1 in ((0, 0, CUT), (64, CUT, T)):
                        mm(acc[p0:p0 + 64, 0:t1 - t0], vbs[:, k, :], e[:, k, t0:t1], start=fresh, stop=False, tile_position=(0, p0), skip_group_check=True)
                    for c in range(5):
                        rows = 128 if c < 4 else 64
                        out = turn[:, 128 * c:128 * c + 128] if c < 4 else score[0:64, 2 * k, 288:416]
                        i = nc.tensor.transpose(out, e[:, k, 128 * c:128 * c + rows], ident[:])
                    i.then_inc(s_t, 1)

                def key_sums(it):
                    wait_apart(pe, (s_w, NW), s_vfs, 12 * b + it + 1)
                    wait_apart(pe, (s_w, NW), s_ata, 36 * b + 3 * it + 3)
                    wait_apart(pe, (s_w, NW), s_atv, 36 * b + 3 * it + 3)
                    for c in range(5):
                        for h in range(2):
                            i = mm(score[64 * h:64 * h + 64, 5, 288:480], vfs[:, c, 64 * h:64 * h + 64], at[:, :, c, h:128:2],
                                   start=(c == 0), stop=(c == 4), tile_position=(0, 64 * h), skip_group_check=True)
                    i.then_inc(s_k, 1)

                def finish(it, k):
                    value_sums(it, k, False)
                    key_sums(it)

                trips(pe, b, consume, finish)
                pe.wait_ge(s_acc, 2 * b + 2)
                pe.wait_ge(s_kc, 12 * b + 12)


def fanin_stage(nc, d, res, xn, o_query_t, o_key_t, ident):
    PARTS = 4
    W = ROWS // PARTS
    BLOCKS = [(0, (0, 128), 0, 2), (0, (0, 64), 2, 3), (1, (64, 128), 2, 3), (1, (0, 128), 3, 4), (1, (0, 64), 4, 5)]
    with ExitStack() as ctx:
        def sb(n, shape, dt=F32):
            return ctx.enter_context(nc.sbuf_tensor("fan_" + n, shape, dt))

        def sem(n):
            return ctx.enter_context(nc.semaphore("fan_" + n))

        w = sb("w", [65, S]); fold = sb("fold", [128, S]); ex = sb("ex", [128, ROWS, S]); den = sb("den", [128, ROWS, S]); yt = sb("yt", [65, B, T])
        o = sb("o", [128, ROWS, S])
        back = ctx.enter_context(nc.psum_tensor("fan_back", [128, 2, 512], F32))
        turned = ctx.enter_context(nc.psum_tensor("fan_turned", [128, 2, 1024], F32))
        out = ctx.enter_context(nc.psum_tensor("fan_out", [128, 2, 512], F32))
        s_w = sem("w"); s_one = sem("one"); s_back = sem("back"); s_key = sem("key_part"); s_o = sem("o"); s_e = sem("e"); s_d = sem("denominator"); s_y = sem("y")
        s_t = sem("t"); s_yt = sem("yt"); s_out = sem("out"); s_x = sem("x"); s_res = sem("res")
        block = ctx.enter_context(nc.Block())

        @block.sync
        def _(sp):
            sp.dma_start(w[:], d["l1_fan"]).then_inc(s_w, 16)
            sp.dma_start(fold[:], d["c_fold"]).then_inc(s_w, 16)

        @block.gpsimd
        def _(pool):
            nc.gpsimd.memset(o[64:128, 4:ROWS:5, :], 0.0).then_inc(s_one, 1)
            pool.wait_ge(s_one, 1)
            nc.gpsimd.memset(yt[S:S + 1, :, :], 1.0).then_inc(s_one, 1)

        @block.vector
        def _(v):
            v.wait_ge(s_one, 1)
            for b in range(B):
                v.wait_ge(s_key, 2 * b + 2)
                for half, rows, c0, c1 in BLOCKS:
                    rows, chunks = slice(*rows), slice(5 * b + c0, 5 * b + c1)
                    i = nc.vector.tensor_tensor(o[rows, chunks, :], o[rows, chunks, :],
                                                back[rows, half, 64 * c0:64 * c1].rearrange("p (c f) -> p c f", f=S), ALU.add)
                i.then_inc(s_o, 1)
            v.wait_ge(s_o, B)
            for p in range(PARTS):
                r = slice(W * p, W * p + W)
                v.wait_ge(s_e, p + 1)
                nc.vector.tensor_scalar(den[:, r, :], ex[:, r, :], 1.0, None, ALU.add).then_inc(s_d, 1)
                v.wait_ge(s_d, 2 * p + 1)
                nc.vector.reciprocal(ex[:, r, :], den[:, r, :]).then_inc(s_d, 1)
                v.wait_ge(s_d, 2 * p + 2)
                nc.vector.tensor_tensor(o[:, r, :], o[:, r, :], ex[:, r, :], ALU.mult).then_inc(s_y, 1)
                nc.vector.tensor_tensor(res[:, r, :], res[:, r, :], xn[:, r, 0:S], ALU.add).then_inc(s_x, 1)
            v.wait_ge(s_x, PARTS)
            for b in range(B):
                v.wait_ge(s_out, b + 1)
                nc.vector.tensor_tensor(res[:, 5 * b:5 * b + 4, :], res[:, 5 * b:5 * b + 4, :],
                                        out[:, b % 2, 0:256].rearrange("p (c f) -> p c f", c=4), ALU.add).then_inc(s_res, 1)
                nc.vector.tensor_tensor(res[0:64, 5 * b + 4, :], res[0:64, 5 * b + 4, :], out[0:64, b % 2, 256:320], ALU.add).then_inc(s_res, 1)

        @block.scalar
        def _(act):
            act.wait_ge(s_one, 1)
            for b in range(B):
                act.wait_ge(s_back, b + 1)
                nc.scalar.copy(o[:, 5 * b:5 * b + 4, :].rearrange("p c f -> p (c f)"), out[:, 0, 0:256]).then_inc(s_key, 1)
                nc.scalar.copy(o[0:64, 5 * b + 4, :], out[0:64, 0, 256:320]).then_inc(s_key, 1)
            for p in range(PARTS):
                r = slice(W * p, W * p + W)
                act.wait_ge(s_o, 2 * p + 2)
                nc.scalar.activation(ex[:, r, :], o[:, r, :], ACT.Exp, scale=-1.702).then_inc(s_e, 1)
            for b in range(B):
                act.wait_ge(s_t, b + 1)
                nc.scalar.copy(yt[0:S, b, :], turned[0:S, b % 2, 0:T]).then_inc(s_yt, 1)

        @block.tensor
        def _(pe):
            pe.wait_ge(s_w, 32)
            pe.wait_ge(s_one, 2)
            for b in range(B):
                if b >= 1:
                    pe.wait_ge(s_o, b)
                for c in range(5):
                    n = min(128, T - 128 * c)
                    nc.tensor.matmul(out[0:n, 0, 64 * c:64 * c + 64], o_key_t[:, b, 128 * c:128 * c + n], fold[:], start=True, stop=True)
                for half, (p0, p1), c0, c1 in BLOCKS:
                    for c in range(c0, c1):
                        src = slice(64 * half, 64 * half + 64)
                        at = 128 * c + p0 - CUT * half
                        i = nc.tensor.matmul(back[p0:p1, half, 64 * c:64 * c + 64], o_query_t[src, b, at:at + p1 - p0], ident[src, src],
                                             start=True, stop=True, tile_position=(src.start, p0))
                i.then_inc(s_back, 1)
            for b in range(B + 1):
                if b < B:
                    pe.wait_ge(s_y, b // 2 + 1)
                    if b >= 2:
                        pe.wait_ge(s_yt, b - 1)
                    for c in range(5):
                        n = min(128, T - 128 * c)
                        i = nc.tensor.transpose(turned[0:S, b % 2, 128 * c:128 * c + n], o[0:n, 5 * b + c, :], ident[0:n, 0:n])
                    i.then_inc(s_t, 1)
                if b >= 1:
                    pe.wait_ge(s_yt, b)
                    if b >= 3:
                        pe.wait_ge(s_res, 2 * (b - 2))
                    for c in range(5):
                        n = min(128, T - 128 * c)
                        i = nc.tensor.matmul(out[0:n, (b - 1) % 2, 64 * c:64 * c + 64], yt[:, b - 1, 128 * c:128 * c + n], w[:], start=True, stop=True)
                    i.then_inc(s_out, 1)


def store_tokens(nc, out, res):
    with ExitStack() as ctx:
        s_out = ctx.enter_context(nc.semaphore("result_stored"))
        r4 = res[:].rearrange("p (b c) f -> p b c f", b=B)
        block = ctx.enter_context(nc.Block())

        @block.sync
        def _(sp):
            for c in range(4):
                sp.dma_start(out[:, 128 * c:128 * c + 128, :].rearrange("b t f -> t b f"), r4[:, :, c, :]).then_inc(s_out, 16)
            sp.dma_start(out[:, 512:576, :].rearrange("b t f -> t b f"), r4[0:64, :, 4, :]).then_inc(s_out, 16)
            sp.wait_ge(s_out, 16 * 5)


def slice_layout(i):
    wx, bx = np.asarray(i["L0_ffn_W_x"]), np.asarray(i["L0_ffn_b_x"])
    wx1 = np.concatenate([wx, bx[None]])
    return {
        "s_wx_t": wx1.reshape(65, 8, S).transpose(2, 1, 0).reshape(S, 8 * 65),
        "s_slice": i["L0_ffn_W_slice"],
        "s_bslice": np.broadcast_to(np.asarray(i["L0_ffn_b_slice"]), (1, 8, S)).reshape(1, 512),
        "s_temp": np.broadcast_to(np.asarray(i["L0_ffn_temperature"]).reshape(1, 8), (65, 8)),
        "s_wfx": np.concatenate([np.asarray(i["L0_ffn_W_fx"]), np.asarray(i["L0_ffn_b_fx"])[None]]),
        "s_wq": padded(i["L0_ffn_W_q"]), "s_wk": padded(i["L0_ffn_W_k"]),
        "s_wv_t": np.asarray(i["L0_ffn_W_v"]).T,
        "s_wout": np.asarray(i["L0_ffn_W_out"]).reshape(8, S, S).transpose(1, 0, 2).reshape(S, 512),
        "s_bout": np.broadcast_to(np.asarray(i["L0_ffn_b_out"]), (128, S)),
    }


def slice_stage(nc, d, res, xn, xt, ident):
    STEPS = [("logit", 5, "v"), ("turn_w", 5, "a"), ("pool", 1, "v"), ("turn_p", 1, "a"), ("token", 1, "v"), ("q", 1, "a"),
             ("k", 1, "v"), ("vo", 1, "a"), ("score", 1, "v"), ("turn_a", 1, "a"), ("ow", 1, "v"), ("out", 1, "v")]
    FIRST, OWNERS = {}, []
    for name, banks, owner in STEPS:
        for k in range(2):
            FIRST[name, k] = len(OWNERS)
            OWNERS += [owner] * banks
    ring = BankRing(OWNERS, 8)
    NF = len(OWNERS)
    assert NF % ring.size == 0
    with ExitStack() as ctx:
        def sb(n, shape, dt=F32):
            return ctx.enter_context(nc.sbuf_tensor("sl_" + n, shape, dt))

        def sem(n):
            return ctx.enter_context(nc.semaphore("sl_" + n))

        wx_t = sb("wx_t", [S, 8 * 65]); wslice = sb("wslice", [S, S]); bslice = sb("bslice", [65, 512]); temp = sb("temp", [65, 8])
        wfx = sb("wfx", [65, 512]); wq = sb("wq", [128, S]); wk = sb("wk", [128, S]); wv_t = sb("wv_t", [S, S]); wout = sb("wout", [S, 512])
        bout = sb("bout", [128, S]); rtemp = sb("rtemp", [65, 8]); wxs = sb("wxs", [128, 512]); wvo = sb("wvo", [S, 512])
        def pair(n, shape):
            return [sb(f"{n}{k}", shape) for k in range(2)]

        xs = pair("xs", [128, T]); mx = pair("mx", [128, 5, 8]); w = pair("w", [128, 5, 512]); sm = pair("sm", [128, 5, 8]); rs = pair("rs", [128, 5, 8])
        wt = pair("wt", [128, 4, T])
        nrm = pair("nrm", [128, 4]); rn = pair("rn", [128, 4]); pooled = pair("pooled", [128, 4, 65]); pt = pair("pt", [65, 512])
        tok = pair("tok", [128, 512]); qt = pair("qt", [S, 512]); kt = pair("kt", [S, 512]); vo = pair("vo", [S, 512])
        amx = pair("amx", [S, 8]); att = pair("att", [S, 512]); asm = pair("asm", [S, 8]); ars = pair("ars", [S, 8]); att_t = pair("att_t", [S, 512])
        ow = pair("ow", [128, 256])
        bank = ctx.enter_context(nc.psum_tensor("sl_bank", [128, ring.size, 512], F32))

        s_w = sem("weights"); s_zero = sem("padding"); s_pre = sem("pre_pe"); s_pv = sem("pre_v"); s_xs = sem("xs"); s_full = sem("full")
        s_ev = sem("emptied_v"); s_ea = sem("emptied_a"); s_mx = sem("max"); s_exp = sem("exp"); s_sum = sem("sum"); s_rs = sem("rsum")
        s_prob = sem("slice_weights"); s_nrm = sem("norm"); s_amx = sem("att_max"); s_aexp = sem("att_exp")
        s_asum = sem("att_sum"); s_att = sem("att"); s_res = sem("res")
        emptied_sem = {"v": s_ev, "a": s_ea}

        NW = 16 * (9 + 1)

        def emptied(eng, n, *fills):
            for who, count in ring.latest(fills):
                wait_apart(eng, (s_w, NW), emptied_sem[who], n * ring.per[who] + count)

        def heads(ap):
            return ap.rearrange("p (h g) -> p h g", h=8)

        def rows_of(c):
            return 128 if c < 4 else 64

        block = ctx.enter_context(nc.Block())
        loads = [(wx_t, "s_wx_t"), (wslice, "s_slice"), (temp, "s_temp"), (wfx, "s_wfx"), (wq, "s_wq"), (wk, "s_wk"), (wv_t, "s_wv_t"),
                 (wout, "s_wout"), (bout, "s_bout")]

        @block.sync
        def _(sp):
            for t, name in loads:
                sp.dma_start(t[:], d[name]).then_inc(s_w, 16)
            sp.dma_start(bslice[S:S + 1, :], d["s_bslice"]).then_inc(s_w, 16)

        @block.gpsimd
        def _(pool):
            nc.gpsimd.memset(wxs[S:128, :], 0.0).then_inc(s_zero, 1)
            pool.wait_ge(s_zero, 1)
            nc.gpsimd.memset(tok[0][S:128, :], 0.0).then_inc(s_zero, 1)
            pool.wait_ge(s_zero, 2)
            nc.gpsimd.memset(tok[1][S:128, :], 0.0).then_inc(s_zero, 1)

        @block.vector
        def _(v):
            v.wait_ge(s_w, NW)
            v.wait_ge(s_zero, 3)
            nc.vector.tensor_scalar(temp[:], temp[:], 0.1, 5.0, ALU.max, ALU.min).then_inc(s_pv, 1)
            v.wait_ge(s_pv, 1)
            nc.vector.reciprocal(rtemp[:], temp[:]).then_inc(s_pv, 1)
            v.wait_ge(s_pre, 1)
            nc.vector.tensor_copy(wxs[0:65, :], bank[0:65, 0, :]).then_inc(s_pv, 1)
            v.wait_ge(s_pv, 3)
            nc.vector.tensor_tensor(wxs[S:S + 1, :], wxs[S:S + 1, :], bslice[S:S + 1, :], ALU.add).then_inc(s_pv, 1)
            v.wait_ge(s_pv, 4)
            w3 = wxs[0:65, :].rearrange("p (h g) -> p h g", h=8)
            nc.vector.tensor_tensor(w3, w3, rtemp[:, :, None].broadcast_to([65, 8, S]), ALU.mult).then_inc(s_pv, 1)
            v.wait_ge(s_pre, 2)
            nc.vector.tensor_copy(wvo[:], bank[0:S, 1, :]).then_inc(s_pv, 1)
            nc.vector.tensor_tensor(res[:], res[:], bout[:, None, :].broadcast_to([128, ROWS, S]), ALU.add).then_inc(s_pv, 1)
            v.wait_ge(s_pv, 7)
            with v.Fori(0, B // 2) as n:
                for k in range(2):
                    nc.vector.tensor_copy(xs[k][:], xt[:, bass.ds(2 * n + k, 1), :].rearrange("p a t -> p (a t)")).then_inc(s_xs, 1)

                def got(name, k, c=0):
                    f = FIRST[name, k] + c
                    v.wait_ge(s_full, NF * n + f + 1)
                    return bank[:, f % ring.size, :]

                for k in range(2):
                    for c in range(5):
                        r = rows_of(c)
                        src = heads(got("logit", k, c)[0:r, :])
                        nc.vector.tensor_reduce(mx[k][0:r, c, :], src, AX, ALU.max).then_inc(s_mx, 1)
                        v.wait_ge(s_mx, 10 * n + 5 * k + c + 1)
                        nc.vector.tensor_tensor(heads(w[k][0:r, c, :]), src, mx[k][0:r, c, :, None].broadcast_to([r, 8, S]), ALU.subtract).then_inc(s_ev, 1)
                for k in range(2):
                    for c in range(5):
                        r = rows_of(c)
                        at = 10 * n + 5 * k + c + 1
                        v.wait_ge(s_exp, at)
                        nc.vector.tensor_reduce(sm[k][0:r, c, :], heads(w[k][0:r, c, :]), AX, ALU.add).then_inc(s_sum, 1)
                        v.wait_ge(s_sum, at)
                        nc.vector.reciprocal(rs[k][0:r, c, :], sm[k][0:r, c, :]).then_inc(s_rs, 1)
                        v.wait_ge(s_rs, at)
                        nc.vector.tensor_tensor(heads(w[k][0:r, c, :]), heads(w[k][0:r, c, :]), rs[k][0:r, c, :, None].broadcast_to([r, 8, S]),
                                                ALU.mult).then_inc(s_prob, 1)
                for k in range(2):
                    src = got("pool", k)[:, 0:260].rearrange("p (a n) -> p a n", a=4)
                    nc.vector.tensor_scalar(nrm[k][:], src[:, :, S], 1e-5, None, ALU.add).then_inc(s_nrm, 1)
                    v.wait_ge(s_nrm, 4 * n + 2 * k + 1)
                    nc.vector.reciprocal(rn[k][:], nrm[k][:]).then_inc(s_nrm, 1)
                    v.wait_ge(s_nrm, 4 * n + 2 * k + 2)
                    nc.vector.tensor_tensor(pooled[k][:], src, rn[k][:, :, None].broadcast_to([128, 4, 65]), ALU.mult).then_inc(s_ev, 1)
                for k in range(2):
                    nc.vector.tensor_copy(tok[k][0:S, :], got("token", k)[0:S, :]).then_inc(s_ev, 1)
                for k in range(2):
                    nc.vector.tensor_copy(kt[k][:], got("k", k)[0:S, :]).then_inc(s_ev, 1)
                for k in range(2):
                    src = heads(got("score", k)[0:S, :])
                    nc.vector.tensor_reduce(amx[k][:], src, AX, ALU.max).then_inc(s_amx, 1)
                    v.wait_ge(s_amx, 2 * n + k + 1)
                    nc.vector.tensor_tensor(heads(att[k][:]), src, amx[k][:, :, None].broadcast_to([S, 8, S]), ALU.subtract).then_inc(s_ev, 1)
                for k in range(2):
                    v.wait_ge(s_aexp, 2 * n + k + 1)
                    nc.vector.tensor_reduce(asm[k][:], heads(att[k][:]), AX, ALU.add).then_inc(s_asum, 1)
                    v.wait_ge(s_asum, 4 * n + 2 * k + 1)
                    nc.vector.reciprocal(ars[k][:], asm[k][:]).then_inc(s_asum, 1)
                    v.wait_ge(s_asum, 4 * n + 2 * k + 2)
                    nc.vector.tensor_tensor(heads(att[k][:]), heads(att[k][:]), ars[k][:, :, None].broadcast_to([S, 8, S]), ALU.mult).then_inc(s_att, 1)
                for k in range(2):
                    nc.vector.tensor_copy(ow[k][:], got("ow", k)[:, 0:256]).then_inc(s_ev, 1)
                for k in range(2):
                    src = got("out", k)
                    r = res[:, bass.ds(10 * n + 5 * k, 4), :]
                    nc.vector.tensor_tensor(r, r, src[:, 0:256].rearrange("p (c f) -> p c f", c=4), ALU.add).then_inc(s_res, 1)
                    r = res[0:64, bass.ds(10 * n + 5 * k + 4, 1), :].rearrange("p c f -> p (c f)")
                    nc.vector.tensor_tensor(r, r, src[0:64, 256:320], ALU.add).then_inc(s_ev, 1)

        @block.scalar
        def _(act):
            with act.Fori(0, B // 2) as n:
                def got(name, k, c=0):
                    f = FIRST[name, k] + c
                    act.wait_ge(s_full, NF * n + f + 1)
                    return bank[:, f % ring.size, :]

                for k in range(2):
                    for c in range(5):
                        act.wait_ge(s_ev, ring.per["v"] * n + 5 * k + c + 1)
                        nc.scalar.activation(w[k][0:rows_of(c), c, :], w[k][0:rows_of(c), c, :], ACT.Exp).then_inc(s_exp, 1)
                for k in range(2):
                    for c in range(5):
                        r = rows_of(c)
                        nc.scalar.copy(wt[k][:, :, 128 * c:128 * c + r], got("turn_w", k, c).rearrange("p (a r) -> p a r", a=4)[:, :, 0:r]).then_inc(s_ea, 1)
                for k in range(2):
                    nc.scalar.copy(pt[k][:], got("turn_p", k)[0:65, :]).then_inc(s_ea, 1)
                for k in range(2):
                    nc.scalar.copy(qt[k][:], got("q", k)[0:S, :]).then_inc(s_ea, 1)
                for k in range(2):
                    nc.scalar.copy(vo[k][:], got("vo", k)[0:S, :]).then_inc(s_ea, 1)
                for k in range(2):
                    who, count = ring.emptied(FIRST["score", k])
                    act.wait_ge(s_ev, ring.per["v"] * n + count)
                    nc.scalar.activation(att[k][:], att[k][:], ACT.Exp, scale=1.0 / 8.0).then_inc(s_aexp, 1)
                for k in range(2):
                    nc.scalar.copy(att_t[k][:], got("turn_a", k)[0:S, :]).then_inc(s_ea, 1)

        @block.tensor
        def _(pe):
            mm, turn = nc.tensor.matmul, nc.tensor.transpose
            pe.wait_ge(s_w, NW)
            for h in range(8):
                i = mm(bank[0:65, 0, 64 * h:64 * h + 64], wx_t[:, 65 * h:65 * h + 65], wslice[:], start=True, stop=True)
            i.then_inc(s_pre, 1)
            mm(bank[0:S, 1, :], wv_t[:], wout[:], start=True, stop=True).then_inc(s_pre, 1)
            pe.wait_ge(s_pv, 7)
            with pe.Fori(0, B // 2) as n:
                def fill(name, k, c=0, reads=()):
                    f = FIRST[name, k] + c
                    emptied(pe, n, *[FIRST[r, k] for r in reads], *([f - ring.size] if f >= ring.size else []))
                    return bank[:, f % ring.size, :]

                def of_head(a, h):
                    return a[:, 64 * h:64 * h + 64]

                for k in range(2):
                    wait_apart(pe, (s_w, NW), s_xs, 2 * n + k + 1)
                    for c in range(5):
                        mm(fill("logit", k, c)[0:rows_of(c), :], xs[k][:, 128 * c:128 * c + rows_of(c)], wxs[:], start=True, stop=True).then_inc(s_full, 1)
                for k in range(2):
                    for c in range(5):
                        r = rows_of(c)
                        wait_apart(pe, (s_w, NW), s_prob, 10 * n + 5 * k + c + 1)
                        out = fill("turn_w", k, c)
                        for hp in range(4):
                            i = turn(out[:, 128 * hp:128 * hp + r], w[k][0:r, c, 128 * hp:128 * hp + 128], ident[0:r, 0:r])
                        i.then_inc(s_full, 1)
                for k in range(2):
                    out = fill("pool", k)
                    for hp in range(4):
                        for c in range(5):
                            r = rows_of(c)
                            i = mm(out[:, 65 * hp:65 * hp + 65], w[k][0:r, c, 128 * hp:128 * hp + 128],
                                   xn[0:r, bass.ds(10 * n + 5 * k + c, 1), :].rearrange("p a n -> p (a n)"), start=(c == 0), stop=(c == 4))
                    i.then_inc(s_full, 1)
                for k in range(2):
                    out = fill("turn_p", k, reads=["pool"])
                    for hp in range(4):
                        i = turn(out[0:65, 128 * hp:128 * hp + 128], pooled[k][:, hp, :], ident[:])
                    i.then_inc(s_full, 1)
                for k in range(2):
                    out = fill("token", k, reads=["turn_p"])
                    for h in range(8):
                        i = mm(of_head(out[0:S, :], h), of_head(wfx, h), of_head(pt[k], h), start=True, stop=True)
                    i.then_inc(s_full, 1)
                for k in range(2):
                    mm(fill("q", k, reads=["token"])[0:S, :], wq[:], tok[k][:], start=True, stop=True).then_inc(s_full, 1)
                for k in range(2):
                    mm(fill("k", k)[0:S, :], wk[:], tok[k][:], start=True, stop=True).then_inc(s_full, 1)
                for k in range(2):
                    out = fill("vo", k)
                    for h in range(8):
                        i = mm(of_head(out[0:S, :], h), of_head(tok[k][0:S, :], h), of_head(wvo, h), start=True, stop=True)
                    i.then_inc(s_full, 1)
                for k in range(2):
                    out = fill("score", k, reads=["q", "k"])
                    for h in range(8):
                        i = mm(of_head(out[0:S, :], h), of_head(qt[k], h), of_head(kt[k], h), start=True, stop=True)
                    i.then_inc(s_full, 1)
                for k in range(2):
                    wait_apart(pe, (s_w, NW), s_att, 2 * n + k + 1)
                    out = fill("turn_a", k)
                    for h in range(8):
                        i = turn(of_head(out[0:S, :], h), of_head(att[k], h), ident[0:S, 0:S])
                    i.then_inc(s_full, 1)
                for k in range(2):
                    out = fill("ow", k, reads=["turn_a", "vo"])
                    for h in range(8):
                        p0 = 64 * (h % 2)
                        i = mm(of_head(out[p0:p0 + 64, :], h // 2), of_head(att_t[k], h), of_head(vo[k], h), start=True, stop=True, tile_position=(0, p0))
                    i.then_inc(s_full, 1)
                for k in range(2):
                    out = fill("out", k, reads=["ow"])
                    for c in range(5):
                        r = rows_of(c)
                        for hp in range(4):
                            i = mm(out[0:r, 64 * c:64 * c + 64], wt[k][:, hp, 128 * c:128 * c + r], ow[k][:, 64 * hp:64 * hp + 64],
                                   start=(hp == 0), stop=(hp == 3))
                    i.then_inc(s_full, 1)


def mqa_layout(i):
    wv = np.asarray(i["L1_attn_Wv"]).T
    return {"m_wq": padded(np.asarray(i["L1_attn_Wq"]).T), "m_wk": padded(np.asarray(i["L1_attn_Wk"]).T),
            "m_wv": padded(np.concatenate([wv, wv], 1)),
            "m_wo": np.asarray(i["L1_attn_Wo"]).T.reshape(4, 128, S).transpose(1, 0, 2).reshape(128, 256)}


def mqa_stage(nc, d, xt, ctx_dram, ident):
    SCALE = 1.0 / np.sqrt(8.0)
    UNITS = 40
    OWNERS = ["v", "v"] + ["a", "v", "a", "v"] + ["a"] * UNITS
    K, V, Q, SCORE = 0, 1, 2, 6
    ring = BankRing(OWNERS, 2)
    NF = len(OWNERS)
    CHUNKS = [(0, 128), (128, 256), (256, CUT), (CUT, CUT + 128), (CUT + 128, T)]
    TURN_LAG, CTX_LAG, COPY_LAG, BACK_LAG, NORM_LAG = 2, 3, 7, 8, 9
    CTX_PARTS = [(0,), (1,), (2,), (3, 4)]
    with ExitStack() as ctx:
        def sb(n, shape, dt=F32):
            return ctx.enter_context(nc.sbuf_tensor("mq_" + n, shape, dt))

        def sem(n):
            return ctx.enter_context(nc.semaphore("mq_" + n))

        wq = sb("wq", [128, 512]); wk = sb("wk", [128, S]); wv = sb("wv", [128, 128])
        keys = sb("keys", [128, 9, S]); q = sb("q", [128, 8, T]); vals = sb("vals", [128, 5, S])
        mx = sb("mx", [128, UNITS]); nmx = sb("nmx", [128, UNITS]); z = sb("z", [128, UNITS]); rz = sb("rz", [128, UNITS])
        p = sb("p", [128, 3, T]); pt = sb("pt", [128, 2, 5, T]); ct = sb("ct", [128, 2, CUT]); c_out = sb("c_out", [128, 5, 512])
        wide = ctx.enter_context(nc.psum_tensor("mq_wide", [128, 2, 2, 512], F32))
        turned = ctx.enter_context(nc.psum_tensor("mq_turned", [128, 2, 512], F32))
        cx = ctx.enter_context(nc.psum_tensor("mq_cx", [128, 512], F32))
        back = ctx.enter_context(nc.psum_tensor("mq_back", [128, 512], F32))
        s_w = sem("weights"); s_init = sem("init"); s_full = sem("full"); s_ev = sem("emptied_v"); s_ea = sem("emptied_a")
        s_mx = sem("max"); s_nmx = sem("minus_max"); s_turn = sem("probs_turned")
        s_pa = sem("pt_a"); s_pv = sem("pt_v"); s_cx = sem("context"); s_ct = sem("context_copied"); s_back = sem("context_turned"); s_rz = sem("rz"); s_cn = sem("context_normed")
        s_store = sem("context_stored")
        emptied_sem = {"v": s_ev, "a": s_ea}

        def emptied(eng, b, *fills):
            for who, count in ring.latest(fills):
                wait_apart(eng, (s_w, 48), emptied_sem[who], b * ring.per[who] + count)

        def keys_of(j):
            return 128 if j < 4 else 64

        def rows_of(c):
            return CHUNKS[c][1] - CHUNKS[c][0]

        def head_at(n, lag):
            h, c = divmod(n - lag, 5)
            return h if 0 <= h < 8 and c == 4 else None

        block = ctx.enter_context(nc.Block())

        @block.sync
        def _(sp):
            for t, name in ((wq, "m_wq"), (wk, "m_wk"), (wv, "m_wv")):
                sp.dma_start(t[:], d[name]).then_inc(s_w, 16)
            with sp.Fori(0, B) as b:
                sp.wait_ge(s_cn, 8 * b + 8)
                sp.dma_start(ctx_dram[bass.ds(b, 1), 0:256, :].rearrange("a (c p) n -> p (a c) n", p=128), c_out[:, 0:2, :]).then_inc(s_store, 16)
                sp.dma_start(ctx_dram[bass.ds(b, 1), 256:CUT, :].rearrange("a p n -> p (a n)"), c_out[0:64, 2, :]).then_inc(s_store, 16)
                sp.dma_start(ctx_dram[bass.ds(b, 1), CUT:T, :].rearrange("a (c p) n -> p (a c) n", p=128), c_out[:, 3:5, :]).then_inc(s_store, 16)
            sp.wait_ge(s_store, 48 * B + 16)

        @block.gpsimd
        def _(pool):
            for n, t in enumerate((keys[S:128, :, :], q[S:128, :, :])):
                if n:
                    pool.wait_ge(s_init, n)
                nc.gpsimd.memset(t, 0.0).then_inc(s_init, 1)
            pool.wait_ge(s_init, 2)
            nc.gpsimd.memset(z[:], 1.0).then_inc(s_init, 1)
            pool.wait_ge(s_init, 3)
            nc.gpsimd.memset(c_out[:, 0, 0:1], 0.0).then_inc(s_store, 16)

        @block.vector
        def _(v):
            v.wait_ge(s_init, 3)
            with v.Fori(0, B) as b:
                def got(n):
                    v.wait_ge(s_full, NF * b + n + 1)
                    return wide[:, n % 2, :, :]

                k4 = keys[0:S, :, :].rearrange("p j (a o) -> p a j o", a=2)
                src = got(K)
                nc.vector.tensor_copy(k4[:, 0], src[0:S, 0, 0:288].rearrange("p (o j) -> p j o", j=9))
                nc.vector.tensor_copy(k4[:, 1], src[0:S, 1, 0:288].rearrange("p (o j) -> p j o", j=9)).then_inc(s_ev, 1)
                src = got(V)
                a = src[:, 0, 0:320].rearrange("p (j f) -> p j f", j=5)
                c = src[:, 1, 0:256].rearrange("p (j f) -> p j f", j=4)
                nc.vector.tensor_copy(vals[0:64, 0:3, :], a[0:64, 0:5:2, :])
                nc.vector.tensor_copy(vals[64:128, 0:2, :], a[64:128, 1:5:2, :])
                nc.vector.tensor_copy(vals[0:64, 3:5, :], c[0:64, 1:4:2, :])
                nc.vector.tensor_copy(vals[64:128, 2:4, :], c[64:128, 0:4:2, :]).then_inc(s_ev, 1)
                for hp in (1, 3):
                    src = got(Q + hp)
                    q3 = q[0:S, 2 * hp:2 * hp + 2, :].rearrange("p h (a t) -> p h a t", a=2)
                    nc.vector.tensor_copy(q3[:, 0], src[0:64, :, 0:288])
                    nc.vector.tensor_copy(q3[:, 1], src[64:128, :, 0:288]).then_inc(s_ev, 1)

                for n in range(UNITS + NORM_LAG):
                    if n < UNITS:
                        r = rows_of(n % 5)
                        nc.vector.tensor_reduce(mx[0:r, n:n + 1], got(SCORE + n)[0:r, :, 0:288], mybir.AxisListType.XY, ALU.max).then_inc(s_mx, 1)
                        v.wait_ge(s_mx, UNITS * b + n + 1)
                        nc.vector.tensor_scalar(nmx[0:r, n:n + 1], mx[0:r, n:n + 1], -float(SCALE), None, ALU.mult).then_inc(s_nmx, 1)
                    m = n - TURN_LAG
                    if 0 <= m < UNITS:
                        r = rows_of(m % 5)
                        v.wait_ge(s_turn, UNITS * b + m + 1)
                        nc.vector.tensor_copy(pt[0:64, m // 5 % 2, 4, slice(*CHUNKS[m % 5])], turned[0:64, 1, 0:r]).then_inc(s_pv, 1)
                    h = head_at(n, NORM_LAG)
                    if h is not None:
                        if h == 0:
                            v.wait_ge(s_store, 48 * b + 16)
                        v.wait_ge(s_back, 8 * b + h + 1)
                        nc.vector.reciprocal(rz[:, 5 * h:5 * h + 5], z[:, 5 * h:5 * h + 5]).then_inc(s_rz, 1)
                        v.wait_ge(s_rz, 24 * b + 3 * h + 1)
                        src = back[:, 0:256].rearrange("p (i half n) -> p i half n", i=2, half=2)
                        for half in range(2):
                            c = 3 * half
                            nc.vector.tensor_tensor(c_out[:, c:c + 2, 64 * h:64 * h + 64], src[:, :, half, :],
                                                    rz[:, 5 * h + c:5 * h + c + 2, None].broadcast_to([128, 2, S]), ALU.mult).then_inc(s_rz, 1)
                        nc.vector.tensor_scalar(c_out[0:64, 2, 64 * h:64 * h + 64], back[0:64, 256:320], rz[0:64, 5 * h + 2:5 * h + 3], None, ALU.mult).then_inc(s_cn, 1)

        @block.scalar
        def _(act):
            act.wait_ge(s_init, 3)
            with act.Fori(0, B) as b:
                def got(n):
                    act.wait_ge(s_full, NF * b + n + 1)
                    return wide[:, n % 2, :, :]

                for hp in (0, 2):
                    src = got(Q + hp)
                    q3 = q[0:S, 2 * hp:2 * hp + 2, :].rearrange("p h (a t) -> p h a t", a=2)
                    nc.scalar.copy(q3[:, 0], src[0:64, :, 0:288])
                    nc.scalar.copy(q3[:, 1], src[64:128, :, 0:288]).then_inc(s_ea, 1)
                for n in range(UNITS + COPY_LAG):
                    m = n - TURN_LAG
                    if 0 <= m < UNITS:
                        r = rows_of(m % 5)
                        act.wait_ge(s_turn, UNITS * b + m + 1)
                        nc.scalar.copy(pt[:, m // 5 % 2, 0:4, slice(*CHUNKS[m % 5])], turned[:, 0, :].rearrange("p (j s) -> p j s", j=4)[:, :, 0:r]).then_inc(s_pa, 1)
                    if n < UNITS:
                        r = rows_of(n % 5)
                        if n >= 3:
                            wait_apart(act, (s_w, 48), s_turn, UNITS * b + n - 2)
                        act.wait_ge(s_nmx, UNITS * b + n + 1)
                        nc.scalar.activation(p[0:r, n % 3, :].rearrange("p (a t) -> p a t", a=2), wide[0:r, (SCORE + n) % 2, :, 0:288], ACT.Exp,
                                             bias=nmx[0:r, n:n + 1], scale=float(SCALE), accum_out=z[0:r, n:n + 1]).then_inc(s_ea, 1)
                    h = head_at(n, COPY_LAG)
                    if h is not None:
                        act.wait_ge(s_cx, 8 * b + h + 1)
                        nc.scalar.copy(ct[:, h % 2, 0:T - CUT], cx[:, 0:T - CUT])
                        nc.scalar.copy(ct[0:64, h % 2, T - CUT:CUT], cx[0:64, T - CUT:CUT]).then_inc(s_ct, 1)

        @block.tensor
        def _(pe):
            mm = nc.tensor.matmul
            pe.wait_ge(s_w, 48)
            pe.wait_ge(s_init, 3)
            with pe.Fori(0, B) as b:
                def fill(n, reads=()):
                    emptied(pe, b, *reads, *([n - 2] if n >= 2 else []))
                    return wide[:, n % 2, :, :]

                def halves(out, lhs, rhs, cut=288):
                    mm(out[:, 0, 0:cut], lhs, rhs(0, cut), start=True, stop=True)
                    mm(out[:, 1, 0:T - cut], lhs, rhs(cut, T), start=True, stop=True).then_inc(s_full, 1)

                def x(t0, t1):
                    return xt[:, bass.ds(b, 1), t0:t1].rearrange("p a t -> p (a t)")

                halves(fill(K)[0:S], wk[:], x)
                halves(fill(V), wv[:], x, cut=320)
                for hp in range(4):
                    halves(fill(Q + hp), wq[:, 128 * hp:128 * hp + 128], x)
                flat = keys[:].rearrange("p j o -> p (j o)")
                for n in range(UNITS + BACK_LAG):
                    if n < UNITS:
                        h, c = divmod(n, 5)
                        reads = ([K] if n == 0 else []) + ([Q + h // 2] if c == 0 and h % 2 == 0 else [])
                        halves(fill(SCORE + n, reads)[0:rows_of(c)], q[:, h, slice(*CHUNKS[c])], lambda t0, t1: flat[:, t0:t1])
                    m = n - TURN_LAG
                    if 0 <= m < UNITS:
                        r = rows_of(m % 5)
                        emptied(pe, b, SCORE + m)
                        if m >= 1:
                            wait_apart(pe, (s_w, 48), s_pa, UNITS * b + m)
                            wait_apart(pe, (s_w, 48), s_pv, UNITS * b + m)
                        for j in range(4):
                            nc.tensor.transpose(turned[:, 0, 128 * j:128 * j + r], p[0:r, m % 3, 128 * j:128 * j + 128], ident[0:r, 0:r])
                        nc.tensor.transpose(turned[0:64, 1, 0:r], p[0:r, m % 3, 512:576], ident[0:r, 0:r]).then_inc(s_turn, 1)
                    for part, chunks in enumerate(CTX_PARTS):
                        h = head_at(n, CTX_LAG + part)
                        if h is None:
                            continue
                        if part == 0:
                            wait_apart(pe, (s_w, 48), s_pa, UNITS * b + 5 * h + 5)
                            wait_apart(pe, (s_w, 48), s_pv, UNITS * b + 5 * h + 5)
                            if h >= 1:
                                wait_apart(pe, (s_w, 48), s_ct, 8 * b + h)
                        for j in chunks:
                            for p0, t0, t1 in ((0, 0, CUT), (64, CUT, T)):
                                i = mm(cx[p0:p0 + 64, 0:t1 - t0], vals[0:keys_of(j), j, :], pt[0:keys_of(j), h % 2, j, t0:t1],
                                       start=(j == 0), stop=(j == 4), tile_position=(0, p0), skip_group_check=True)
                        if part == len(CTX_PARTS) - 1:
                            i.then_inc(s_cx, 1)
                    h = head_at(n, BACK_LAG)
                    if h is not None:
                        wait_apart(pe, (s_w, 48), s_ct, 8 * b + h + 1)
                        if h >= 1:
                            wait_apart(pe, (s_w, 48), s_cn, 8 * b + h)
                        for k in range(2):
                            nc.tensor.transpose(back[:, 128 * k:128 * k + 128], ct[:, h % 2, 128 * k:128 * k + 128], ident[:])
                        nc.tensor.transpose(back[0:64, 256:320], ct[0:64, h % 2, 256:CUT], ident[0:64, 0:64]).then_inc(s_back, 1)


def mqa_out_stage(nc, d, ctx_dram, res):
    with ExitStack() as ctx:
        def sem(n):
            return ctx.enter_context(nc.semaphore("mo_" + n))

        wo = ctx.enter_context(nc.sbuf_tensor("mo_wo", [128, 256], F32))
        cr = ctx.enter_context(nc.sbuf_tensor("mo_cr", [128, 2, 4, T], F32))
        out = ctx.enter_context(nc.psum_tensor("mo_out", [128, 2, 512], F32))
        s_w = sem("weights"); s_c = [sem("context0"), sem("context1")]; s_out = sem("out"); s_res = sem("res")
        view = ctx_dram.rearrange("b s n -> b (s n)").rearrange("b (i p t) -> b p i t", p=128, t=T)
        block = ctx.enter_context(nc.Block())

        @block.sync
        def _(sp):
            sp.dma_start(wo[:], d["m_wo"]).then_inc(s_w, 16)
            for k in range(2):
                sp.dma_start(cr[:, k], view[k]).then_inc(s_c[k], 16)
            with sp.Fori(1, B // 2) as n:
                for k in range(2):
                    sp.wait_ge(s_out, 2 * n + k - 1)
                    sp.dma_start(cr[:, k], view[bass.ds(2 * n + k, 1)].rearrange("a p i t -> p (a i) t")).then_inc(s_c[k], 16)

        @block.vector
        def _(v):
            with v.Fori(0, B // 2) as n:
                for k in range(2):
                    v.wait_ge(s_out, 2 * n + k + 1)
                    r = res[:, bass.ds(10 * n + 5 * k, 4), :]
                    nc.vector.tensor_tensor(r, r, out[:, k, 0:256].rearrange("p (c f) -> p c f", c=4), ALU.add).then_inc(s_res, 1)
                    r = res[0:64, bass.ds(10 * n + 5 * k + 4, 1), :].rearrange("p c f -> p (c f)")
                    nc.vector.tensor_tensor(r, r, out[0:64, k, 256:320], ALU.add).then_inc(s_res, 1)

        @block.tensor
        def _(pe):
            pe.wait_ge(s_w, 16)

            def pair(n, first):
                for k in range(2):
                    pe.wait_ge(s_c[k], 16 * (n + 1))
                    if not first:
                        pe.wait_ge(s_res, 4 * n + 2 * k - 2)
                    for c in range(5):
                        rows = 128 if c < 4 else 64
                        for i4 in range(4):
                            i = nc.tensor.matmul(out[0:rows, k, 64 * c:64 * c + 64], cr[:, k, i4, 128 * c:128 * c + rows],
                                                 wo[:, 64 * i4:64 * i4 + 64], start=(i4 == 0), stop=(i4 == 3))
                    i.then_inc(s_out, 1)

            pair(0, True)
            with pe.Fori(1, B // 2) as n:
                pair(n, False)


def moe_layout(i):
    a = {"e_sw1": padded(i["L1_ffn_sW1"]), "e_sw2": padded(i["L1_ffn_sW2"]), "e_sw3": i["L1_ffn_sW3"]}
    a["e_sb1"] = np.asarray(i["L1_ffn_sb1"])[:, None]
    a["e_sb2"] = np.asarray(i["L1_ffn_sb2"])[:, None]
    a["e_sb3"] = np.broadcast_to(np.asarray(i["L1_ffn_sb3"]), (128, S))
    a["e_w1"] = padded(np.asarray(i["L1_ffn_eW1"]).transpose(1, 0, 2).reshape(S, 512))
    a["e_b1"] = np.asarray(i["L1_ffn_eb1"]).T
    a["e_w2"] = np.asarray(i["L1_ffn_eW2"]).transpose(1, 0, 2).reshape(128, 256)
    a["e_b2"] = np.asarray(i["L1_ffn_eb2"]).T
    w3 = np.concatenate([np.asarray(i["L1_ffn_eW3"]), np.asarray(i["L1_ffn_eb3"])[:, None]], 1)
    a["e_w3"] = padded(w3.transpose(1, 0, 2).reshape(65, 256))
    a["e_gate"] = padded(np.concatenate([np.asarray(i["L1_ffn_gW"]), np.asarray(i["L1_ffn_gb"])[None]]))
    return a


def moe_constants():
    return {"c_before": np.broadcast_to(np.tril(np.ones((4, 4)), -1).reshape(1, 16), (128, 16)).astype(np.float32)}


def moe_stage(nc, d, res, xt):
    NAMES = ["shared1", "e1_0", "shared2", "e1_1", "e2_0", "e1_2", "e2_1", "e1_3", "e2_2", "e2_3"] + [f"out{c}" for c in range(5)]
    OWNERS = ["a" if n.startswith("e1") or n == "shared1" else "v" for n in NAMES]
    FILL = {name: n for n, name in enumerate(NAMES)}
    ring = BankRing(OWNERS, 3)
    NF = len(OWNERS)
    assert NF % ring.size == 0
    with ExitStack() as ctx:
        def sb(n, shape, dt=F32):
            return ctx.enter_context(nc.sbuf_tensor("me_" + n, shape, dt))

        def sem(n):
            return ctx.enter_context(nc.semaphore("me_" + n))

        sw1 = sb("sw1", [128, S]); sw2 = sb("sw2", [128, 128]); sw3 = sb("sw3", [128, S]); sb1 = sb("sb1", [S, 1]); sb2 = sb("sb2", [128, 1])
        sb3 = sb("sb3", [128, S]); w1 = sb("w1", [128, 512]); b1 = sb("b1", [128, 4]); w2 = sb("w2", [128, 256]); b2 = sb("b2", [S, 4])
        w3 = sb("w3", [128, 256]); gate = sb("gate", [128, 4]); before = sb("before", [128, 4, 4])
        h1 = sb("h1", [128, T]); h2 = sb("h2", [128, T]); g1 = sb("g1", [128, 2, T]); g2 = sb("g2", [128, 4, T])
        gl = sb("gl", [128, ROWS, 4]); gm = sb("gm", [128, ROWS]); gc = sb("gc", [128, ROWS, 4]); ge = sb("ge", [128, ROWS, 4])
        gs = sb("gs", [128, ROWS]); gr = sb("gr", [128, ROWS]); gp = sb("gp", [128, ROWS, 4])
        eq = sb("eq", [128, ROWS, 4, 4]); gt = sb("gt", [128, ROWS, 4, 4])
        rank = sb("rank", [128, ROWS, 4]); top = sb("top", [128, ROWS, 4]); tm = sb("tm", [128, ROWS]); tc = sb("tc", [128, ROWS, 4])
        te = sb("te", [128, ROWS, 4]); ts = sb("ts", [128, ROWS]); tr = sb("tr", [128, ROWS]); tw = sb("tw", [128, ROWS, 5])
        mixed = sb("mixed", [128, 2, 5, S]); msum = sb("msum", [128, 2, S])
        wide = ctx.enter_context(nc.psum_tensor("me_wide", [128, 3, 2, 512], F32))
        gates = ctx.enter_context(nc.psum_tensor("me_gates", [128, 512], F32))
        s_w = sem("weights"); s_one = sem("ones"); s_full = sem("full"); s_ev = sem("emptied_v"); s_ea = sem("emptied_a")
        s_gf = sem("gates_full"); s_g = sem("gates_v"); s_ga = sem("gates_a"); s_mix = sem("mix"); s_res = sem("res")
        emptied_sem = {"v": s_ev, "a": s_ea}

        NW = 16 * 13

        def emptied(eng, b, *fills):
            for who, count in ring.latest(fills):
                wait_apart(eng, (s_w, NW), emptied_sem[who], b * ring.per[who] + (ring.per[who] + count))

        block = ctx.enter_context(nc.Block())
        loads = [(gate, "e_gate"), (sw1, "e_sw1"), (w1, "e_w1"), (sw2, "e_sw2"), (sw3, "e_sw3"), (sb1, "e_sb1"), (sb2, "e_sb2"),
                 (sb3, "e_sb3"), (b1, "e_b1"), (w2, "e_w2"), (b2, "e_b2"), (w3, "e_w3")]
        assert NW == 16 * (len(loads) + 1)

        @block.sync
        def _(sp):
            for t, name in loads:
                sp.dma_start(t[:], d[name]).then_inc(s_w, 16)
            sp.dma_start(before[:], d["c_before"].rearrange("p (i j) -> p i j", i=4)).then_inc(s_w, 16)

        @block.gpsimd
        def _(pool):
            fills = [(gl[:], 0.0), (h1[S:128, :], 0.0), (g2[S:128, :, :], 0.0), (g2[S:S + 1, :, :], 1.0), (tw[:, :, 0:1], 1.0)]
            for n, (t, value) in enumerate(fills):
                if n:
                    pool.wait_ge(s_one, n)
                nc.gpsimd.memset(t, value).then_inc(s_one, 1)
            pool.wait_ge(s_one, 5)
            nc.gpsimd.memset(msum[:, 0, 0:1], 0.0).then_inc(s_ev, ring.per["v"])
            nc.gpsimd.memset(msum[:, 1, 0:1], 0.0).then_inc(s_ea, ring.per["a"])

        @block.vector
        def _(v):
            v.wait_ge(s_w, NW)
            v.wait_ge(s_one, 5)
            v.wait_ge(s_ea, ring.per["a"])
            nc.vector.tensor_tensor(res[:], res[:], sb3[:, None, :].broadcast_to([128, ROWS, S]), ALU.add).then_inc(s_res, 1)
            step = [0]

            def done(i):
                i.then_inc(s_g, 1)
                step[0] += 1
                v.wait_ge(s_g, step[0])

            def over_experts(a):
                return a[:, :, None].broadcast_to([128, ROWS, 4])

            v.wait_ge(s_gf, 1)
            src = gates[:, 0:4 * ROWS].rearrange("p (b c e) -> p b c e", b=B, e=4)
            g4 = gl[:].rearrange("p (b c) e -> p b c e", b=B)
            done(nc.vector.tensor_copy(g4[:, :, 0:4, :], src[:, :, 0:4, :]))
            done(nc.vector.tensor_copy(g4[0:64, :, 4, :], src[0:64, :, 4, :]))
            done(nc.vector.tensor_reduce(gm[:], gl[:], AX, ALU.max))
            done(nc.vector.tensor_tensor(gc[:], gl[:], over_experts(gm), ALU.subtract))
            CENTRED = step[0]
            v.wait_ge(s_ga, 1)
            done(nc.vector.tensor_reduce(gs[:], ge[:], AX, ALU.add))
            done(nc.vector.reciprocal(gr[:], gs[:]))
            done(nc.vector.tensor_tensor(gp[:], ge[:], over_experts(gr), ALU.mult))
            mine, other = gp[:, :, :, None].broadcast_to([128, ROWS, 4, 4]), gp[:, :, None, :].broadcast_to([128, ROWS, 4, 4])
            done(nc.vector.tensor_tensor(gt[:], other, mine, ALU.is_gt))
            done(nc.vector.tensor_tensor(eq[:], other, mine, ALU.is_equal))
            done(nc.vector.tensor_tensor(eq[:], eq[:], before[:, None, :, :].broadcast_to([128, ROWS, 4, 4]), ALU.mult))
            done(nc.vector.tensor_tensor(gt[:], gt[:], eq[:], ALU.add))
            done(nc.vector.tensor_reduce(rank[:], gt[:], AX, ALU.add))
            done(nc.vector.tensor_scalar(top[:], rank[:], 1.5, None, ALU.is_lt))
            done(nc.vector.tensor_reduce(tm[:], gp[:], AX, ALU.max))
            done(nc.vector.tensor_tensor(tc[:], gp[:], over_experts(tm), ALU.subtract))
            KEPT = step[0]
            v.wait_ge(s_ga, 2)
            done(nc.vector.tensor_tensor(te[:], te[:], top[:], ALU.mult))
            done(nc.vector.tensor_reduce(ts[:], te[:], AX, ALU.add))
            done(nc.vector.reciprocal(tr[:], ts[:]))
            done(nc.vector.tensor_tensor(tw[:, :, 1:5], te[:], over_experts(tr), ALU.mult))
            assert (CENTRED, KEPT) == (4, 15)
            v.wait_ge(s_res, 1)

            with v.Fori(0, B) as b:
                def got(name):
                    v.wait_ge(s_full, NF * b + FILL[name] + 1)
                    return wide[:, FILL[name] % ring.size, :, :]

                def hidden(name, out, bias):
                    rows = out.shape[0]
                    nc.vector.tensor_scalar(out.rearrange("p (a t) -> p a t", a=2), got(name)[0:rows, :, 0:288], bias, 0.0, ALU.add, ALU.max).then_inc(s_ev, 1)

                hidden("shared2", h2[:], sb2[:, 0:1])
                for x in range(4):
                    hidden(f"e2_{x}", g2[0:S, x, :], b2[:, x:x + 1])
                for c in range(5):
                    rows = 128 if c < 4 else 64
                    src = got(f"out{c}")[0:rows, 0, 0:320].rearrange("p (e f) -> p e f", e=5)
                    m = mixed[0:rows, c % 2]
                    weights = tw[0:rows, bass.ds(5 * b + c, 1), :].rearrange("p a e -> p (a e)")[:, :, None].broadcast_to([rows, 5, S])
                    nc.vector.tensor_tensor(m, src, weights, ALU.mult).then_inc(s_ev, 1)
                    v.wait_ge(s_ev, ring.per["v"] * b + (ring.per["v"] + 5 + c + 1))
                    nc.vector.tensor_reduce(msum[0:rows, c % 2, :], m.rearrange("p e f -> p f e"), AX, ALU.add).then_inc(s_mix, 1)
                    v.wait_ge(s_mix, 5 * b + c + 1)
                    r = res[0:rows, bass.ds(5 * b + c, 1), :].rearrange("p c f -> p (c f)")
                    nc.vector.tensor_tensor(r, r, msum[0:rows, c % 2, :], ALU.add).then_inc(s_res, 1)

        @block.scalar
        def _(act):
            act.wait_ge(s_w, NW)
            act.wait_ge(s_g, 4)
            nc.scalar.activation(ge[:], gc[:], ACT.Exp).then_inc(s_ga, 1)
            act.wait_ge(s_g, 15)
            nc.scalar.activation(te[:], tc[:], ACT.Exp).then_inc(s_ga, 1)
            with act.Fori(0, B) as b:
                def hidden(name, out, bias):
                    n = FILL[name]
                    act.wait_ge(s_full, NF * b + n + 1)
                    rows = out.shape[0]
                    nc.scalar.activation(out.rearrange("p (a t) -> p a t", a=2), wide[0:rows, n % ring.size, :, 0:288], ACT.Relu, bias=bias, scale=1.0).then_inc(s_ea, 1)

                hidden("shared1", h1[0:S, :], sb1[:, 0:1])
                for x in range(4):
                    hidden(f"e1_{x}", g1[:, x % 2, :], b1[:, x:x + 1])

        @block.tensor
        def _(pe):
            mm = nc.tensor.matmul
            pe.wait_ge(s_w, NW)
            pe.wait_ge(s_one, 5)
            for b in range(B):
                for c in range(5):
                    rows = 128 if c < 4 else 64
                    at = 4 * (5 * b + c)
                    i = mm(gates[0:rows, at:at + 4], xt[:, b, 128 * c:128 * c + rows], gate[:], start=True, stop=True)
            i.then_inc(s_gf, 1)
            with pe.Fori(0, B) as b:
                def fill(name, *reads):
                    n = FILL[name]
                    emptied(pe, b, n - ring.size, *[FILL[r] for r in reads])
                    return wide[:, n % ring.size, :, :]

                def layer(name, rows, lhs, rhs, *reads):
                    out = fill(name, *reads)
                    for a in range(2):
                        i = mm(out[0:rows, a, 0:288], lhs, rhs(288 * a, 288 * a + 288), start=True, stop=True)
                    i.then_inc(s_full, 1)

                def x_in(t0, t1):
                    return xt[:, bass.ds(b, 1), t0:t1].rearrange("p a t -> p (a t)")

                def first(x):
                    layer(f"e1_{x}", 128, w1[:, 128 * x:128 * x + 128], x_in)

                def second(x):
                    layer(f"e2_{x}", S, w2[:, 64 * x:64 * x + 64], lambda t0, t1: g1[:, x % 2, t0:t1], f"e1_{x}")

                layer("shared1", S, sw1[:], x_in)
                first(0)
                layer("shared2", 128, sw2[:], lambda t0, t1: h1[:, t0:t1], "shared1")
                first(1)
                second(0)
                first(2)
                second(1)
                first(3)
                second(2)
                second(3)
                for c in range(5):
                    rows = 128 if c < 4 else 64
                    out = fill(f"out{c}", "shared2", "e2_3")
                    mm(out[0:rows, 0, 0:S], h2[:, 128 * c:128 * c + rows], sw3[:], start=True, stop=True)
                    for x in range(4):
                        i = mm(out[0:rows, 0, 64 * x + 64:64 * x + 128], g2[:, x, 128 * c:128 * c + rows], w3[:, 64 * x:64 * x + 64], start=True, stop=True)
                    i.then_inc(s_full, 1)


def early_fusion_kernel(nc, d, out, ctx_dram, h_spatial):
    fno_stage(nc, d, h_spatial)
    with ExitStack() as ctx:
        def sb(n, shape):
            return ctx.enter_context(nc.sbuf_tensor(n, shape, F32))

        res = sb("res", [128, ROWS, S])
        xn = sb("xn", [128, ROWS, S + 1])
        xt = sb("xt", [128, B, T])
        ident = sb("ident", [128, 128])
        s_id = ctx.enter_context(nc.semaphore("ident_loaded"))
        s_zero = ctx.enter_context(nc.semaphore("xt_padded"))
        with nc.Block() as block:
            @block.gpsimd
            def _(pool):
                nc.gpsimd.memset(xt[S:128, :, :], 0.0).then_inc(s_zero, 1)
                pool.wait_ge(s_zero, 1)

            @block.sync
            def _(sp):
                sp.dma_start(ident[:], d["c_ident"]).then_inc(s_id, 16)
                sp.wait_ge(s_id, 16)
        load_tokens(nc, d, h_spatial, res)
        norm_stage(nc, "n1", res, xn, xt, ident)
        with ExitStack() as inner:
            o_query_t = inner.enter_context(nc.sbuf_tensor("o_query_t", [128, B, CUT], F32))
            o_key_t = inner.enter_context(nc.sbuf_tensor("o_key_t", [128, B, T], F32))
            l1_stage(nc, d, xt, o_query_t, o_key_t, ident)
            fanin_stage(nc, d, res, xn, o_query_t, o_key_t, ident)
        norm_stage(nc, "n2", res, xn, xt, ident)
        slice_stage(nc, d, res, xn, xt, ident)
        norm_stage(nc, "n3", res, xn, xt, ident)
        mqa_stage(nc, d, xt, ctx_dram, ident)
        mqa_out_stage(nc, d, ctx_dram, res)
        norm_stage(nc, "n4", res, xn, xt, ident)
        moe_stage(nc, d, res, xt)
        store_tokens(nc, out, res)


def kernel(**inputs):
    import concourse.bacc as bacc
    from concourse.bass_utils import run_bass_kernel_spmd

    nc = bacc.Bacc("TRN2", target_bir_lowering=False, num_devices=1)
    constants = {**fno_constants(), **l1_constants(), **moe_constants()}
    laid = {**constants, **fno_layout(inputs, constants), **l1_layout(inputs), **slice_layout(inputs), **mqa_layout(inputs),
            **moe_layout(inputs), "txt": inputs["txt"]}
    arrays, d = {}, {}
    for name, a in laid.items():
        a = np.ascontiguousarray(a)
        arrays["in_" + name] = a
        d[name] = nc.dram_tensor("in_" + name, a.shape, mybir.dt.from_np(a.dtype), kind="ExternalInput").ap()
    out = nc.dram_tensor("out_0_dram", (B, T, S), F32, kind="ExternalOutput").ap()
    ctx_dram = nc.dram_tensor("ctx_scratch", (B, T, 512), F32, kind="Internal").ap()
    h_spatial = nc.dram_tensor("h_scratch", (B, S, S), F32, kind="Internal").ap()
    early_fusion_kernel(nc, d, out, ctx_dram, h_spatial)
    r = run_bass_kernel_spmd(nc, [arrays], core_ids=[0])
    return r.results[0]["out_0_dram"]
```
